# Optimizing a Trainium2 kernel written in Bass

```python
import numpy as np
import jax
import jax.numpy as jnp

def _softmax(x, axis=-1):
    return jax.nn.softmax(x, axis=axis)

def _gelu(x):
    return jax.nn.gelu(x, approximate=True)

def _silu(x):
    return jax.nn.silu(x)

def _sigmoid(x):
    return jax.nn.sigmoid(x)

def _layernorm(x, axis=-1, eps=1e-05):
    m = jnp.mean(x, axis=axis, keepdims=True)
    v = jnp.var(x, axis=axis, keepdims=True)
    return (x - m) / jnp.sqrt(v + eps)

def _scatter_add(tgt, idx, src, axis=0):
    return tgt.at[idx].add(src)

def _segment_sum(src, seg, n):
    return jax.ops.segment_sum(src, seg, n)
kernel_name = 'mk_sandwich_d2_jaxref_r8_a6d8a6'

def setup_inputs(seed: int=0):
    np.random.seed(seed)
    _w = jnp.asarray

    def _L0_attn_setup():
        import jax, jax.numpy as jnp
        import numpy as np
        B, S, D = (2, 256, 512)
        H = 32
        HD = D // H
        THETA = 10000.0

        def _rope_cos_sin(seq_len, head_dim, theta=THETA):
            inv = 1.0 / theta ** (np.arange(0, head_dim, 2)[:head_dim // 2].astype(np.float32) / head_dim)
            t = np.arange(seq_len)
            f = np.outer(t, inv).astype(np.float32)
            return (jnp.asarray(np.cos(f)), jnp.asarray(np.sin(f)))

        def _apply_rotary(x, cos, sin):
            xr = x.astype(jnp.float32).reshape(*x.shape[:-1], HD // 2, 2)
            x0, x1 = (xr[..., 0], xr[..., 1])
            c = cos[None, :, None, :]
            s = sin[None, :, None, :]
            o0 = x0 * c - x1 * s
            o1 = x0 * s + x1 * c
            return jnp.stack((o0, o1), axis=-1).reshape(*x.shape[:-1], HD)
        key = jax.random.key(seed)
        ks = jax.random.split(key, 5)
        std = 0.02
        return {'x': jax.random.normal(ks[0], (B, S, D), dtype=jnp.float32), 'wq': jax.random.normal(ks[1], (D, D), dtype=jnp.float32) * std, 'wk': jax.random.normal(ks[2], (D, D), dtype=jnp.float32) * std, 'wv': jax.random.normal(ks[3], (D, D), dtype=jnp.float32) * std, 'wo': jax.random.normal(ks[4], (D, D), dtype=jnp.float32) * std}
    _L0_attn_in = _L0_attn_setup()

    def _L0_ffn_setup():
        import jax, jax.numpy as jnp
        import numpy as np
        D_MODEL = 512
        D_HIDDEN = 1376
        RANK = 16
        BATCH, SEQ = (2, 256)

        def _matmul_lora(x, w, a, b, scale=1.0):
            out = jnp.einsum('bsd,hd->bsh', x, w)
            out = out + jnp.einsum('bsr,hr->bsh', jnp.einsum('bsd,rd->bsr', x, a), b) * scale
            return out
        key = jax.random.key(seed)
        ks = jax.random.split(key, 10)
        s = 0.02
        return {'x': jax.random.normal(ks[0], (BATCH, SEQ, D_MODEL), jnp.float32), 'gate_w': jax.random.normal(ks[1], (D_HIDDEN, D_MODEL), jnp.float32) * s, 'up_w': jax.random.normal(ks[2], (D_HIDDEN, D_MODEL), jnp.float32) * s, 'down_w': jax.random.normal(ks[3], (D_MODEL, D_HIDDEN), jnp.float32) * s, 'gate_a': jax.random.normal(ks[4], (RANK, D_MODEL), jnp.float32) * s, 'gate_b': jax.random.normal(ks[5], (D_HIDDEN, RANK), jnp.float32) * s, 'up_a': jax.random.normal(ks[6], (RANK, D_MODEL), jnp.float32) * s, 'up_b': jax.random.normal(ks[7], (D_HIDDEN, RANK), jnp.float32) * s, 'down_a': jax.random.normal(ks[8], (RANK, D_HIDDEN), jnp.float32) * s, 'down_b': jax.random.normal(ks[9], (D_MODEL, RANK), jnp.float32) * s}
    _L0_ffn_in = _L0_ffn_setup()

    def _L1_attn_setup():
        import jax, jax.numpy as jnp
        import numpy as np
        DEPTH, DIM, DFF, VOCAB = (4, 64, 256, 512)
        EPS = 1e-05

        def layernorm(x, w, b):
            mu = jnp.mean(x, axis=-1, keepdims=True)
            var = jnp.mean((x - mu) ** 2, axis=-1, keepdims=True)
            return (x - mu) * jax.lax.rsqrt(var + EPS) * w + b

        def sconv(x, phazor_c, last_conv_c):
            B, L, D = x.shape
            r = jnp.abs(phazor_c)
            p = jnp.tanh(r) * jnp.exp(1j * jnp.angle(phazor_c))
            prog = p[None, :] ** jnp.arange(L, dtype=jnp.float32)[:, None]
            filt_fft = jnp.fft.fft(prog, n=2 * L, axis=0)
            x_fft = jnp.fft.fft(x.astype(jnp.complex64), n=2 * L, axis=1)
            conv = jnp.fft.ifft(filt_fft[None] * x_fft, axis=1)[:, :L]
            conv = conv + last_conv_c[None, None, :] * prog[None] * p[None, None, :]
            return conv.real.astype(x.dtype)

        def _forward(x, Win, bin, ln1_w, ln1_b, phz_re, phz_im, lc_re, lc_im, sc_lin, ln2_w, ln2_b, W1, b1, W2, b2, lnl_w, lnl_b, Wout, bout):
            h = jnp.einsum('blv,dv->bld', x, Win) + bin

            def body(h, p):
                l1w, l1b, pr, pi, lr, li, scl, l2w, l2b, w1, b1_, w2, b2_ = p
                y = jax.nn.silu(layernorm(h, l1w, l1b))
                y = sconv(y, pr + 1j * pi, lr + 1j * li)
                h = h + y * scl
                y = layernorm(h, l2w, l2b)
                y = jax.nn.silu(jnp.einsum('bld,fd->blf', y, w1) + b1_)
                y = jnp.einsum('blf,df->bld', y, w2) + b2_
                return (h + y, None)
            xs = (ln1_w, ln1_b, phz_re, phz_im, lc_re, lc_im, sc_lin, ln2_w, ln2_b, W1, b1, W2, b2)
            h, _ = jax.lax.scan(body, h, xs)
            h = layernorm(h, lnl_w, lnl_b)
            return jnp.einsum('bld,vd->blv', h, Wout) + bout
        key = jax.random.key(seed)
        ks = jax.random.split(key, 20)
        f32 = jnp.float32
        inp = {}
        inp['x'] = jax.random.normal(ks[0], (2, 512, VOCAB), dtype=f32)
        inp['Win'] = jax.random.normal(ks[1], (DIM, VOCAB), dtype=f32) * VOCAB ** (-0.5)
        inp['bin'] = jnp.zeros((DIM,), f32)
        inp['ln1_w'] = jnp.ones((DEPTH, DIM), f32)
        inp['ln1_b'] = jnp.zeros((DEPTH, DIM), f32)
        ang = 2 * np.pi * jnp.arange(DIM, dtype=f32) / DIM
        mag = jnp.abs(jax.random.normal(ks[2], (DEPTH, DIM), dtype=f32))
        inp['phz_re'] = mag * jnp.cos(ang)[None]
        inp['phz_im'] = mag * jnp.sin(ang)[None]
        inp['lc_re'] = jax.random.normal(ks[3], (DEPTH, DIM), dtype=f32)
        inp['lc_im'] = jax.random.normal(ks[4], (DEPTH, DIM), dtype=f32)
        inp['sc_lin'] = jnp.ones((DEPTH, DIM), f32)
        inp['ln2_w'] = jnp.ones((DEPTH, DIM), f32)
        inp['ln2_b'] = jnp.zeros((DEPTH, DIM), f32)
        inp['W1'] = jax.random.normal(ks[5], (DEPTH, DFF, DIM), dtype=f32) * DIM ** (-0.5)
        inp['b1'] = jnp.zeros((DEPTH, DFF), f32)
        inp['W2'] = jax.random.normal(ks[6], (DEPTH, DIM, DFF), dtype=f32) * DFF ** (-0.5)
        inp['b2'] = jnp.zeros((DEPTH, DIM), f32)
        inp['lnl_w'] = jnp.ones((DIM,), f32)
        inp['lnl_b'] = jnp.zeros((DIM,), f32)
        inp['Wout'] = jax.random.normal(ks[7], (VOCAB, DIM), dtype=f32) * DIM ** (-0.5)
        inp['bout'] = jnp.zeros((VOCAB,), f32)
        return inp
    _L1_attn_in = _L1_attn_setup()

    def _L1_ffn_setup():
        import jax, jax.numpy as jnp
        import numpy as np
        GROUP = 64

        def dequant_q40(w, s, out_features, in_features):
            msb = w >> 4
            lsb = (w & 15 ^ 8) - 8
            g = jnp.concatenate([msb, lsb], axis=1).reshape(-1, GROUP)
            deq = g.astype(s.dtype) * s[:, None]
            return deq.reshape(out_features, in_features)
        key = jax.random.key(seed)
        ks = jax.random.split(key, 7)
        dim, hidden = (512, 1376)
        B, S = (2, 256)

        def packed(k, din, dout):
            return jax.random.randint(k, (din * dout // GROUP // 2, GROUP), -128, 128, dtype=jnp.int32)

        def scales(k, din, dout):
            return (jax.random.uniform(k, (din * dout // GROUP,), dtype=jnp.float32) + 0.5) * 0.01
        x = jax.random.normal(ks[0], (B, S, dim), dtype=jnp.float32)
        w1 = packed(ks[1], dim, hidden)
        s1 = scales(ks[2], dim, hidden)
        w2 = packed(ks[3], hidden, dim)
        s2 = scales(ks[4], hidden, dim)
        w3 = packed(ks[5], dim, hidden)
        s3 = scales(ks[6], dim, hidden)
        return {'x': x, 'w1': w1, 's1': s1, 'w2': w2, 's2': s2, 'w3': w3, 's3': s3}
    _L1_ffn_in = _L1_ffn_setup()
    _d = {'L0_attn_x': _L0_attn_in['x'], 'L0_attn_wq': _L0_attn_in['wq'], 'L0_attn_wk': _L0_attn_in['wk'], 'L0_attn_wv': _L0_attn_in['wv'], 'L0_attn_wo': _L0_attn_in['wo'], 'L0_ffn_gate_w': _L0_ffn_in['gate_w'], 'L0_ffn_up_w': _L0_ffn_in['up_w'], 'L0_ffn_down_w': _L0_ffn_in['down_w'], 'L0_ffn_gate_a': _L0_ffn_in['gate_a'], 'L0_ffn_gate_b': _L0_ffn_in['gate_b'], 'L0_ffn_up_a': _L0_ffn_in['up_a'], 'L0_ffn_up_b': _L0_ffn_in['up_b'], 'L0_ffn_down_a': _L0_ffn_in['down_a'], 'L0_ffn_down_b': _L0_ffn_in['down_b'], 'L1_attn_Win': _L1_attn_in['Win'], 'L1_attn_bin': _L1_attn_in['bin'], 'L1_attn_ln1_w': _L1_attn_in['ln1_w'], 'L1_attn_ln1_b': _L1_attn_in['ln1_b'], 'L1_attn_phz_re': _L1_attn_in['phz_re'], 'L1_attn_phz_im': _L1_attn_in['phz_im'], 'L1_attn_lc_re': _L1_attn_in['lc_re'], 'L1_attn_lc_im': _L1_attn_in['lc_im'], 'L1_attn_sc_lin': _L1_attn_in['sc_lin'], 'L1_attn_ln2_w': _L1_attn_in['ln2_w'], 'L1_attn_ln2_b': _L1_attn_in['ln2_b'], 'L1_attn_W1': _L1_attn_in['W1'], 'L1_attn_b1': _L1_attn_in['b1'], 'L1_attn_W2': _L1_attn_in['W2'], 'L1_attn_b2': _L1_attn_in['b2'], 'L1_attn_lnl_w': _L1_attn_in['lnl_w'], 'L1_attn_lnl_b': _L1_attn_in['lnl_b'], 'L1_attn_Wout': _L1_attn_in['Wout'], 'L1_attn_bout': _L1_attn_in['bout'], 'L1_ffn_w1': _L1_ffn_in['w1'], 'L1_ffn_s1': _L1_ffn_in['s1'], 'L1_ffn_w2': _L1_ffn_in['w2'], 'L1_ffn_s2': _L1_ffn_in['s2'], 'L1_ffn_w3': _L1_ffn_in['w3'], 'L1_ffn_s3': _L1_ffn_in['s3']}
    _x0 = _d['L0_attn_x']
    _d['L0_attn_x'] = jax.random.normal(jax.random.fold_in(jax.random.key(seed), 1), (2, 512, 512), dtype=_x0.dtype)
    del _x0
    return _d

def reference(L0_attn_x, L0_attn_wq, L0_attn_wk, L0_attn_wv, L0_attn_wo, L0_ffn_gate_w, L0_ffn_up_w, L0_ffn_down_w, L0_ffn_gate_a, L0_ffn_gate_b, L0_ffn_up_a, L0_ffn_up_b, L0_ffn_down_a, L0_ffn_down_b, L1_attn_Win, L1_attn_bin, L1_attn_ln1_w, L1_attn_ln1_b, L1_attn_phz_re, L1_attn_phz_im, L1_attn_lc_re, L1_attn_lc_im, L1_attn_sc_lin, L1_attn_ln2_w, L1_attn_ln2_b, L1_attn_W1, L1_attn_b1, L1_attn_W2, L1_attn_b2, L1_attn_lnl_w, L1_attn_lnl_b, L1_attn_Wout, L1_attn_bout, L1_ffn_w1, L1_ffn_s1, L1_ffn_w2, L1_ffn_s2, L1_ffn_w3, L1_ffn_s3):

    def _L0_attn_ref(x, wq, wk, wv, wo):
        import jax, jax.numpy as jnp
        import numpy as np
        B, S, D = (2, 256, 512)
        H = 32
        HD = D // H
        THETA = 10000.0

        def _rope_cos_sin(seq_len, head_dim, theta=THETA):
            inv = 1.0 / theta ** (np.arange(0, head_dim, 2)[:head_dim // 2].astype(np.float32) / head_dim)
            t = np.arange(seq_len)
            f = np.outer(t, inv).astype(np.float32)
            return (jnp.asarray(np.cos(f)), jnp.asarray(np.sin(f)))

        def _apply_rotary(x, cos, sin):
            xr = x.astype(jnp.float32).reshape(*x.shape[:-1], HD // 2, 2)
            x0, x1 = (xr[..., 0], xr[..., 1])
            c = cos[None, :, None, :]
            s = sin[None, :, None, :]
            o0 = x0 * c - x1 * s
            o1 = x0 * s + x1 * c
            return jnp.stack((o0, o1), axis=-1).reshape(*x.shape[:-1], HD)
        b, s, d = x.shape
        q = (x @ wq).reshape(b, s, H, HD)
        k = (x @ wk).reshape(b, s, H, HD)
        v = (x @ wv).reshape(b, s, H, HD)
        cos, sin = _rope_cos_sin(s, HD)
        q = _apply_rotary(q, cos, sin)
        k = _apply_rotary(k, cos, sin)
        scale = 1.0 / jnp.sqrt(jnp.float32(HD))
        scores = jnp.einsum('bqhd,bkhd->bhqk', q, k) * scale
        causal = jnp.tril(jnp.ones((s, s), dtype=bool))
        scores = jnp.where(causal[None, None], scores, jnp.finfo(scores.dtype).min)
        probs = jax.nn.softmax(scores, axis=-1)
        out = jnp.einsum('bhqk,bkhd->bqhd', probs, v).reshape(b, s, d)
        return out @ wo

    def _L0_ffn_ref(x, gate_w, up_w, down_w, gate_a, gate_b, up_a, up_b, down_a, down_b):
        import jax, jax.numpy as jnp
        import numpy as np
        D_MODEL = 512
        D_HIDDEN = 1376
        RANK = 16
        BATCH, SEQ = (2, 256)

        def _matmul_lora(x, w, a, b, scale=1.0):
            out = jnp.einsum('bsd,hd->bsh', x, w)
            out = out + jnp.einsum('bsr,hr->bsh', jnp.einsum('bsd,rd->bsr', x, a), b) * scale
            return out
        gate = _matmul_lora(x, gate_w, gate_a, gate_b)
        up = _matmul_lora(x, up_w, up_a, up_b)
        hidden = jax.nn.silu(gate) * up
        out = _matmul_lora(hidden, down_w, down_a, down_b)
        return out

    def _L1_attn_ref(x, Win, bin, ln1_w, ln1_b, phz_re, phz_im, lc_re, lc_im, sc_lin, ln2_w, ln2_b, W1, b1, W2, b2, lnl_w, lnl_b, Wout, bout):
        import jax, jax.numpy as jnp
        import numpy as np
        DEPTH, DIM, DFF, VOCAB = (4, 64, 256, 512)
        EPS = 1e-05

        def layernorm(x, w, b):
            mu = jnp.mean(x, axis=-1, keepdims=True)
            var = jnp.mean((x - mu) ** 2, axis=-1, keepdims=True)
            return (x - mu) * jax.lax.rsqrt(var + EPS) * w + b

        def sconv(x, phazor_c, last_conv_c):
            B, L, D = x.shape
            r = jnp.abs(phazor_c)
            p = jnp.tanh(r) * jnp.exp(1j * jnp.angle(phazor_c))
            prog = p[None, :] ** jnp.arange(L, dtype=jnp.float32)[:, None]
            filt_fft = jnp.fft.fft(prog, n=2 * L, axis=0)
            x_fft = jnp.fft.fft(x.astype(jnp.complex64), n=2 * L, axis=1)
            conv = jnp.fft.ifft(filt_fft[None] * x_fft, axis=1)[:, :L]
            conv = conv + last_conv_c[None, None, :] * prog[None] * p[None, None, :]
            return conv.real.astype(x.dtype)

        def _forward(x, Win, bin, ln1_w, ln1_b, phz_re, phz_im, lc_re, lc_im, sc_lin, ln2_w, ln2_b, W1, b1, W2, b2, lnl_w, lnl_b, Wout, bout):
            h = jnp.einsum('blv,dv->bld', x, Win) + bin

            def body(h, p):
                l1w, l1b, pr, pi, lr, li, scl, l2w, l2b, w1, b1_, w2, b2_ = p
                y = jax.nn.silu(layernorm(h, l1w, l1b))
                y = sconv(y, pr + 1j * pi, lr + 1j * li)
                h = h + y * scl
                y = layernorm(h, l2w, l2b)
                y = jax.nn.silu(jnp.einsum('bld,fd->blf', y, w1) + b1_)
                y = jnp.einsum('blf,df->bld', y, w2) + b2_
                return (h + y, None)
            xs = (ln1_w, ln1_b, phz_re, phz_im, lc_re, lc_im, sc_lin, ln2_w, ln2_b, W1, b1, W2, b2)
            h, _ = jax.lax.scan(body, h, xs)
            h = layernorm(h, lnl_w, lnl_b)
            return jnp.einsum('bld,vd->blv', h, Wout) + bout
        return _forward(x, Win, bin, ln1_w, ln1_b, phz_re, phz_im, lc_re, lc_im, sc_lin, ln2_w, ln2_b, W1, b1, W2, b2, lnl_w, lnl_b, Wout, bout)

    def _L1_ffn_ref(x, w1, s1, w2, s2, w3, s3):
        import jax, jax.numpy as jnp
        import numpy as np
        GROUP = 64

        def dequant_q40(w, s, out_features, in_features):
            msb = w >> 4
            lsb = (w & 15 ^ 8) - 8
            g = jnp.concatenate([msb, lsb], axis=1).reshape(-1, GROUP)
            deq = g.astype(s.dtype) * s[:, None]
            return deq.reshape(out_features, in_features)
        dim = x.shape[-1]
        hidden = w1.shape[0] * w1.shape[1] * 2 // dim
        W1 = dequant_q40(w1, s1, hidden, dim)
        W3 = dequant_q40(w3, s3, hidden, dim)
        W2 = dequant_q40(w2, s2, dim, hidden)
        a = jnp.einsum('bsd,hd->bsh', x, W1)
        b = jnp.einsum('bsd,hd->bsh', x, W3)
        h = jax.nn.silu(a) * b
        return jnp.einsum('bsh,dh->bsd', h, W2)
    x = L0_attn_x
    x = x + _layernorm(_L0_attn_ref(_layernorm(x, axis=-1), L0_attn_wq, L0_attn_wk, L0_attn_wv, L0_attn_wo), axis=-1)
    x = x + _layernorm(_L0_ffn_ref(_layernorm(x, axis=-1), L0_ffn_gate_w, L0_ffn_up_w, L0_ffn_down_w, L0_ffn_gate_a, L0_ffn_gate_b, L0_ffn_up_a, L0_ffn_up_b, L0_ffn_down_a, L0_ffn_down_b), axis=-1)
    x = x + _layernorm(_L1_attn_ref(_layernorm(x, axis=-1), L1_attn_Win, L1_attn_bin, L1_attn_ln1_w, L1_attn_ln1_b, L1_attn_phz_re, L1_attn_phz_im, L1_attn_lc_re, L1_attn_lc_im, L1_attn_sc_lin, L1_attn_ln2_w, L1_attn_ln2_b, L1_attn_W1, L1_attn_b1, L1_attn_W2, L1_attn_b2, L1_attn_lnl_w, L1_attn_lnl_b, L1_attn_Wout, L1_attn_bout), axis=-1)
    x = x + _layernorm(_L1_ffn_ref(_layernorm(x, axis=-1), L1_ffn_w1, L1_ffn_s1, L1_ffn_w2, L1_ffn_s2, L1_ffn_w3, L1_ffn_s3), axis=-1)
    return x

_drawn_inputs = setup_inputs


def setup_inputs(seed=0):
    import zlib

    import numpy as np

    out = dict(_drawn_inputs(seed))
    spreads = {'L1_attn_bin': (0.0, 0.1),
     'L1_attn_ln1_w': (1.0, 0.2),
     'L1_attn_ln1_b': (0.0, 0.1),
     'L1_attn_sc_lin': (1.0, 0.2),
     'L1_attn_ln2_w': (1.0, 0.2),
     'L1_attn_ln2_b': (0.0, 0.332),
     'L1_attn_b1': (0.0, 0.389),
     'L1_attn_b2': (0.0, 0.1),
     'L1_attn_lnl_w': (1.0, 0.2),
     'L1_attn_lnl_b': (0.0, 0.1),
     'L1_attn_bout': (0.0, 0.1)}
    factors = {'L1_attn_lc_re': 3.015, 'L1_attn_lc_im': 2.824}
    for name, (base, spread) in spreads.items():
        noise = np.random.default_rng([zlib.crc32(name.encode()), seed]).standard_normal(out[name].shape)
        drawn = base * np.exp(spread * noise) if base else spread * noise
        out[name] = jnp.asarray(drawn.astype(out[name].dtype))
    for name, factor in factors.items():
        out[name] = (out[name] * factor).astype(out[name].dtype)
    return out
```

```python
from contextlib import ExitStack

import concourse.bass as bass
from concourse import mybir

F32 = mybir.dt.float32
F32R = mybir.dt.float32r
BF16 = mybir.dt.bfloat16
I32 = mybir.dt.int32
ALU = mybir.AluOpType
ACT = mybir.ActivationFunctionType
AX_X = mybir.AxisListType.X

P = 128
B, S, D = 2, 512, 512
N = B * S
NT = N // P
TB = S // P
KD = D // P
H, HD = 32, 16
NPAIR = H // 2
F = 1376
HT = [(k * P, min(P, F - k * P)) for k in range((F + P - 1) // P)]
GROUPS = [(0, 6), (6, 11)]
RING = 7
RANK = 16
GROUP4 = 64
C = 64
DEPTH, DFF = 4, 256
EPS = 1e-5


def sandwich(nc, a, out):
    es = ExitStack()
    sems = {}

    def sem(name):
        if name not in sems:
            sems[name] = es.enter_context(nc.semaphore(name))
        return sems[name]

    def sb(ctx, name, shape, dt=F32):
        return ctx.enter_context(nc.sbuf_tensor(name, shape, dt))

    with es:
        bank = [es.enter_context(nc.psum_tensor(f"bank{i}", [P, 512], F32)) for i in range(8)]
        x = sb(es, "x", [P, NT, D])
        xt_hi = sb(es, "xt_hi", [P, KD, N], F32R)
        xt_lo = sb(es, "xt_lo", [P, KD, N], F32R)
        y = sb(es, "y", [P, NT, D])
        ident = sb(es, "ident", [P, P])
        ident16 = sb(es, "ident16", [P, P], BF16)
        causal16 = sb(es, "causal16", [P, P], BF16)
        neghalf = sb(es, "neghalf", [P, 4])
        epst = sb(es, "epst", [P, 1])
        bnst = sb(es, "bnst", [P, 6])
        mv = sb(es, "mv", [P, 8, NT, 2])
        ve = sb(es, "ve", [P, 8, NT])
        rstd = sb(es, "rstd", [P, 8, NT])
        xn = sb(es, "xn", [P, 2, D])
        at = ExitStack()
        with at:
            w_hi = sb(at, "w_hi", [P, 3, KD, D], F32R)
            w_lo = sb(at, "w_lo", [P, 3, KD, D], F32R)
            qk = sb(at, "qk", [P, 2, NT, D])
            v = sb(at, "v", [P, NT, D])
            rope_c = sb(at, "rope_c", [P, 2, TB, HD])
            rope_s = sb(at, "rope_s", [P, 2, TB, HD])
            negmax = sb(at, "negmax", [P, B * H * TB])
            esum = sb(at, "esum", [P, B * H * TB])
            einv = sb(at, "einv", [P, B * H * TB])
            with ExitStack() as sub:
                w_raw = sb(sub, "w_raw", [P, KD, D])
                rot_c = sb(sub, "rot_c", [P, 2, D])
                rot_s = sb(sub, "rot_s", [P, 2, D])
            with ExitStack() as sub:
                spread = sb(sub, "spread", [P, 4, 4, P], F32R)
                stack = sb(sub, "stack", [P, 2, 2, D], F32R)
                probs = sb(sub, "probs", [P, 3, D])
                probs_t = sb(sub, "probs_t", [P, 2, D])
                o_hi = sb(sub, "o_hi", [P, 2, KD, P], F32R)
                o_lo = sb(sub, "o_lo", [P, 2, KD, P], F32R)
        with ExitStack() as ff:
            h_hi = sb(ff, "h_hi", [P, RING, N], F32R)
            h_lo = sb(ff, "h_lo", [P, RING, N], F32R)
            wd_hi = sb(ff, "wd_hi", [P, RING, D], F32R)
            wd_lo = sb(ff, "wd_lo", [P, RING, D], F32R)
            wgu_raw = sb(ff, "wgu_raw", [P, 4, KD, P])
            wgu_hi = sb(ff, "wgu_hi", [P, 4, KD, P], F32R)
            wgu_lo = sb(ff, "wgu_lo", [P, 4, KD, P], F32R)
            wd_raw = sb(ff, "wd_raw", [P, 2, D])
            sg = sb(ff, "sg", [P, 2, D])
            hf = sb(ff, "hf", [P, 2, D])
            shifts = sb(ff, "shifts", [P, 5, 2], I32)
            with ExitStack() as sub:
                lora_a = sb(sub, "lora_a", [96, F])
                lora_b = sb(sub, "lora_b", [96, D])
            with ExitStack() as sub:
                s4 = sb(sub, "s4", [40, F])
                s4sel = sb(sub, "s4sel", [40, KD, P])
                s4d = sb(sub, "s4d", [107, D // 2])
                s4dsel = sb(sub, "s4dsel", [107, F])
        with ExitStack() as mx:
            win_raw = sb(mx, "win_raw", [P, KD, P])
            win_hi = sb(mx, "win_hi", [P, KD, P], F32R)
            win_lo = sb(mx, "win_lo", [P, KD, P], F32R)
            w1t = sb(mx, "w1t", [P, DEPTH, DFF])
            w2t = sb(mx, "w2t", [P, DEPTH, 2, C])
            wout = sb(mx, "wout", [P, D])
            bout = sb(mx, "bout", [P, D])
            cmat = sb(mx, "cmat", [P, P])
            bmat = sb(mx, "bmat", [P, P])
            chan = sb(mx, "chan", [P, 10, DEPTH])
            b1 = sb(mx, "b1", [P, DEPTH, 2])
            last = sb(mx, "last", [P, 3])
            ct = sb(mx, "ct", [P, DEPTH, S])
            sn = sb(mx, "sn", [P, DEPTH, S])
            tw = sb(mx, "tw", [P, 2, DEPTH, S // 2])
            pw = sb(mx, "pw", [P, 12, DEPTH])
            step_c = sb(mx, "step_c", [P, 10, DEPTH])
            step_s = sb(mx, "step_s", [P, 10, DEPTH])
            hm = sb(mx, "hm", [P, S])
            wk = sb(mx, "wk", [P, 10, S])
            g1 = sb(mx, "g1", [P, 4, S])
        block = es.enter_context(nc.Block())

        UNITS = [(b, h, i) for b in range(B) for h in range(H) for i in range(TB)]
        PAIRS = [(b, p) for b in range(B) for p in range(NPAIR)]
        UP = 2 * TB
        COMBOS = ((0, 0), (0, 1), (1, 0))
        XT_LAG = 4
        XT = (xt_hi, xt_lo)

        def hid(m):
            return HT[m][1]

        @block.sync
        def _(sp):
            for t in range(NT):
                sp.dma_start(x[:, t, :], a["x"][t * P:(t + 1) * P, :]).then_inc(sem(f"x_in{t}"), 16)
                if t == 0:
                    sp.dma_start(ident[:, :], a["ident"]).then_inc(sem("consts_in"), 16)
                    sp.dma_start(neghalf[:, :], a["neghalf"]).then_inc(sem("consts_in"), 16)
                    sp.dma_start(rope_c[:, :, :, :], a["rope_c"]).then_inc(sem("consts_in"), 16)
                    sp.dma_start(rope_s[:, :, :, :], a["rope_s"]).then_inc(sem("consts_in"), 16)
                    sp.dma_start(ident16[:, :], a["ident16"]).then_inc(sem("consts_in"), 16)
                    sp.dma_start(causal16[:, :], a["causal16"]).then_inc(sem("consts_in"), 16)
            for j, name in enumerate(("wq", "wk", "wv", "wo")):
                if j:
                    sp.wait_ge(sem("w_split"), j)
                sp.dma_start(w_raw[:, :, :], a[name].rearrange("(k p) n -> p k n", p=P)).then_inc(sem("w_in"), 16)
            sp.wait_ge(sem("w_split"), 4)
            sp.dma_start(w_raw[:, :, :], a["spread"]).then_inc(sem("w_in"), 16)

            def ffn_loads(s):
                sp.wait_ge(sem(f"xt_ready{s}"), NT)
                if s == 1:
                    for r, (na, nb) in enumerate((("gate_bt", "gate_a"), ("up_bt", "up_a"), ("down_a", "down_bt"))):
                        sp.dma_start(lora_a[32 * r:32 * r + RANK, :], a[na]).then_inc(sem("side_in1"), 16)
                        sp.dma_start(lora_b[32 * r:32 * r + RANK, :], a[nb]).then_inc(sem("side_in1"), 16)
                    wgu, wd, raw_gu, raw_d = a["gu_t"], a["down_t"], wgu_raw[:, :, :, :], wd_raw[:, :, :]
                else:
                    for c in range(2):
                        sp.dma_start(s4[32 * c:32 * c + 8, :], a["s13"][c]).then_inc(sem("side_in3"), 16)
                        sp.dma_start(s4sel[32 * c:32 * c + 8, :, :], a["s4sel"]).then_inc(sem("side_in3"), 16)
                        sp.dma_start(s4d[64 * c:64 * c + 43, :], a["s2"]).then_inc(sem("side_in3"), 16)
                        sp.dma_start(s4dsel[64 * c:64 * c + 43, :], a["s4dsel"][c]).then_inc(sem("side_in3"), 16)
                    sp.dma_start(shifts[:, :, :], a["shifts"]).then_inc(sem("side_in3"), 16)
                    wgu, wd = a["w13"], a["w2"]
                    raw_gu, raw_d = wgu_raw[:, :, :, :].bitcast(I32), wd_raw[:, :, :].bitcast(I32)
                for m, (h0, n) in enumerate(HT):
                    if m >= 2:
                        sp.wait_ge(sem(f"wlo{s}"), 3 * (m - 1))
                    for g in range(2):
                        sp.dma_start(raw_gu[:, 2 * (m % 2) + g, :, 0:n],
                                     wgu[g].rearrange("(k p) h -> p k h", p=P)[:, :, h0:h0 + n]).then_inc(sem(f"wraw{s}_{m % 2}"), 16)
                    sp.dma_start(raw_d[0:n, m % 2, :], wd[h0:h0 + n, :]).then_inc(sem(f"wraw{s}_{m % 2}"), 16)

            ffn_loads(1)
            sp.wait_ge(sem("y_ready1"), NT)
            for dst, name in ((win_raw[:, :, :], "win_t"), (w1t[:, :, :], "w1_t"), (w2t[:, :, :, :], "w2_t"), (wout[:, :], "wout_t"),
                              (cmat[:, :], "cmat"), (bmat[:, :], "bmat"), (chan[:, :, :], "chan"), (b1[:, :, :], "b1"),
                              (last[:, :], "last")):
                sp.dma_start(dst, a[name]).then_inc(sem("mixer_in"), 16)
            sp.dma_start(bout[:, :], a["bout"].partition_broadcast(P)).then_inc(sem("mixer_in"), 16)
            ffn_loads(3)
            for t in range(NT):
                sp.wait_ge(sem("x_sum3"), t + 1)
                sp.dma_start(out[t * P:(t + 1) * P, :], x[:, t, :]).then_inc(sem("stored"), 16)
            sp.wait_ge(sem("stored"), 16 * NT)

        @block.gpsimd
        def _(pool):
            pool_steps = [0]

            def link(ins):
                pool_steps[0] += 1
                ins.then_inc(sem("pool_step"), 1)
                pool.wait_ge(sem("pool_step"), pool_steps[0])

            def inv_std(n, t, stats, done):
                pool.wait_ge(sem(stats), t + 1)
                link(nc.gpsimd.tensor_scalar(ve[:, n, t:t + 1], mv[:, n, t, 1:2], EPS, None, ALU.add))
                nc.gpsimd.tensor_tensor(rstd[:, n, t:t + 1], ve[:, n, t:t + 1], neghalf[:, 0:1], ALU.pow).then_inc(sem(done), 1)

            def norm_out(s):
                for t in range(NT + 2):
                    if t < NT:
                        inv_std(2 * s + 1, t, f"y_stats{s}", f"y_rstd{s}")
                    if 1 <= t <= NT:
                        u = t - 1
                        pool.wait_ge(sem(f"y_norm{s}"), u + 1)
                        nc.gpsimd.tensor_tensor(x[:, u, :], x[:, u, :], y[:, u, :], ALU.add).then_inc(sem(f"x_sum{s}"), 1)
                    if t >= 2 and s < 3:
                        inv_std(2 * s + 2, t - 2, f"x_stats{s + 1}", f"x_rstd{s + 1}")

            nc.gpsimd.memset(epst[:, :], EPS).then_inc(sem("eps_set"), 1)
            pool.wait_ge(sem("consts_in"), 6 * 16)
            for t in range(NT):
                inv_std(0, t, "x_stats0", "x_rstd0")
            for t in range(NT):
                for j in range(2):
                    u = 2 * t + j
                    pool.wait_ge(sem("rotated"), u + 1)
                    nc.gpsimd.tensor_tensor(qk[:, j, t, :], rot_c[:, j, :], rot_s[:, j, :], ALU.add).then_inc(sem("qk_ready"), 1)
            norm_out(0)

            def ffn(s):
                for v_ in range(len(HT) + 1):
                    if v_ < len(HT):
                        m, n = v_, hid(v_)
                        for g in range(2):
                            pool.wait_ge(sem(f"whi{s}"), 3 * m + g + 1)
                            if m >= 2:
                                pool.wait_ge(sem(f"gu{s}"), 2 * (m - 1))
                            r = 2 * (m % 2) + g
                            nc.gpsimd.tensor_tensor(wgu_lo[:, r, :, 0:n], wgu_raw[:, r, :, 0:n],
                                                    wgu_hi[:, r, :, 0:n].bitcast(F32), ALU.subtract).then_inc(sem(f"wlo{s}"), 1)
                        pool.wait_ge(sem(f"whi{s}"), 3 * m + 3)
                        if m >= RING:
                            pool.wait_ge(sem(f"down{s}"), NT)
                        nc.gpsimd.tensor_tensor(wd_lo[0:n, m % RING, :], wd_raw[0:n, m % 2, :],
                                                wd_hi[0:n, m % RING, :].bitcast(F32), ALU.subtract).then_inc(sem(f"wlo{s}"), 1)
                    if v_ >= 1:
                        m, n = v_ - 1, hid(v_ - 1)
                        for hf_ in range(2):
                            u = 2 * m + hf_
                            pool.wait_ge(sem(f"h_hi{s}"), u + 1)
                            if m >= RING:
                                pool.wait_ge(sem(f"down{s}"), NT)
                            nc.gpsimd.tensor_tensor(h_lo[0:n, m % RING, hf_ * 512:hf_ * 512 + 512], hf[0:n, u % 2, :],
                                                    h_hi[0:n, m % RING, hf_ * 512:hf_ * 512 + 512].bitcast(F32),
                                                    ALU.subtract).then_inc(sem(f"h_lo{s}"), 1)

            ffn(1)
            norm_out(1)
            pool.wait_ge(sem("p_sq"), 1)
            nc.gpsimd.tensor_tensor(pw[:, 1, :], pw[:, 0, :], neghalf[:, 0:4], ALU.pow).then_inc(sem("p_inv"), 1)
            for l in range(DEPTH):
                pool.wait_ge(sem("mix_silu"), l + 1)
                nc.gpsimd.tensor_tensor(wk[:, 4, :], wk[:, 2, :], sn[:, l, :], ALU.mult).then_inc(sem("sin_mod"), 1)
                pool.wait_ge(sem("sin_scan"), l + 1)
                nc.gpsimd.tensor_tensor(wk[:, 8, :], wk[:, 6, :], sn[:, l, :], ALU.mult).then_inc(sem("sin_demod"), 1)
            norm_out(2)
            ffn(3)
            norm_out(3)

        @block.scalar
        def _(act):
            def xt_tile(s, t):
                if 0 <= t < NT:
                    act.wait_ge(sem(f"xt_psum{s}"), t + 1)
                    nc.scalar.activation(xt_hi[:, :, t * P:(t + 1) * P], bank[6 + t % 2][:, :].rearrange("p (k n) -> p k n", k=KD),
                                         ACT.Copy).then_inc(sem(f"xt_hi{s}"), 1)

            for t in range(NT):
                xt_tile(0, t)
            for j in range(3):
                act.wait_ge(sem("w_in"), 16 * (j + 1))
                nc.scalar.activation(w_hi[:, j, :, :], w_raw[:, :, :], ACT.Copy).then_inc(sem("w_split_hi"), 1)
            for t in range(NT):
                act.wait_ge(sem("proj"), 3 * t + 3)
                nc.scalar.activation(v[:, t, :], bank[(3 * t + 2) % 6][:, :], ACT.Copy).then_inc(sem("v_ready"), 1)
            act.wait_ge(sem("w_in"), 64)
            act.wait_ge(sem("proj"), 3 * NT)
            nc.scalar.activation(w_hi[:, 0, :, :], w_raw[:, :, :], ACT.Copy).then_inc(sem("w_split_hi"), 1)
            act.wait_ge(sem("w_in"), 80)
            act.wait_ge(sem("qk_ready"), 2 * NT)
            nc.scalar.activation(spread[:, :, :, :], w_raw[:, :, :].rearrange("p a (b c) -> p a b c", b=4), ACT.Copy).then_inc(sem("spread_ready"), 1)
            act.wait_ge(sem("spread_ready"), 1)

            def block_hi(n):
                for j in range(2):
                    act.wait_ge(sem("block_psum"), 2 * n + j + 1)
                    nc.scalar.activation(w_hi[:, 1 + n % 2, j, :], bank[6 + j][:, :], ACT.Copy).then_inc(sem("block_hi"), 1)

            def stack_q(g):
                act.wait_ge(sem("stack_psum"), 2 * g + 1)
                nc.scalar.activation(stack[:, g % 2, 0, :], bank[6][:, :], ACT.Copy).then_inc(sem("stack_q"), 1)

            def evac(u):
                i = UNITS[u][2]
                act.wait_ge(sem("pt_psum"), u + 1)
                if u >= 2:
                    act.wait_ge(sem("pv"), u - 1)
                nc.scalar.activation(probs_t[:, u % 2, 0:(i + 1) * P], bank[2 + u % 2][:, 0:(i + 1) * P],
                                     ACT.Copy).then_inc(sem("pt_act"), 1)

            block_hi(0)
            stack_q(0)
            for u, (b, h, i) in enumerate(UNITS):
                g = u // UP
                if u % UP == 1 and (g + 1) % 4 == 0 and g + 1 < len(PAIRS):
                    block_hi((g + 1) // 4)
                if u % UP == 4 and g + 1 < len(PAIRS):
                    stack_q(g + 1)
                act.wait_ge(sem("row_max"), u + 1)
                if u >= 3:
                    act.wait_ge(sem("pt_psum"), u - 2)
                nc.scalar.activation(probs[:, u % 3, 0:(i + 1) * P], bank[u % 2][:, 0:(i + 1) * P], ACT.Exp,
                                     bias=negmax[:, u:u + 1], accum_out=esum[:, u:u + 1]).then_inc(sem("exp"), 1)
                if u >= 1 and (u - 1) % 2 == 1:
                    evac(u - 1)
            evac(len(UNITS) - 1)
            for t in range(NT + XT_LAG + 1):
                if t < NT:
                    act.wait_ge(sem("o_psum"), t + 1)
                    if t >= 2:
                        act.wait_ge(sem("wo_done"), t - 1)
                    nc.scalar.activation(o_hi[:, t % 2, :, :], bank[4 + t % 2][:, :].rearrange("p (k n) -> p k n", k=KD),
                                         ACT.Copy).then_inc(sem("o_hi"), 1)
                if 1 <= t <= NT:
                    act.wait_ge(sem("wo_done"), t)
                    nc.scalar.activation(y[:, t - 1, :], bank[(t - 1) % 2][:, :], ACT.Copy).then_inc(sem("y_ready0"), 1)
                xt_tile(1, t - 1 - XT_LAG)

            def ffn(s):
                def w_high(m):
                    n = hid(m)
                    for g in range(2):
                        r = 2 * (m % 2) + g
                        act.wait_ge(sem(f"wfull{s}"), 3 * m + g + 1)
                        if m >= 2:
                            act.wait_ge(sem(f"gu{s}"), 2 * (m - 1))
                        nc.scalar.activation(wgu_hi[:, r, :, 0:n], wgu_raw[:, r, :, 0:n], ACT.Copy).then_inc(sem(f"whi{s}"), 1)

                def wd_high(m):
                    n = hid(m)
                    act.wait_ge(sem(f"wfull{s}"), 3 * m + 3)
                    if m >= RING:
                        act.wait_ge(sem(f"down{s}"), NT)
                    nc.scalar.activation(wd_hi[0:n, m % RING, :], wd_raw[0:n, m % 2, :], ACT.Copy).then_inc(sem(f"whi{s}"), 1)

                def hidden(m):
                    n = hid(m)
                    for hf_ in range(2):
                        u = 2 * m + hf_
                        act.wait_ge(sem(f"gu{s}"), u + 1)
                        if u >= 2:
                            act.wait_ge(sem(f"h_full{s}"), u - 1)
                        nc.scalar.activation(sg[0:n, u % 2, :], bank[2 * (u % 2)][0:n, :], ACT.Silu).then_inc(sem(f"silu{s}"), 1)
                        act.wait_ge(sem(f"h_full{s}"), u + 1)
                        if m >= RING:
                            act.wait_ge(sem(f"down{s}"), NT)
                        nc.scalar.activation(h_hi[0:n, m % RING, hf_ * 512:hf_ * 512 + 512], hf[0:n, u % 2, :],
                                             ACT.Copy).then_inc(sem(f"h_hi{s}"), 1)

                def partial():
                    for t in range(NT):
                        act.wait_ge(sem(f"down{s}"), t + 1)
                        nc.scalar.activation(y[:, t, :], bank[4 + t % 2][:, :], ACT.Copy).then_inc(sem(f"y_part{s}"), 1)

                w_high(0)
                wd_high(0)
                for m in range(len(HT)):
                    if m + 1 < len(HT):
                        w_high(m + 1)
                        if m != GROUPS[0][1]:
                            wd_high(m + 1)
                    hidden(m)
                    if m == GROUPS[0][1]:
                        partial()
                        wd_high(m + 1)

            ffn(1)
            for t in range(NT):
                xt_tile(2, t)
            act.wait_ge(sem("mixer_in"), 160)
            nc.scalar.activation(win_hi[:, :, :], win_raw[:, :, :], ACT.Copy).then_inc(sem("win_hi"), 1)
            act.wait_ge(sem("p_abs"), 1)
            nc.scalar.activation(pw[:, 3, :], pw[:, 2, :], ACT.Tanh).then_inc(sem("decay"), 1)
            act.wait_ge(sem("eps_set"), 1)

            def mix_norm(n):
                act.wait_ge(sem("centred"), n + 1)
                nc.scalar.activation(wk[:, 0, :], bank[0][:, :], ACT.Square).then_inc(sem("mix_sq"), 1)
                act.wait_ge(sem("mix_var"), n + 1)
                nc.scalar.activation(wk[:, 1, :], bank[1][:, :], ACT.Ln, bias=epst[:, 0:1]).then_inc(sem("mix_ln"), 1)
                act.wait_ge(sem("mix_ln"), n + 1)
                nc.scalar.activation(wk[:, 9, :], wk[:, 1, :], ACT.Exp, scale=-0.5).then_inc(sem("mix_rstd"), 1)

            for l in range(DEPTH):
                mix_norm(2 * l)
                act.wait_ge(sem("mix_norm"), 2 * l + 1)
                nc.scalar.activation(wk[:, 2, :], wk[:, 7, :], ACT.Silu, bias=chan[:, 1, l:l + 1],
                                     scale=chan[:, 0, l:l + 1]).then_inc(sem("mix_silu"), 1)
                mix_norm(2 * l + 1)
                for f in range(2):
                    for b in range(B):
                        act.wait_ge(sem("mix_up"), 4 * l + 2 * f + b + 1)
                        nc.scalar.activation(g1[:, 2 * f + b, :], bank[2 + 2 * f + b][:, :], ACT.Silu,
                                             bias=b1[:, l, f:f + 1]).then_inc(sem("mix_act"), 1)
            mix_norm(2 * DEPTH)
            for t in range(NT):
                xt_tile(3, t)
            ffn(3)

        @block.vector
        def _(dve):
            dve_steps = [0]

            def link(ins):
                dve_steps[0] += 1
                ins.then_inc(sem("dve_step"), 1)
                dve.wait_ge(sem("dve_step"), dve_steps[0])

            def stats(n, t, src, done):
                link(nc.vector.bn_stats(bnst[:, :], src))
                nc.vector.bn_aggr(mv[:, n, t, :], bnst[:, :]).then_inc(sem(done), 1)
                dve.wait_ge(sem(done), t + 1)

            def norm_x(s, t):
                dve.wait_ge(sem(f"x_rstd{s}"), t + 1)
                if t >= 2:
                    dve.wait_ge(sem(f"xt_psum{s}"), t - 1)
                nc.vector.tensor_scalar(xn[:, t % 2, :], x[:, t, :], mv[:, 2 * s, t, 0:1], rstd[:, 2 * s, t:t + 1],
                                        ALU.subtract, ALU.mult).then_inc(sem(f"xn{s}"), 1)

            def low_xt(s, t):
                dve.wait_ge(sem(f"xt_hi{s}"), t + 1)
                nc.vector.tensor_tensor(xt_lo[:, :, t * P:(t + 1) * P], bank[6 + t % 2][:, :].rearrange("p (k n) -> p k n", k=KD),
                                        xt_hi[:, :, t * P:(t + 1) * P].bitcast(F32), ALU.subtract).then_inc(sem(f"xt_ready{s}"), 1)

            def norm_out(s, make_y=None):
                for t in range(NT + XT_LAG):
                    if t < NT:
                        if make_y:
                            make_y(t)
                        dve.wait_ge(sem(f"y_ready{s}"), t + 1)
                        stats(2 * s + 1, t, y[:, t, :], f"y_stats{s}")
                    if 1 <= t <= NT:
                        dve.wait_ge(sem(f"y_rstd{s}"), t)
                        nc.vector.tensor_scalar(y[:, t - 1, :], y[:, t - 1, :], mv[:, 2 * s + 1, t - 1, 0:1],
                                                rstd[:, 2 * s + 1, t - 1:t], ALU.subtract, ALU.mult).then_inc(sem(f"y_norm{s}"), 1)
                    if s < 3:
                        if 2 <= t <= NT + 1:
                            dve.wait_ge(sem(f"x_sum{s}"), t - 1)
                            stats(2 * s + 2, t - 2, x[:, t - 2, :], f"x_stats{s + 1}")
                        if 3 <= t <= NT + 2:
                            norm_x(s + 1, t - 3)
                        if t >= 4:
                            low_xt(s + 1, t - 4)

            for t in range(NT + 2):
                if t < NT:
                    dve.wait_ge(sem(f"x_in{t}"), 16)
                    stats(0, t, x[:, t, :], "x_stats0")
                if 1 <= t <= NT:
                    norm_x(0, t - 1)
                if t >= 2:
                    low_xt(0, t - 2)

            def w_low(j, dst):
                dve.wait_ge(sem("w_split_hi"), j + 1)
                nc.vector.tensor_tensor(w_lo[:, dst, :, :], w_raw[:, :, :], w_hi[:, dst, :, :].bitcast(F32),
                                        ALU.subtract).then_inc(sem("w_split"), 1)

            dve.wait_ge(sem("consts_in"), 6 * 16)
            for j in range(3):
                w_low(j, j)
            for t in range(NT):
                for j in range(2):
                    u = 2 * t + j
                    dve.wait_ge(sem("proj"), 3 * t + j + 1)
                    if t:
                        dve.wait_ge(sem("qk_ready"), u - 1)
                    src = bank[(3 * t + j) % 6][:, :].rearrange("p (h d) -> p h d", h=H)
                    cs = rope_c[:, j, t % TB, :].unsqueeze(1).to_broadcast([P, H, HD])
                    nc.vector.tensor_tensor(rot_c[:, j, :].rearrange("p (h d) -> p h d", h=H), src, cs, ALU.mult)
                    src = bank[(3 * t + j) % 6][:, :].rearrange("p (h f two) -> p h f two", h=H, two=2)
                    dst = rot_s[:, j, :].rearrange("p (h f two) -> p h f two", h=H, two=2)
                    ss = rope_s[:, j, t % TB, :].rearrange("p (f two) -> p f two", two=2)
                    for e in range(2):
                        ins = nc.vector.tensor_tensor(dst[:, :, :, e], src[:, :, :, 1 - e],
                                                      ss[:, :, e].unsqueeze(1).to_broadcast([P, H, HD // 2]), ALU.mult)
                    ins.then_inc(sem("rotated"), 1)
            w_low(3, 0)
            dve.wait_ge(sem("w_split"), 4)
            dve.wait_ge(sem("spread_ready"), 1)

            def block_lo(n):
                for j in range(2):
                    dve.wait_ge(sem("block_hi"), 2 * n + j + 1)
                    nc.vector.tensor_tensor(w_lo[:, 1 + n % 2, j, :], bank[6 + j][:, :], w_hi[:, 1 + n % 2, j, :].bitcast(F32),
                                            ALU.subtract).then_inc(sem("block_split"), 1)

            def stack_k(g):
                dve.wait_ge(sem("stack_psum"), 2 * g + 2)
                nc.vector.tensor_copy(stack[:, g % 2, 1, :], bank[7][:, :]).then_inc(sem("stack_k"), 1)

            def evac(u):
                i = UNITS[u][2]
                dve.wait_ge(sem("pt_psum"), u + 1)
                if u >= 2:
                    dve.wait_ge(sem("pv"), u - 1)
                nc.vector.tensor_copy(probs_t[:, u % 2, 0:(i + 1) * P], bank[2 + u % 2][:, 0:(i + 1) * P]).then_inc(sem("pt_dve"), 1)

            def finish_pair(g):
                b, p = PAIRS[g]
                dve.wait_ge(sem("exp"), UP * (g + 1))
                dve.wait_ge(sem("pv"), UP * (g + 1))
                link(nc.vector.reciprocal(einv[:, UP * g:UP * g + UP], esum[:, UP * g:UP * g + UP]))
                src = bank[4 + g % 2][:, 0:UP * HD].rearrange("p (h i d) -> p i h d", h=2, i=TB)
                inv = einv[:, UP * g:UP * g + UP].rearrange("p (h i) -> p i h", h=2).unsqueeze(3).to_broadcast([P, TB, 2, HD])
                dst = y[:, TB * b:TB * b + TB, 2 * HD * p:2 * HD * p + 2 * HD].rearrange("p i (h d) -> p i h d", h=2)
                nc.vector.tensor_tensor(dst, src, inv, ALU.mult).then_inc(sem("o_ready"), 1)

            block_lo(0)
            stack_k(0)
            for u, (b, h, i) in enumerate(UNITS):
                g = u // UP
                if u % UP == 1 and (g + 1) % 4 == 0 and g + 1 < len(PAIRS):
                    block_lo((g + 1) // 4)
                if u % UP == 4 and g + 1 < len(PAIRS):
                    stack_k(g + 1)
                dve.wait_ge(sem("scores"), u + 1)
                nc.vector.tensor_reduce(negmax[:, u:u + 1], bank[u % 2][:, 0:(i + 1) * P], AX_X, ALU.max,
                                        negate=True).then_inc(sem("row_max"), 1)
                if u >= 1 and (u - 1) % 2 == 0:
                    evac(u - 1)
                if u % UP == 3 and u // UP:
                    finish_pair(u // UP - 1)
            finish_pair(len(PAIRS) - 1)
            def turned_low(t):
                dve.wait_ge(sem("o_hi"), t + 1)
                nc.vector.tensor_tensor(o_lo[:, t % 2, :, :], bank[4 + t % 2][:, :].rearrange("p (k n) -> p k n", k=KD),
                                        o_hi[:, t % 2, :, :].bitcast(F32), ALU.subtract).then_inc(sem("o_split"), 1)

            norm_out(0, turned_low)

            def ffn(s):
                prep = "prep%d" % s

                def full(m, c):
                    n, q = hid(m), 3 * m + c
                    dve.wait_ge(sem(f"wraw{s}_{m % 2}"), 48 * (m // 2 + 1))
                    if c < 2:
                        r = 2 * (m % 2) + c
                        w, ps = wgu_raw[:, r, :, 0:n], bank[6 + q % 2][:, :].rearrange("p (k n) -> p k n", k=KD)[:, :, 0:n]
                    else:
                        w, ps = wd_raw[0:n, m % 2, :], bank[6 + q % 2][0:n, :]
                    if s == 1:
                        dve.wait_ge(sem(prep), q + 1)
                        nc.vector.tensor_tensor(w, w, ps, ALU.add).then_inc(sem(f"wfull{s}"), 1)
                        return
                    wi = w.bitcast(I32)
                    if c < 2:
                        link(nc.vector.tensor_scalar(wi, wi, shifts[:, 4, 0:1], shifts[:, 4, 1:2],
                                                     ALU.logical_shift_left, ALU.arith_shift_right))
                    else:
                        for e in range(4):
                            part = wi.rearrange("p (d e) -> p d e", e=4)[:, :, e]
                            ins = nc.vector.tensor_scalar(part, part, shifts[0:n, e, 0:1], shifts[0:n, e, 1:2],
                                                          ALU.logical_shift_left, ALU.arith_shift_right)
                        link(ins)
                    dve.wait_ge(sem(prep), q + 1)
                    if c < 2:
                        nc.vector.tensor_tensor(w, wi, ps, ALU.mult).then_inc(sem(f"wfull{s}"), 1)
                    else:
                        nc.vector.tensor_tensor(w.rearrange("p (e two) -> p two e", two=2), wi.rearrange("p (e two) -> p two e", two=2),
                                                ps.rearrange("p (two e) -> p two e", two=2), ALU.mult).then_inc(sem(f"wfull{s}"), 1)

                def hidden(m):
                    n = hid(m)
                    for hf_ in range(2):
                        u = 2 * m + hf_
                        dve.wait_ge(sem(f"silu{s}"), u + 1)
                        if u >= 2:
                            dve.wait_ge(sem(f"h_lo{s}"), u - 1)
                        nc.vector.tensor_tensor(hf[0:n, u % 2, :], sg[0:n, u % 2, :], bank[2 * (u % 2) + 1][0:n, :],
                                                ALU.mult).then_inc(sem(f"h_full{s}"), 1)

                if s == 3:
                    dve.wait_ge(sem("side_in3"), 144)
                for c in range(3):
                    full(0, c)
                for m in range(len(HT)):
                    if m + 1 < len(HT):
                        for c in range(3):
                            full(m + 1, c)
                    hidden(m)

                def make_y(t):
                    dve.wait_ge(sem(f"down{s}"), NT + t + 1)
                    dve.wait_ge(sem(f"y_part{s}"), t + 1)
                    nc.vector.tensor_tensor(y[:, t, :], y[:, t, :], bank[4 + t % 2][:, :], ALU.add).then_inc(sem(f"y_ready{s}"), 1)

                norm_out(s, make_y)

            ffn(1)

            dve.wait_ge(sem("mixer_in"), 160)
            dve.wait_ge(sem("win_hi"), 1)
            nc.vector.tensor_tensor(win_lo[:, :, :], win_raw[:, :, :], win_hi[:, :, :].bitcast(F32), ALU.subtract).then_inc(sem("win_split"), 1)
            PR, PI, LR, LI = 2, 3, 4, 5
            link(nc.vector.tensor_tensor(pw[:, 4, :], chan[:, PR, :], chan[:, PR, :], ALU.mult))
            link(nc.vector.tensor_tensor(pw[:, 5, :], chan[:, PI, :], chan[:, PI, :], ALU.mult))
            link(nc.vector.tensor_tensor(pw[:, 10, :], pw[:, 4, :], pw[:, 5, :], ALU.add))
            link(nc.vector.tensor_scalar(pw[:, 11, :], pw[:, 10, :], 0.0, None, ALU.is_equal))
            nc.vector.tensor_tensor(pw[:, 0, :], pw[:, 10, :], pw[:, 11, :], ALU.add).then_inc(sem("p_sq"), 1)
            dve.wait_ge(sem("p_inv"), 1)
            nc.vector.tensor_tensor(pw[:, 2, :], pw[:, 10, :], pw[:, 1, :], ALU.mult).then_inc(sem("p_abs"), 1)
            link(nc.vector.tensor_tensor(step_c[:, 0, :], chan[:, PR, :], pw[:, 1, :], ALU.mult))
            link(nc.vector.tensor_tensor(step_c[:, 0, :], step_c[:, 0, :], pw[:, 11, :], ALU.add))
            link(nc.vector.tensor_tensor(step_s[:, 0, :], chan[:, PI, :], pw[:, 1, :], ALU.mult))

            def complex_mul(dc, ds, ac, as_, bc, bs, t1, t2):
                link(nc.vector.tensor_tensor(t1, ac, bc, ALU.mult))
                link(nc.vector.tensor_tensor(t2, as_, bs, ALU.mult))
                link(nc.vector.tensor_tensor(dc, t1, t2, ALU.subtract))
                link(nc.vector.tensor_tensor(t1, ac, bs, ALU.mult))
                link(nc.vector.tensor_tensor(t2, as_, bc, ALU.mult))
                link(nc.vector.tensor_tensor(ds, t1, t2, ALU.add))

            link(nc.vector.memset(ct[:, :, 0:1], 1.0))
            link(nc.vector.memset(sn[:, :, 0:1], 0.0))
            n, k = 1, 0
            while n < S:
                sc = step_c[:, k, :].unsqueeze(2).to_broadcast([P, DEPTH, n])
                ss = step_s[:, k, :].unsqueeze(2).to_broadcast([P, DEPTH, n])
                complex_mul(ct[:, :, n:2 * n], sn[:, :, n:2 * n], ct[:, :, 0:n], sn[:, :, 0:n], sc, ss,
                            tw[:, 0, :, 0:n], tw[:, 1, :, 0:n])
                complex_mul(step_c[:, k + 1, :], step_s[:, k + 1, :], step_c[:, k, :], step_s[:, k, :],
                            step_c[:, k, :], step_s[:, k, :], pw[:, 4, :], pw[:, 5, :])
                n, k = 2 * n, k + 1
            complex_mul(pw[:, 6, :], pw[:, 7, :], chan[:, LR, :], chan[:, LI, :], step_c[:, 0, :], step_s[:, 0, :],
                        pw[:, 4, :], pw[:, 5, :])
            link(nc.vector.tensor_scalar(pw[:, 8, :], pw[:, 7, :], -1.0, None, ALU.mult))
            for b in range(B):
                rows = slice(C * b, C * b + C)
                dve.wait_ge(sem("mix_in"), b + 1)
                link(nc.vector.tensor_scalar(hm[rows, :], bank[b][rows, :], last[rows, 0:1], None, ALU.add))
            dve.wait_ge(sem("decay"), 1)
            nc.vector.tensor_copy(wk[:, 9, 0:1], hm[:, 0:1]).then_inc(sem("h_ready"), 1)

            def mix_norm(n):
                dve.wait_ge(sem("mix_rstd"), n + 1)
                nc.vector.tensor_tensor(wk[:, 7, :], bank[0][:, :], wk[:, 9, :], ALU.mult).then_inc(sem("mix_norm"), 1)

            for l in range(DEPTH):
                mix_norm(2 * l)
                dve.wait_ge(sem("mix_silu"), l + 1)
                link(nc.vector.tensor_tensor(wk[:, 3, :], wk[:, 2, :], ct[:, l, :], ALU.mult))
                decay = pw[:, 3, l:l + 1].to_broadcast([P, S])
                link(nc.vector.tensor_tensor_scan(wk[:, 5, :], decay, wk[:, 3, :], pw[:, 6, l:l + 1], ALU.mult, ALU.add))
                dve.wait_ge(sem("sin_mod"), l + 1)
                nc.vector.tensor_tensor_scan(wk[:, 6, :], decay, wk[:, 4, :], pw[:, 8, l:l + 1], ALU.mult, ALU.add).then_inc(sem("sin_scan"), 1)
                link(nc.vector.tensor_tensor(wk[:, 7, :], wk[:, 5, :], ct[:, l, :], ALU.mult))
                dve.wait_ge(sem("sin_demod"), l + 1)
                link(nc.vector.tensor_tensor(wk[:, 7, :], wk[:, 7, :], wk[:, 8, :], ALU.add))
                nc.vector.scalar_tensor_tensor(out=hm[:, :], in0=wk[:, 7, :], scalar=chan[:, 6, l:l + 1], in1=hm[:, :],
                                               op0=ALU.mult, op1=ALU.add).then_inc(sem("h_ready"), 1)
                dve.wait_ge(sem("h_ready"), 2 * l + 2)
                mix_norm(2 * l + 1)
                dve.wait_ge(sem("mix_norm"), 2 * l + 2)
                nc.vector.tensor_scalar(wk[:, 8, :], wk[:, 7, :], chan[:, 7, l:l + 1], chan[:, 8, l:l + 1],
                                        ALU.mult, ALU.add).then_inc(sem("mix_affine"), 1)
                dve.wait_ge(sem("mix_down"), l + 1)
                nc.vector.scalar_tensor_tensor(out=hm[:, :], in0=bank[6][:, :], scalar=chan[:, 9, l:l + 1], in1=hm[:, :],
                                               op0=ALU.add, op1=ALU.add).then_inc(sem("h_ready"), 1)
                dve.wait_ge(sem("h_ready"), 2 * l + 3)
            mix_norm(2 * DEPTH)
            dve.wait_ge(sem("mix_norm"), 2 * DEPTH + 1)
            nc.vector.tensor_scalar(wk[:, 8, :], wk[:, 7, :], last[:, 1:2], last[:, 2:3], ALU.mult, ALU.add).then_inc(sem("mix_affine"), 1)

            def mixer_y(t):
                dve.wait_ge(sem("mix_out"), t + 1)
                nc.vector.tensor_tensor(y[:, t, :], bank[2 + t % 2][:, :], bout[:, :], ALU.add).then_inc(sem("y_ready2"), 1)

            norm_out(2, mixer_y)
            ffn(3)

        @block.tensor
        def _(pe):
            def xt_tile(s, t):
                if 0 <= t < NT:
                    pe.wait_ge(sem(f"xn{s}"), t + 1)
                    if t >= 2:
                        pe.wait_ge(sem(f"xt_ready{s}"), t - 1)
                    for k in range(KD):
                        ins = nc.tensor.transpose(bank[6 + t % 2][:, k * P:(k + 1) * P], xn[:, t % 2, k * P:(k + 1) * P], ident[:, :])
                    ins.then_inc(sem(f"xt_psum{s}"), 1)

            def split_product(dst, lhs, rhs, ks, start=True, stop=True):
                todo = [(k, i, j) for k in ks for i, j in COMBOS]
                for n, (k, i, j) in enumerate(todo):
                    ins = nc.tensor.matmul(dst, lhs(i, k), rhs(j, k), start=start and n == 0, stop=stop and n == len(todo) - 1)
                return ins

            pe.wait_ge(sem("consts_in"), 6 * 16)
            for t in range(NT):
                xt_tile(0, t)
            pe.wait_ge(sem("xt_ready0"), NT)
            W = (w_hi, w_lo)
            for t in range(NT):
                for j in range(3):
                    u = 3 * t + j
                    if t == 0:
                        pe.wait_ge(sem("w_split"), j + 1)
                    if t >= 2:
                        pe.wait_ge(sem("v_ready" if j == 2 else "rotated"), t - 1 if j == 2 else 2 * (t - 2) + j + 1)
                    split_product(bank[u % 6][:, :], lambda i, k: XT[i][:, k, t * P:(t + 1) * P],
                                  lambda i, k: W[i][:, j, k, :], range(KD)).then_inc(sem("proj"), 1)

            pe.wait_ge(sem("qk_ready"), 2 * NT)
            pe.wait_ge(sem("v_ready"), NT)

            def turn_block(n):
                b, c = divmod(n, KD)
                if n:
                    pe.wait_ge(sem("stack_q"), 4 * n)
                    pe.wait_ge(sem("stack_k"), 4 * n)
                for j in range(2):
                    for i in range(TB):
                        ins = nc.tensor.transpose(bank[6 + j][:, i * P:(i + 1) * P], qk[:, j, TB * b + i, c * P:(c + 1) * P], ident[:, :])
                    ins.then_inc(sem("block_psum"), 1)

            def stacks(g):
                n = g // 4
                for j in range(2):
                    if g % 4 == 0:
                        pe.wait_ge(sem("block_split"), 2 * n + j + 1)
                    else:
                        pe.wait_ge(sem("stack_k" if j else "stack_q"), g)
                    for part in range(2):
                        ins = nc.tensor.matmul(bank[6 + j][:, :], spread[:, 2 * j + part, g % 4, :], W[part][:, 1 + n % 2, j, :],
                                               start=(part == 0), stop=(part == 1))
                    ins.then_inc(sem("stack_psum"), 1)

            def scores(u):
                b, h, i = UNITS[u]
                g = u // UP
                if u % UP == 0:
                    pe.wait_ge(sem("stack_q"), g + 1)
                    pe.wait_ge(sem("stack_k"), g + 1)
                if u >= 2:
                    pe.wait_ge(sem("exp"), u - 1)
                rows = slice(64 * (h % 2), 64 * (h % 2) + 64)
                dst = bank[u % 2]
                nc.tensor.matmul(dst[:, 0:(i + 1) * P], stack[rows, g % 2, 0, i * P:(i + 1) * P],
                                 stack[rows, g % 2, 1, 0:(i + 1) * P], start=True, stop=False)
                nc.tensor.matmul(dst[:, i * P:(i + 1) * P], ident16[:, :], causal16[:, :], start=False, stop=True).then_inc(sem("scores"), 1)

            def turn(u):
                i = UNITS[u][2]
                pe.wait_ge(sem("exp"), u + 1)
                if u >= 2:
                    pe.wait_ge(sem("pt_dve" if u % 2 == 0 else "pt_act"), (u - 2) // 2 + 1)
                for k in range(i + 1):
                    ins = nc.tensor.transpose(bank[2 + u % 2][:, k * P:(k + 1) * P], probs[:, u % 3, k * P:(k + 1) * P], ident[:, :])
                ins.then_inc(sem("pt_psum"), 1)

            def weighted(u):
                b, h, i = UNITS[u]
                g = u // UP
                pe.wait_ge(sem("pt_dve" if u % 2 == 0 else "pt_act"), u // 2 + 1)
                if u % UP == 0 and g >= 2:
                    pe.wait_ge(sem("o_ready"), g - 1)
                col = (u % UP) * HD
                for k in range(i + 1):
                    ins = nc.tensor.matmul(bank[4 + g % 2][:, col:col + HD], probs_t[:, u % 2, k * P:(k + 1) * P],
                                           v[:, TB * b + k, HD * h:HD * h + HD], start=(k == 0), stop=(k == i))
                ins.then_inc(sem("pv"), 1)

            pe.wait_ge(sem("spread_ready"), 1)
            turn_block(0)
            stacks(0)
            scores(0)
            scores(1)
            for u in range(len(UNITS)):
                g = u // UP
                if u % UP == 0 and (g + 1) % 4 == 0 and g + 1 < len(PAIRS):
                    turn_block((g + 1) // 4)
                if u % UP == 3 and g + 1 < len(PAIRS):
                    stacks(g + 1)
                turn(u)
                if u + 2 < len(UNITS):
                    scores(u + 2)
                if u:
                    weighted(u - 1)
            weighted(len(UNITS) - 1)
            pe.wait_ge(sem("o_ready"), len(PAIRS))
            for t in range(NT + XT_LAG + 1):
                if t < NT:
                    if t >= 2:
                        pe.wait_ge(sem("o_split"), t - 1)
                    for k in range(KD):
                        ins = nc.tensor.transpose(bank[4 + t % 2][:, k * P:(k + 1) * P], y[:, t, k * P:(k + 1) * P], ident[:, :])
                    ins.then_inc(sem("o_psum"), 1)
                if 1 <= t <= NT:
                    c = t - 1
                    pe.wait_ge(sem("o_split"), c + 1)
                    if c >= 2:
                        pe.wait_ge(sem("y_ready0"), c - 1)
                    split_product(bank[c % 2][:, :], lambda i, k: (o_hi, o_lo)[i][:, c % 2, k, :],
                                  lambda i, k: W[i][:, 0, k, :], range(KD)).then_inc(sem("wo_done"), 1)
                xt_tile(1, t - 1 - XT_LAG)

            def ffn(s):
                def prep(m):
                    h0, n = HT[m]
                    for c in range(3):
                        q = 3 * m + c
                        if q >= 2:
                            pe.wait_ge(sem(f"wfull{s}"), q - 1)
                        elif q == 0:
                            pe.wait_ge(sem(f"side_in{s}"), 96 if s == 1 else 144)
                            pe.wait_ge(sem(f"xt_ready{s}"), NT)
                        dst = bank[6 + q % 2]
                        if c < 2:
                            for k in range(KD):
                                if s == 1:
                                    lhs, rhs = lora_b[32 * c:32 * c + RANK, k * P:(k + 1) * P], lora_a[32 * c:32 * c + RANK, h0:h0 + n]
                                else:
                                    lhs, rhs = s4sel[32 * c:32 * c + 8, k, :], s4[32 * c:32 * c + 8, h0:h0 + n]
                                ins = nc.tensor.matmul(dst[:, k * P:k * P + n], lhs, rhs, start=True, stop=True)
                        elif s == 1:
                            ins = nc.tensor.matmul(dst[0:n, :], lora_a[64:64 + RANK, h0:h0 + n], lora_b[64:64 + RANK, :], start=True, stop=True)
                        else:
                            for e in range(2):
                                if e:
                                    ins.then_inc(sem("scales_even"), 1)
                                    pe.wait_ge(sem("scales_even"), m + 1)
                                ins = nc.tensor.matmul(dst[0:n, e * 256:e * 256 + 256], s4dsel[64 * e:64 * e + 43, h0:h0 + n], s4d[64 * e:64 * e + 43, :], start=True, stop=True)
                        ins.then_inc(sem(f"prep{s}"), 1)

                def gate_up(m):
                    n = hid(m)
                    for hf_ in range(2):
                        u = 2 * m + hf_
                        pe.wait_ge(sem(f"wlo{s}"), 3 * m + 2)
                        if u >= 2:
                            pe.wait_ge(sem(f"h_full{s}"), u - 1)
                        for g in range(2):
                            ins = split_product(bank[2 * (u % 2) + g][0:n, :],
                                                lambda i, k: (wgu_hi, wgu_lo)[i][:, 2 * (m % 2) + g, k, 0:n],
                                                lambda i, k: XT[i][:, k, hf_ * 512:hf_ * 512 + 512], range(KD))
                        ins.then_inc(sem(f"gu{s}"), 1)

                def down(gq):
                    m0, m1 = GROUPS[gq]
                    pe.wait_ge(sem(f"h_lo{s}"), 2 * m1)
                    pe.wait_ge(sem(f"wlo{s}"), 3 * m1)
                    for t in range(NT):
                        if t >= 2:
                            pe.wait_ge(sem(f"y_ready{s}" if gq else f"y_part{s}"), t - 1)
                        elif gq:
                            pe.wait_ge(sem(f"y_part{s}"), NT)
                        todo = [(m, i, j) for m in range(m0, m1) for i, j in COMBOS]
                        for c, (m, i, j) in enumerate(todo):
                            n = hid(m)
                            ins = nc.tensor.matmul(bank[4 + t % 2][:, :], (h_hi, h_lo)[i][0:n, m % RING, t * P:(t + 1) * P],
                                                   (wd_hi, wd_lo)[j][0:n, m % RING, :], start=(c == 0), stop=(c == len(todo) - 1))
                        ins.then_inc(sem(f"down{s}"), 1)
                        if gq and s < 3:
                            xt_tile(s + 1, t - XT_LAG)

                prep(0)
                for m in range(len(HT)):
                    if m + 1 < len(HT):
                        prep(m + 1)
                    gate_up(m)
                    if m == GROUPS[0][1]:
                        down(0)
                down(1)

            ffn(1)
            for t in range(NT - XT_LAG, NT):
                xt_tile(2, t)
            pe.wait_ge(sem("xt_ready2"), NT)
            pe.wait_ge(sem("win_split"), 1)
            for b in range(B):
                split_product(bank[b][:, :], lambda i, k: (win_hi, win_lo)[i][:, k, :],
                              lambda i, k: XT[i][:, k, b * S:(b + 1) * S], range(KD)).then_inc(sem("mix_in"), 1)

            def mix_norm(n):
                pe.wait_ge(sem("h_ready"), n + 1)
                nc.tensor.matmul(bank[0][:, :], cmat[:, :], hm[:, :], start=True, stop=True).then_inc(sem("centred"), 1)
                pe.wait_ge(sem("mix_sq"), n + 1)
                nc.tensor.matmul(bank[1][:, :], bmat[:, :], wk[:, 0, :], start=True, stop=True).then_inc(sem("mix_var"), 1)

            for l in range(DEPTH):
                mix_norm(2 * l)
                mix_norm(2 * l + 1)
                pe.wait_ge(sem("mix_affine"), l + 1)
                for f in range(2):
                    for b in range(B):
                        rows = slice(C * b, C * b + C)
                        nc.tensor.matmul(bank[2 + 2 * f + b][:, :], w1t[rows, l, f * P:(f + 1) * P], wk[rows, 8, :],
                                         start=True, stop=True).then_inc(sem("mix_up"), 1)
                pe.wait_ge(sem("mix_act"), 4 * l + 4)
                for b in range(B):
                    for f in range(2):
                        ins = nc.tensor.matmul(bank[6][C * b:C * b + C, :], w2t[:, l, f, :], g1[:, 2 * f + b, :],
                                               start=(f == 0), stop=(f == 1))
                ins.then_inc(sem("mix_down"), 1)
            mix_norm(2 * DEPTH)
            pe.wait_ge(sem("mix_affine"), DEPTH + 1)
            for t in range(NT + XT_LAG):
                if t < NT:
                    rows = slice(C * (t // TB), C * (t // TB) + C)
                    if t >= 2:
                        pe.wait_ge(sem("y_ready2"), t - 1)
                    nc.tensor.matmul(bank[2 + t % 2][:, :], wk[rows, 8, (t % TB) * P:(t % TB + 1) * P], wout[rows, :],
                                     start=True, stop=True).then_inc(sem("mix_out"), 1)
                xt_tile(3, t - XT_LAG)
            ffn(3)


def kernel(**inputs):
    import numpy as np
    import concourse.bacc as bacc
    from concourse import mybir as _mybir
    from concourse.bass_utils import run_bass_kernel_spmd as _run
    import ml_dtypes

    A = {k: np.asarray(w) for k, w in inputs.items()}
    f32 = np.float32
    arr = {}
    arr["x"] = A["L0_attn_x"].reshape(N, D)
    for n in ("wq", "wk", "wv", "wo"):
        arr[n] = A["L0_attn_" + n]
    arr["ident"] = np.eye(P, dtype=f32)
    arr["ident16"] = np.eye(P).astype(ml_dtypes.bfloat16)
    arr["causal16"] = np.where(np.arange(P)[None, :] > np.arange(P)[:, None], -1e30, 0.0).astype(ml_dtypes.bfloat16)
    arr["neghalf"] = np.full((P, 4), -0.5, f32)
    inv = 1.0 / 10000.0 ** (np.arange(0, HD, 2)[:HD // 2].astype(f32) / HD)
    ang = np.outer(np.arange(S), inv).astype(f32)
    cos, sin = np.cos(ang), np.sin(ang)
    c2 = np.stack([cos, cos], -1).reshape(TB, P, HD).transpose(1, 0, 2)
    s2 = np.stack([-sin, sin], -1).reshape(TB, P, HD).transpose(1, 0, 2)
    scale = 1.0 / np.sqrt(f32(HD))
    arr["rope_c"] = np.stack([c2 * scale, c2], 1).astype(f32)
    arr["rope_s"] = np.stack([s2 * scale, s2], 1).astype(f32)
    row = np.arange(P)
    copy = row % 64 // HD
    spread = np.zeros((P, 2, 2, 4, P), f32)
    for j, low in enumerate((copy >= 2, copy % 2 == 1)):
        for pair in range(4):
            for r in row:
                spread[2 * HD * pair + HD * (r // 64) + r % HD, j, int(low[r]), pair, r] = 1.0
    arr["spread"] = spread.reshape(P, 4, D)
    arr["gu_t"] = np.stack([A["L0_ffn_gate_w"].T, A["L0_ffn_up_w"].T])
    arr["down_t"] = A["L0_ffn_down_w"].T
    for n in ("gate", "up"):
        arr[n + "_a"] = A[f"L0_ffn_{n}_a"]
        arr[n + "_bt"] = A[f"L0_ffn_{n}_b"].T
    arr["down_a"] = A["L0_ffn_down_a"]
    arr["down_bt"] = A["L0_ffn_down_b"].T
    def byte_of(w, rows, cols):
        return np.concatenate([w, w], axis=1).reshape(rows, cols).T
    arr["w13"] = np.stack([byte_of(A["L1_ffn_w1"], F, D), byte_of(A["L1_ffn_w3"], F, D)])
    arr["w2"] = byte_of(A["L1_ffn_w2"], D, F)
    arr["s13"] = np.stack([A["L1_ffn_s1"].reshape(F, 8).T, A["L1_ffn_s3"].reshape(F, 8).T])
    arr["s2"] = A["L1_ffn_s2"].reshape(D // 2, 43).T
    sel = np.zeros((8, KD, P), f32)
    for k in range(KD):
        for p in range(P):
            sel[2 * k + p // GROUP4, k, p] = 1.0
    arr["s4sel"] = sel
    dsel = np.zeros((2, 43, F), f32)
    for e in range(2):
        dsel[e, (F * e + np.arange(F)) // GROUP4, np.arange(F)] = 1.0
    arr["s4dsel"] = dsel
    sh = np.zeros((P, 5, 2), np.int32)
    for e in range(5):
        low = ((F * e + np.arange(P)) % P if e < 4 else np.arange(P)) >= GROUP4
        sh[:, e, 0] = np.where(low, 28, 0)
        sh[:, e, 1] = np.where(low, 28, 4)
    arr["shifts"] = sh
    arr["win_t"] = np.concatenate([A["L1_attn_Win"], A["L1_attn_Win"]], 0).T.reshape(KD, P, P).transpose(1, 0, 2)
    w1 = A["L1_attn_W1"].transpose(2, 0, 1)
    arr["w1_t"] = np.concatenate([w1, w1], 0)
    arr["w2_t"] = A["L1_attn_W2"].transpose(0, 2, 1).reshape(DEPTH, 2, P, C).transpose(2, 0, 1, 3)
    arr["wout_t"] = np.concatenate([A["L1_attn_Wout"].T] * 2, 0)
    block64 = np.kron(np.eye(2), np.full((C, C), 1.0 / C))
    arr["bmat"] = block64.astype(f32)
    arr["cmat"] = (np.eye(P) - block64).astype(f32)
    names = ("ln1_w", "ln1_b", "phz_re", "phz_im", "lc_re", "lc_im", "sc_lin", "ln2_w", "ln2_b", "b2")
    ch = np.stack([A["L1_attn_" + n].T for n in names], 1)
    arr["chan"] = np.concatenate([ch, ch], 0)
    arr["b1"] = A["L1_attn_b1"].reshape(DEPTH, 2, P).transpose(2, 0, 1)
    la = np.stack([A["L1_attn_bin"], A["L1_attn_lnl_w"], A["L1_attn_lnl_b"]], 1)
    arr["last"] = np.concatenate([la, la], 0)
    arr["bout"] = A["L1_attn_bout"]

    nc = bacc.Bacc("TRN2", target_bir_lowering=False, num_devices=1)
    arrays, aps = {}, {}
    for name, w in arr.items():
        w = np.ascontiguousarray(w)
        arrays["in_" + name] = w
        aps[name] = nc.dram_tensor("in_" + name, w.shape, _mybir.dt.from_np(w.dtype), kind="ExternalInput").ap()
    out = nc.dram_tensor("out", (N, D), F32, kind="ExternalOutput").ap()
    sandwich(nc, aps, out)
    r = _run(nc, [arrays], core_ids=[0])
    return r.results[0]["out"].reshape(B, S, D)
```

```python
from contextlib import ExitStack

import concourse.bass as bass
from concourse import mybir

F32 = mybir.dt.float32
F32R = mybir.dt.float32r
BF16 = mybir.dt.bfloat16
I32 = mybir.dt.int32
ALU = mybir.AluOpType
ACT = mybir.ActivationFunctionType
AX_X = mybir.AxisListType.X

P = 128
B, S, D = 2, 512, 512
N = B * S
NT = N // P
TB = S // P
KD = D // P
H, HD = 32, 16
NPAIR = H // 2
F = 1376
HT = [(k * P, min(P, F - k * P)) for k in range((F + P - 1) // P)]
GROUPS = [(0, 6), (6, 11)]
RING = 7
RANK = 16
GROUP4 = 64
C = 64
DEPTH, DFF = 4, 256
EPS = 1e-5


def sandwich(nc, a, out):
    es = ExitStack()
    sems = {}

    def sem(name):
        if name not in sems:
            sems[name] = es.enter_context(nc.semaphore(name))
        return sems[name]

    def sb(ctx, name, shape, dt=F32):
        return ctx.enter_context(nc.sbuf_tensor(name, shape, dt))

    with es:
        psum = es.enter_context(nc.psum_tensor("psum", [P, 8, 512], F32))
        bank = [psum[:, i, :] for i in range(8)]
        PAIRS = [(b, p) for b in range(B) for p in range(NPAIR)]
        x = sb(es, "x", [P, NT, D])
        xt_hi = sb(es, "xt_hi", [P, KD, N], F32R)
        xt_lo = sb(es, "xt_lo", [P, KD, N], F32R)
        y = sb(es, "y", [P, NT, D])
        ident = sb(es, "ident", [P, P])
        ident16 = sb(es, "ident16", [P, P], BF16)
        causal16 = sb(es, "causal16", [P, P], BF16)
        neghalf = sb(es, "neghalf", [P, 4])
        epst = sb(es, "epst", [P, 1])
        bnst = sb(es, "bnst", [P, 6])
        mv = sb(es, "mv", [P, 8, NT, 2])
        ve = sb(es, "ve", [P, 8, NT])
        rstd = sb(es, "rstd", [P, 8, NT])
        xn = sb(es, "xn", [P, 2, D])
        at = ExitStack()
        with at:
            w_hi = sb(at, "w_hi", [P, 3, KD, D], F32R)
            w_lo = sb(at, "w_lo", [P, 3, KD, D], F32R)
            qk = sb(at, "qk", [P, 2, NT, D])
            v = sb(at, "v", [P, NT, H * (HD + 1) + 32 - (HD + 1)])
            rope_c = sb(at, "rope_c", [P, 2, TB, HD])
            rope_s = sb(at, "rope_s", [P, 2, TB, HD])
            negmax = sb(at, "negmax", [P, len(PAIRS), TB, 2])
            einv = sb(at, "einv", [P, len(PAIRS) // 2, TB, 4])
            k_one = sb(at, "k_one", [P, 1])
            with ExitStack() as sub:
                w_raw = sb(sub, "w_raw", [P, KD, D])
                rot_c = sb(sub, "rot_c", [P, 2, D])
                rot_s = sb(sub, "rot_s", [P, 2, D])
            with ExitStack() as sub:
                spread = sb(sub, "spread", [P, 4, 4, P], F32R)
                probs = sb(sub, "probs", [P, 3, 2, S])
                heads_t = sb(sub, "heads_t", [P, 2, S])
                max_row = sb(sub, "max_row", [P, TB, P], F32R)
                ident_r = sb(sub, "ident_r", [P, P], F32R)
                o_hi = sb(sub, "o_hi", [P, 2, KD, P], F32R)
                o_lo = sb(sub, "o_lo", [P, 2, KD, P], F32R)
        with ExitStack() as ff:
            h_hi = sb(ff, "h_hi", [P, RING, N], F32R)
            h_lo = sb(ff, "h_lo", [P, RING, N], F32R)
            wd_hi = sb(ff, "wd_hi", [P, RING, D], F32R)
            wd_lo = sb(ff, "wd_lo", [P, RING, D], F32R)
            wgu_raw = sb(ff, "wgu_raw", [P, 4, KD, P])
            wgu_hi = sb(ff, "wgu_hi", [P, 4, KD, P], F32R)
            wgu_lo = sb(ff, "wgu_lo", [P, 4, KD, P], F32R)
            wd_raw = sb(ff, "wd_raw", [P, 2, D])
            sg = sb(ff, "sg", [P, 2, D])
            hf = sb(ff, "hf", [P, 2, D])
            shifts = sb(ff, "shifts", [P, 5, 2], I32)
            with ExitStack() as sub:
                lora_a = sb(sub, "lora_a", [96, F])
                lora_b = sb(sub, "lora_b", [96, D])
            with ExitStack() as sub:
                s4 = sb(sub, "s4", [40, F])
                s4sel = sb(sub, "s4sel", [40, KD, P])
                s4d = sb(sub, "s4d", [107, D // 2])
                s4dsel = sb(sub, "s4dsel", [107, F])
        with ExitStack() as mx:
            win_raw = sb(mx, "win_raw", [P, KD, P])
            win_hi = sb(mx, "win_hi", [P, KD, P], F32R)
            win_lo = sb(mx, "win_lo", [P, KD, P], F32R)
            w1t = sb(mx, "w1t", [P, DEPTH, DFF])
            w2t = sb(mx, "w2t", [P, DEPTH, 2, C])
            wout = sb(mx, "wout", [P, D])
            bout = sb(mx, "bout", [P, D])
            cmat = sb(mx, "cmat", [P, P])
            bmat = sb(mx, "bmat", [P, P])
            chan = sb(mx, "chan", [P, 10, DEPTH])
            b1 = sb(mx, "b1", [P, DEPTH, 2])
            last = sb(mx, "last", [P, 3])
            ct = sb(mx, "ct", [P, DEPTH, S])
            sn = sb(mx, "sn", [P, DEPTH, S])
            tw = sb(mx, "tw", [P, 2, DEPTH, S // 2])
            pw = sb(mx, "pw", [P, 12, DEPTH])
            step_c = sb(mx, "step_c", [P, 10, DEPTH])
            step_s = sb(mx, "step_s", [P, 10, DEPTH])
            hm = sb(mx, "hm", [P, S])
            wk = sb(mx, "wk", [P, 10, S])
            g1 = sb(mx, "g1", [P, 4, S])
        block = es.enter_context(nc.Block())

        ONE, TWO, TURN, FLIP, SPREAD, PV, PLACE = range(7)
        NPR = len(PAIRS)
        PERIODS = []
        for g in range(-3, NPR + 1):
            todo = [(ONE, g + 1, 3), (TWO, g, 0), (TURN, (g + 3) // 4, 0), (FLIP, g // 2 - 1, 0), (ONE, g + 1, 2), (TWO, g, 1), (ONE, g + 1, 1),
                    (PV, g, 0), (ONE, g + 1, 0), (TWO, g, 2), (PV, g, 1), (PLACE, g + 1, 0), (SPREAD, g + 2, 0), (TWO, g, 3), (PV, g, 2),
                    (PV, g, 3)]
            PERIODS += [(what, p, i) for what, p, i in todo
                        if ((g + 3) % 4 == 0 and g + 3 < NPR if what == TURN else
                            g % 2 == 0 and g >= 2 if what == FLIP else 0 <= p < NPR)]
        RINGED = [e for e in PERIODS if e[0] in (ONE, TWO, TURN, FLIP, SPREAD)]
        nth = {}
        for what in (ONE, TWO, TURN, FLIP, SPREAD):
            for n, e in enumerate([e for e in RINGED if e[0] == what]):
                nth[e] = n
        ring = {e: n % 3 for n, e in enumerate(RINGED)}

        def pair_of_banks(e):
            return psum[:, 2 * ring[e]:2 * ring[e] + 2, :]

        COMBOS = ((0, 0), (0, 1), (1, 0))
        XT_LAG = 4
        XT = (xt_hi, xt_lo)

        def k_stack(g):
            return w_hi[:, 1 + g % 3 // 2, 2 + g % 3 % 2, :]

        def q_stack(g):
            return (w_hi, w_lo)[g % 2][:, 2, 3, :]

        def q_less_max(g):
            return w_lo[:, 1, 2 + g % 2, :]

        def hid(m):
            return HT[m][1]

        @block.sync
        def _(sp):
            for t in range(NT):
                sp.dma_start(x[:, t, :], a["x"][t * P:(t + 1) * P, :]).then_inc(sem(f"x_in{t}"), 16)
                if t == 0:
                    sp.dma_start(ident[:, :], a["ident"]).then_inc(sem("consts_in"), 16)
                    sp.dma_start(neghalf[:, :], a["neghalf"]).then_inc(sem("consts_in"), 16)
                    sp.dma_start(rope_c[:, :, :, :], a["rope_c"]).then_inc(sem("consts_in"), 16)
                    sp.dma_start(rope_s[:, :, :, :], a["rope_s"]).then_inc(sem("consts_in"), 16)
                    sp.dma_start(ident16[:, :], a["ident16"]).then_inc(sem("consts_in"), 16)
                    sp.dma_start(causal16[:, :], a["causal16"]).then_inc(sem("consts_in"), 16)
                    sp.dma_start(k_one[:, :], a["k_one"]).then_inc(sem("consts_in"), 16)
            for j, name in enumerate(("wq", "wk", "wv", "wo")):
                if j:
                    sp.wait_ge(sem("w_split"), j)
                sp.dma_start(w_raw[:, :, :], a[name].rearrange("(k p) n -> p k n", p=P)).then_inc(sem("w_in"), 16)
            sp.wait_ge(sem("w_split"), 4)
            sp.dma_start(w_raw[:, :, :], a["spread"]).then_inc(sem("w_in"), 16)

            def ffn_loads(s):
                sp.wait_ge(sem(f"xt_ready{s}"), NT)
                if s == 1:
                    for r, (na, nb) in enumerate((("gate_bt", "gate_a"), ("up_bt", "up_a"), ("down_a", "down_bt"))):
                        sp.dma_start(lora_a[32 * r:32 * r + RANK, :], a[na]).then_inc(sem("side_in1"), 16)
                        sp.dma_start(lora_b[32 * r:32 * r + RANK, :], a[nb]).then_inc(sem("side_in1"), 16)
                    wgu, wd, raw_gu, raw_d = a["gu_t"], a["down_t"], wgu_raw[:, :, :, :], wd_raw[:, :, :]
                else:
                    for c in range(2):
                        sp.dma_start(s4[32 * c:32 * c + 8, :], a["s13"][c]).then_inc(sem("side_in3"), 16)
                        sp.dma_start(s4sel[32 * c:32 * c + 8, :, :], a["s4sel"]).then_inc(sem("side_in3"), 16)
                        sp.dma_start(s4d[64 * c:64 * c + 43, :], a["s2"]).then_inc(sem("side_in3"), 16)
                        sp.dma_start(s4dsel[64 * c:64 * c + 43, :], a["s4dsel"][c]).then_inc(sem("side_in3"), 16)
                    sp.dma_start(shifts[:, :, :], a["shifts"]).then_inc(sem("side_in3"), 16)
                    wgu, wd = a["w13"], a["w2"]
                    raw_gu, raw_d = wgu_raw[:, :, :, :].bitcast(I32), wd_raw[:, :, :].bitcast(I32)
                for m, (h0, n) in enumerate(HT):
                    if m >= 2:
                        sp.wait_ge(sem(f"wlo{s}"), 3 * (m - 1))
                    for g in range(2):
                        sp.dma_start(raw_gu[:, 2 * (m % 2) + g, :, 0:n],
                                     wgu[g].rearrange("(k p) h -> p k h", p=P)[:, :, h0:h0 + n]).then_inc(sem(f"wraw{s}_{m % 2}"), 16)
                    sp.dma_start(raw_d[0:n, m % 2, :], wd[h0:h0 + n, :]).then_inc(sem(f"wraw{s}_{m % 2}"), 16)

            ffn_loads(1)
            sp.wait_ge(sem("y_ready1"), NT)
            for dst, name in ((win_raw[:, :, :], "win_t"), (w1t[:, :, :], "w1_t"), (w2t[:, :, :, :], "w2_t"), (wout[:, :], "wout_t"),
                              (cmat[:, :], "cmat"), (bmat[:, :], "bmat"), (chan[:, :, :], "chan"), (b1[:, :, :], "b1"),
                              (last[:, :], "last")):
                sp.dma_start(dst, a[name]).then_inc(sem("mixer_in"), 16)
            sp.dma_start(bout[:, :], a["bout"].partition_broadcast(P)).then_inc(sem("mixer_in"), 16)
            ffn_loads(3)
            for t in range(NT):
                sp.wait_ge(sem("x_sum3"), t + 1)
                sp.dma_start(out[t * P:(t + 1) * P, :], x[:, t, :]).then_inc(sem("stored"), 16)
            sp.wait_ge(sem("stored"), 16 * NT)

        @block.gpsimd
        def _(pool):
            pool_steps = [0]

            def link(ins):
                pool_steps[0] += 1
                ins.then_inc(sem("pool_step"), 1)
                pool.wait_ge(sem("pool_step"), pool_steps[0])

            def inv_std(n, t, stats, done):
                pool.wait_ge(sem(stats), t + 1)
                link(nc.gpsimd.tensor_scalar(ve[:, n, t:t + 1], mv[:, n, t, 1:2], EPS, None, ALU.add))
                nc.gpsimd.tensor_tensor(rstd[:, n, t:t + 1], ve[:, n, t:t + 1], neghalf[:, 0:1], ALU.pow).then_inc(sem(done), 1)

            def norm_out(s):
                for t in range(NT + 2):
                    if t < NT:
                        inv_std(2 * s + 1, t, f"y_stats{s}", f"y_rstd{s}")
                    if 1 <= t <= NT:
                        u = t - 1
                        pool.wait_ge(sem(f"y_norm{s}"), u + 1)
                        nc.gpsimd.tensor_tensor(x[:, u, :], x[:, u, :], y[:, u, :], ALU.add).then_inc(sem(f"x_sum{s}"), 1)
                    if t >= 2 and s < 3:
                        inv_std(2 * s + 2, t - 2, f"x_stats{s + 1}", f"x_rstd{s + 1}")

            nc.gpsimd.memset(epst[:, :], EPS).then_inc(sem("eps_set"), 1)
            nc.gpsimd.memset(v[:, :, :], 1.0).then_inc(sem("v_ones"), 1)
            pool.wait_ge(sem("consts_in"), 7 * 16)
            for t in range(NT):
                inv_std(0, t, "x_stats0", "x_rstd0")
            for t in range(NT):
                for j in range(2):
                    u = 2 * t + j
                    pool.wait_ge(sem("rotated"), u + 1)
                    nc.gpsimd.tensor_tensor(qk[:, j, t, :], rot_c[:, j, :], rot_s[:, j, :], ALU.add).then_inc(sem("qk_ready"), 1)
            norm_out(0)

            def ffn(s):
                for v_ in range(len(HT) + 1):
                    if v_ < len(HT):
                        m, n = v_, hid(v_)
                        for g in range(2):
                            pool.wait_ge(sem(f"whi{s}"), 3 * m + g + 1)
                            if m >= 2:
                                pool.wait_ge(sem(f"gu{s}"), 2 * (m - 1))
                            r = 2 * (m % 2) + g
                            nc.gpsimd.tensor_tensor(wgu_lo[:, r, :, 0:n], wgu_raw[:, r, :, 0:n],
                                                    wgu_hi[:, r, :, 0:n].bitcast(F32), ALU.subtract).then_inc(sem(f"wlo{s}"), 1)
                        pool.wait_ge(sem(f"whi{s}"), 3 * m + 3)
                        if m >= RING:
                            pool.wait_ge(sem(f"down{s}"), NT)
                        nc.gpsimd.tensor_tensor(wd_lo[0:n, m % RING, :], wd_raw[0:n, m % 2, :],
                                                wd_hi[0:n, m % RING, :].bitcast(F32), ALU.subtract).then_inc(sem(f"wlo{s}"), 1)
                    if v_ >= 1:
                        m, n = v_ - 1, hid(v_ - 1)
                        for hf_ in range(2):
                            u = 2 * m + hf_
                            pool.wait_ge(sem(f"h_hi{s}"), u + 1)
                            if m >= RING:
                                pool.wait_ge(sem(f"down{s}"), NT)
                            nc.gpsimd.tensor_tensor(h_lo[0:n, m % RING, hf_ * 512:hf_ * 512 + 512], hf[0:n, u % 2, :],
                                                    h_hi[0:n, m % RING, hf_ * 512:hf_ * 512 + 512].bitcast(F32),
                                                    ALU.subtract).then_inc(sem(f"h_lo{s}"), 1)

            ffn(1)
            norm_out(1)
            pool.wait_ge(sem("p_sq"), 1)
            nc.gpsimd.tensor_tensor(pw[:, 1, :], pw[:, 0, :], neghalf[:, 0:4], ALU.pow).then_inc(sem("p_inv"), 1)
            for l in range(DEPTH):
                pool.wait_ge(sem("mix_silu"), l + 1)
                nc.gpsimd.tensor_tensor(wk[:, 4, :], wk[:, 2, :], sn[:, l, :], ALU.mult).then_inc(sem("sin_mod"), 1)
                pool.wait_ge(sem("sin_scan"), l + 1)
                nc.gpsimd.tensor_tensor(wk[:, 8, :], wk[:, 6, :], sn[:, l, :], ALU.mult).then_inc(sem("sin_demod"), 1)
            norm_out(2)
            ffn(3)
            norm_out(3)

        @block.scalar
        def _(act):
            def xt_tile(s, t):
                if 0 <= t < NT:
                    act.wait_ge(sem(f"xt_psum{s}"), t + 1)
                    nc.scalar.activation(xt_hi[:, :, t * P:(t + 1) * P], bank[6 + t % 2][:, :].rearrange("p (k n) -> p k n", k=KD),
                                         ACT.Copy).then_inc(sem(f"xt_hi{s}"), 1)

            for t in range(NT):
                xt_tile(0, t)
            for j in range(3):
                act.wait_ge(sem("w_in"), 16 * (j + 1))
                nc.scalar.activation(w_hi[:, j, :, :], w_raw[:, :, :], ACT.Copy).then_inc(sem("w_split_hi"), 1)
            act.wait_ge(sem("v_ones"), 1)
            for t in range(NT):
                act.wait_ge(sem("proj"), 3 * t + 3)
                nc.scalar.activation(v[:, t, 0:H * (HD + 1)].rearrange("p (h d) -> p h d", h=H)[:, :, 0:HD], bank[(3 * t + 2) % 6][:, :].rearrange("p (h d) -> p h d", h=H),
                                     ACT.Copy).then_inc(sem("v_ready"), 1)
            act.wait_ge(sem("w_in"), 64)
            act.wait_ge(sem("proj"), 3 * NT)
            nc.scalar.activation(w_hi[:, 0, :, :], w_raw[:, :, :], ACT.Copy).then_inc(sem("w_split_hi"), 1)
            act.wait_ge(sem("w_in"), 80)
            act.wait_ge(sem("qk_ready"), 2 * NT)
            nc.scalar.activation(spread[:, :, :, :], w_raw[:, :, :].rearrange("p a (b c) -> p a b c", b=4), ACT.Copy).then_inc(sem("spread_ready"), 1)
            act.wait_ge(sem("spread_ready"), 1)

            nc.scalar.activation(ident_r[:, :], ident[:, :], ACT.Copy).then_inc(sem("ident_r"), 1)

            for e in PERIODS:
                what, g, i = e
                if what == TURN:
                    act.wait_ge(sem("block_psum"), g + 1)
                    nc.scalar.activation(w_hi[:, 1 + g % 2, 0:2, :], pair_of_banks(e), ACT.Copy).then_inc(sem("block_hi"), 1)
                elif what == TWO:
                    act.wait_ge(sem("scores_t"), nth[e] + 1)
                    if nth[e] >= 3:
                        act.wait_ge(sem("pv"), nth[e] - 2)
                    nc.scalar.activation(probs[:, nth[e] % 3, :, 0:(TB - i) * P], pair_of_banks(e)[:, :, 0:(TB - i) * P],
                                         ACT.Exp).then_inc(sem("exp"), 1)
                elif what == PV and i == TB - 1 and g % 2:
                    act.wait_ge(sem("pv"), TB * (g + 1))
                    if g >= 4:
                        act.wait_ge(sem("flipped"), g // 2 - 1)
                    nc.scalar.activation(heads_t[:, g // 2 % 2, :], bank[7][:, :], ACT.Copy).then_inc(sem("heads_t"), 1)
                elif what == SPREAD:
                    act.wait_ge(sem("stack_psum"), g + 1)
                    nc.scalar.activation(k_stack(g), pair_of_banks(e)[:, 1, :], ACT.Identity, bias=k_one[:, 0:1]).then_inc(sem("k_stack"), 1)
            for t in range(NT + XT_LAG + 1):
                if t < NT:
                    act.wait_ge(sem("o_psum"), t + 1)
                    if t >= 2:
                        act.wait_ge(sem("wo_done"), t - 1)
                    nc.scalar.activation(o_hi[:, t % 2, :, :], bank[4 + t % 2][:, :].rearrange("p (k n) -> p k n", k=KD),
                                         ACT.Copy).then_inc(sem("o_hi"), 1)
                if 1 <= t <= NT:
                    act.wait_ge(sem("wo_done"), t)
                    nc.scalar.activation(y[:, t - 1, :], bank[(t - 1) % 2][:, :], ACT.Copy).then_inc(sem("y_ready0"), 1)
                xt_tile(1, t - 1 - XT_LAG)

            def ffn(s):
                def w_high(m):
                    n = hid(m)
                    for g in range(2):
                        r = 2 * (m % 2) + g
                        act.wait_ge(sem(f"wfull{s}"), 3 * m + g + 1)
                        if m >= 2:
                            act.wait_ge(sem(f"gu{s}"), 2 * (m - 1))
                        nc.scalar.activation(wgu_hi[:, r, :, 0:n], wgu_raw[:, r, :, 0:n], ACT.Copy).then_inc(sem(f"whi{s}"), 1)

                def wd_high(m):
                    n = hid(m)
                    act.wait_ge(sem(f"wfull{s}"), 3 * m + 3)
                    if m >= RING:
                        act.wait_ge(sem(f"down{s}"), NT)
                    nc.scalar.activation(wd_hi[0:n, m % RING, :], wd_raw[0:n, m % 2, :], ACT.Copy).then_inc(sem(f"whi{s}"), 1)

                def hidden(m):
                    n = hid(m)
                    for hf_ in range(2):
                        u = 2 * m + hf_
                        act.wait_ge(sem(f"gu{s}"), u + 1)
                        if u >= 2:
                            act.wait_ge(sem(f"h_full{s}"), u - 1)
                        nc.scalar.activation(sg[0:n, u % 2, :], bank[2 * (u % 2)][0:n, :], ACT.Silu).then_inc(sem(f"silu{s}"), 1)
                        act.wait_ge(sem(f"h_full{s}"), u + 1)
                        if m >= RING:
                            act.wait_ge(sem(f"down{s}"), NT)
                        nc.scalar.activation(h_hi[0:n, m % RING, hf_ * 512:hf_ * 512 + 512], hf[0:n, u % 2, :],
                                             ACT.Copy).then_inc(sem(f"h_hi{s}"), 1)

                def partial():
                    for t in range(NT):
                        act.wait_ge(sem(f"down{s}"), t + 1)
                        nc.scalar.activation(y[:, t, :], bank[4 + t % 2][:, :], ACT.Copy).then_inc(sem(f"y_part{s}"), 1)

                w_high(0)
                wd_high(0)
                for m in range(len(HT)):
                    if m + 1 < len(HT):
                        w_high(m + 1)
                        if m != GROUPS[0][1]:
                            wd_high(m + 1)
                    hidden(m)
                    if m == GROUPS[0][1]:
                        partial()
                        wd_high(m + 1)

            ffn(1)
            for t in range(NT):
                xt_tile(2, t)
            act.wait_ge(sem("mixer_in"), 160)
            nc.scalar.activation(win_hi[:, :, :], win_raw[:, :, :], ACT.Copy).then_inc(sem("win_hi"), 1)
            act.wait_ge(sem("p_abs"), 1)
            nc.scalar.activation(pw[:, 3, :], pw[:, 2, :], ACT.Tanh).then_inc(sem("decay"), 1)
            act.wait_ge(sem("eps_set"), 1)

            def mix_norm(n):
                act.wait_ge(sem("centred"), n + 1)
                nc.scalar.activation(wk[:, 0, :], bank[0][:, :], ACT.Square).then_inc(sem("mix_sq"), 1)
                act.wait_ge(sem("mix_var"), n + 1)
                nc.scalar.activation(wk[:, 1, :], bank[1][:, :], ACT.Ln, bias=epst[:, 0:1]).then_inc(sem("mix_ln"), 1)
                act.wait_ge(sem("mix_ln"), n + 1)
                nc.scalar.activation(wk[:, 9, :], wk[:, 1, :], ACT.Exp, scale=-0.5).then_inc(sem("mix_rstd"), 1)

            for l in range(DEPTH):
                mix_norm(2 * l)
                act.wait_ge(sem("mix_norm"), 2 * l + 1)
                nc.scalar.activation(wk[:, 2, :], wk[:, 7, :], ACT.Silu, bias=chan[:, 1, l:l + 1],
                                     scale=chan[:, 0, l:l + 1]).then_inc(sem("mix_silu"), 1)
                mix_norm(2 * l + 1)
                for f in range(2):
                    for b in range(B):
                        act.wait_ge(sem("mix_up"), 4 * l + 2 * f + b + 1)
                        nc.scalar.activation(g1[:, 2 * f + b, :], bank[2 + 2 * f + b][:, :], ACT.Silu,
                                             bias=b1[:, l, f:f + 1]).then_inc(sem("mix_act"), 1)
            mix_norm(2 * DEPTH)
            for t in range(NT):
                xt_tile(3, t)
            ffn(3)

        @block.vector
        def _(dve):
            dve_steps = [0]

            def link(ins):
                dve_steps[0] += 1
                ins.then_inc(sem("dve_step"), 1)
                dve.wait_ge(sem("dve_step"), dve_steps[0])

            def stats(n, t, src, done):
                link(nc.vector.bn_stats(bnst[:, :], src))
                nc.vector.bn_aggr(mv[:, n, t, :], bnst[:, :]).then_inc(sem(done), 1)
                dve.wait_ge(sem(done), t + 1)

            def norm_x(s, t):
                dve.wait_ge(sem(f"x_rstd{s}"), t + 1)
                if t >= 2:
                    dve.wait_ge(sem(f"xt_psum{s}"), t - 1)
                nc.vector.tensor_scalar(xn[:, t % 2, :], x[:, t, :], mv[:, 2 * s, t, 0:1], rstd[:, 2 * s, t:t + 1],
                                        ALU.subtract, ALU.mult).then_inc(sem(f"xn{s}"), 1)

            def low_xt(s, t):
                dve.wait_ge(sem(f"xt_hi{s}"), t + 1)
                nc.vector.tensor_tensor(xt_lo[:, :, t * P:(t + 1) * P], bank[6 + t % 2][:, :].rearrange("p (k n) -> p k n", k=KD),
                                        xt_hi[:, :, t * P:(t + 1) * P].bitcast(F32), ALU.subtract).then_inc(sem(f"xt_ready{s}"), 1)

            def norm_out(s, make_y=None):
                for t in range(NT + XT_LAG):
                    if t < NT:
                        if make_y:
                            make_y(t)
                        dve.wait_ge(sem(f"y_ready{s}"), t + 1)
                        stats(2 * s + 1, t, y[:, t, :], f"y_stats{s}")
                    if 1 <= t <= NT:
                        dve.wait_ge(sem(f"y_rstd{s}"), t)
                        nc.vector.tensor_scalar(y[:, t - 1, :], y[:, t - 1, :], mv[:, 2 * s + 1, t - 1, 0:1],
                                                rstd[:, 2 * s + 1, t - 1:t], ALU.subtract, ALU.mult).then_inc(sem(f"y_norm{s}"), 1)
                    if s < 3:
                        if 2 <= t <= NT + 1:
                            dve.wait_ge(sem(f"x_sum{s}"), t - 1)
                            stats(2 * s + 2, t - 2, x[:, t - 2, :], f"x_stats{s + 1}")
                        if 3 <= t <= NT + 2:
                            norm_x(s + 1, t - 3)
                        if t >= 4:
                            low_xt(s + 1, t - 4)

            for t in range(NT + 2):
                if t < NT:
                    dve.wait_ge(sem(f"x_in{t}"), 16)
                    stats(0, t, x[:, t, :], "x_stats0")
                if 1 <= t <= NT:
                    norm_x(0, t - 1)
                if t >= 2:
                    low_xt(0, t - 2)

            def w_low(j, dst):
                dve.wait_ge(sem("w_split_hi"), j + 1)
                nc.vector.tensor_tensor(w_lo[:, dst, :, :], w_raw[:, :, :], w_hi[:, dst, :, :].bitcast(F32),
                                        ALU.subtract).then_inc(sem("w_split"), 1)

            dve.wait_ge(sem("consts_in"), 7 * 16)
            for j in range(3):
                w_low(j, j)
            for t in range(NT):
                for j in range(2):
                    u = 2 * t + j
                    dve.wait_ge(sem("proj"), 3 * t + j + 1)
                    if t:
                        dve.wait_ge(sem("qk_ready"), u - 1)
                    src = bank[(3 * t + j) % 6][:, :].rearrange("p (h d) -> p h d", h=H)
                    cs = rope_c[:, j, t % TB, :].unsqueeze(1).to_broadcast([P, H, HD])
                    nc.vector.tensor_tensor(rot_c[:, j, :].rearrange("p (h d) -> p h d", h=H), src, cs, ALU.mult)
                    src = bank[(3 * t + j) % 6][:, :].rearrange("p (h f two) -> p h f two", h=H, two=2)
                    dst = rot_s[:, j, :].rearrange("p (h f two) -> p h f two", h=H, two=2)
                    ss = rope_s[:, j, t % TB, :].rearrange("p (f two) -> p f two", two=2)
                    for e in range(2):
                        ins = nc.vector.tensor_tensor(dst[:, :, :, e], src[:, :, :, 1 - e],
                                                      ss[:, :, e].unsqueeze(1).to_broadcast([P, H, HD // 2]), ALU.mult)
                    ins.then_inc(sem("rotated"), 1)
            w_low(3, 0)
            dve.wait_ge(sem("w_split"), 4)
            dve.wait_ge(sem("spread_ready"), 1)

            nc.vector.memset(max_row[:, :, :].bitcast(F32), 0.0).then_inc(sem("max_row_zero"), 1)
            dve.wait_ge(sem("max_row_zero"), 1)

            for e in PERIODS:
                what, g, i = e
                if what == TURN:
                    dve.wait_ge(sem("block_hi"), g + 1)
                    nc.vector.tensor_tensor(w_lo[:, 1 + g % 2, 0:2, :], pair_of_banks(e), w_hi[:, 1 + g % 2, 0:2, :].bitcast(F32),
                                            ALU.subtract).then_inc(sem("block_split"), 1)
                elif what == ONE:
                    dve.wait_ge(sem("scores"), nth[e] + 1)
                    nc.vector.tensor_reduce(negmax[:, g, i, :], pair_of_banks(e)[:, :, 0:(i + 1) * P], AX_X, ALU.max,
                                            negate=True).then_inc(sem("row_max"), 1)
                    if i == 0:
                        dve.wait_ge(sem("row_max"), TB * (g + 1))
                        rows = max_row[:, :, :].rearrange("p i (h r) -> p i h r", h=2)
                        link(nc.vector.tensor_copy(rows[:, :, :, 3 * HD], negmax[:, g, :, :]))
                        nc.vector.tensor_tensor(rows[:, :, :, 3 * HD + 1], negmax[:, g, :, :], rows[:, :, :, 3 * HD].bitcast(F32),
                                                ALU.subtract).then_inc(sem("max_row"), 1)
                elif what == FLIP:
                    b, n = divmod(g, NPAIR // 2)
                    dve.wait_ge(sem("flipped"), g + 1)
                    src = pair_of_banks(e)[:, 0, :].rearrange("p (i h r) -> p i h r", i=TB, h=4)
                    link(nc.vector.reciprocal(einv[:, g, :, :], src[:, :, :, HD]))
                    nc.vector.tensor_tensor(y[:, TB * b:TB * b + TB, 4 * HD * n:4 * HD * (n + 1)].rearrange("p i (h d) -> p i h d", h=4),
                                            src[:, :, :, 0:HD], einv[:, g, :, :].unsqueeze(3).to_broadcast([P, TB, 4, HD]),
                                            ALU.mult).then_inc(sem("o_ready"), 1)
                elif what == SPREAD:
                    dve.wait_ge(sem("stack_psum"), g + 1)
                    nc.vector.tensor_copy(q_stack(g), pair_of_banks(e)[:, 0, :]).then_inc(sem("q_stack"), 1)
                elif what == PLACE:
                    dve.wait_ge(sem("placed"), g + 1)
                    nc.vector.tensor_tensor(q_less_max(g), bank[6][:, :], q_stack(g).bitcast(F32), ALU.add).then_inc(sem("q_less_max"), 1)

            def turned_low(t):
                dve.wait_ge(sem("o_hi"), t + 1)
                nc.vector.tensor_tensor(o_lo[:, t % 2, :, :], bank[4 + t % 2][:, :].rearrange("p (k n) -> p k n", k=KD),
                                        o_hi[:, t % 2, :, :].bitcast(F32), ALU.subtract).then_inc(sem("o_split"), 1)

            norm_out(0, turned_low)

            def ffn(s):
                prep = "prep%d" % s

                def full(m, c):
                    n, q = hid(m), 3 * m + c
                    dve.wait_ge(sem(f"wraw{s}_{m % 2}"), 48 * (m // 2 + 1))
                    if c < 2:
                        r = 2 * (m % 2) + c
                        w, ps = wgu_raw[:, r, :, 0:n], bank[6 + q % 2][:, :].rearrange("p (k n) -> p k n", k=KD)[:, :, 0:n]
                    else:
                        w, ps = wd_raw[0:n, m % 2, :], bank[6 + q % 2][0:n, :]
                    if s == 1:
                        dve.wait_ge(sem(prep), q + 1)
                        nc.vector.tensor_tensor(w, w, ps, ALU.add).then_inc(sem(f"wfull{s}"), 1)
                        return
                    wi = w.bitcast(I32)
                    if c < 2:
                        link(nc.vector.tensor_scalar(wi, wi, shifts[:, 4, 0:1], shifts[:, 4, 1:2],
                                                     ALU.logical_shift_left, ALU.arith_shift_right))
                    else:
                        for e in range(4):
                            part = wi.rearrange("p (d e) -> p d e", e=4)[:, :, e]
                            ins = nc.vector.tensor_scalar(part, part, shifts[0:n, e, 0:1], shifts[0:n, e, 1:2],
                                                          ALU.logical_shift_left, ALU.arith_shift_right)
                        link(ins)
                    dve.wait_ge(sem(prep), q + 1)
                    if c < 2:
                        nc.vector.tensor_tensor(w, wi, ps, ALU.mult).then_inc(sem(f"wfull{s}"), 1)
                    else:
                        nc.vector.tensor_tensor(w.rearrange("p (e two) -> p two e", two=2), wi.rearrange("p (e two) -> p two e", two=2),
                                                ps.rearrange("p (two e) -> p two e", two=2), ALU.mult).then_inc(sem(f"wfull{s}"), 1)

                def hidden(m):
                    n = hid(m)
                    for hf_ in range(2):
                        u = 2 * m + hf_
                        dve.wait_ge(sem(f"silu{s}"), u + 1)
                        if u >= 2:
                            dve.wait_ge(sem(f"h_lo{s}"), u - 1)
                        nc.vector.tensor_tensor(hf[0:n, u % 2, :], sg[0:n, u % 2, :], bank[2 * (u % 2) + 1][0:n, :],
                                                ALU.mult).then_inc(sem(f"h_full{s}"), 1)

                if s == 3:
                    dve.wait_ge(sem("side_in3"), 144)
                for c in range(3):
                    full(0, c)
                for m in range(len(HT)):
                    if m + 1 < len(HT):
                        for c in range(3):
                            full(m + 1, c)
                    hidden(m)

                def make_y(t):
                    dve.wait_ge(sem(f"down{s}"), NT + t + 1)
                    dve.wait_ge(sem(f"y_part{s}"), t + 1)
                    nc.vector.tensor_tensor(y[:, t, :], y[:, t, :], bank[4 + t % 2][:, :], ALU.add).then_inc(sem(f"y_ready{s}"), 1)

                norm_out(s, make_y)

            ffn(1)

            dve.wait_ge(sem("mixer_in"), 160)
            dve.wait_ge(sem("win_hi"), 1)
            nc.vector.tensor_tensor(win_lo[:, :, :], win_raw[:, :, :], win_hi[:, :, :].bitcast(F32), ALU.subtract).then_inc(sem("win_split"), 1)
            PR, PI, LR, LI = 2, 3, 4, 5
            link(nc.vector.tensor_tensor(pw[:, 4, :], chan[:, PR, :], chan[:, PR, :], ALU.mult))
            link(nc.vector.tensor_tensor(pw[:, 5, :], chan[:, PI, :], chan[:, PI, :], ALU.mult))
            link(nc.vector.tensor_tensor(pw[:, 10, :], pw[:, 4, :], pw[:, 5, :], ALU.add))
            link(nc.vector.tensor_scalar(pw[:, 11, :], pw[:, 10, :], 0.0, None, ALU.is_equal))
            nc.vector.tensor_tensor(pw[:, 0, :], pw[:, 10, :], pw[:, 11, :], ALU.add).then_inc(sem("p_sq"), 1)
            dve.wait_ge(sem("p_inv"), 1)
            nc.vector.tensor_tensor(pw[:, 2, :], pw[:, 10, :], pw[:, 1, :], ALU.mult).then_inc(sem("p_abs"), 1)
            link(nc.vector.tensor_tensor(step_c[:, 0, :], chan[:, PR, :], pw[:, 1, :], ALU.mult))
            link(nc.vector.tensor_tensor(step_c[:, 0, :], step_c[:, 0, :], pw[:, 11, :], ALU.add))
            link(nc.vector.tensor_tensor(step_s[:, 0, :], chan[:, PI, :], pw[:, 1, :], ALU.mult))

            def complex_mul(dc, ds, ac, as_, bc, bs, t1, t2):
                link(nc.vector.tensor_tensor(t1, ac, bc, ALU.mult))
                link(nc.vector.tensor_tensor(t2, as_, bs, ALU.mult))
                link(nc.vector.tensor_tensor(dc, t1, t2, ALU.subtract))
                link(nc.vector.tensor_tensor(t1, ac, bs, ALU.mult))
                link(nc.vector.tensor_tensor(t2, as_, bc, ALU.mult))
                link(nc.vector.tensor_tensor(ds, t1, t2, ALU.add))

            link(nc.vector.memset(ct[:, :, 0:1], 1.0))
            link(nc.vector.memset(sn[:, :, 0:1], 0.0))
            n, k = 1, 0
            while n < S:
                sc = step_c[:, k, :].unsqueeze(2).to_broadcast([P, DEPTH, n])
                ss = step_s[:, k, :].unsqueeze(2).to_broadcast([P, DEPTH, n])
                complex_mul(ct[:, :, n:2 * n], sn[:, :, n:2 * n], ct[:, :, 0:n], sn[:, :, 0:n], sc, ss,
                            tw[:, 0, :, 0:n], tw[:, 1, :, 0:n])
                complex_mul(step_c[:, k + 1, :], step_s[:, k + 1, :], step_c[:, k, :], step_s[:, k, :],
                            step_c[:, k, :], step_s[:, k, :], pw[:, 4, :], pw[:, 5, :])
                n, k = 2 * n, k + 1
            complex_mul(pw[:, 6, :], pw[:, 7, :], chan[:, LR, :], chan[:, LI, :], step_c[:, 0, :], step_s[:, 0, :],
                        pw[:, 4, :], pw[:, 5, :])
            link(nc.vector.tensor_scalar(pw[:, 8, :], pw[:, 7, :], -1.0, None, ALU.mult))
            for b in range(B):
                rows = slice(C * b, C * b + C)
                dve.wait_ge(sem("mix_in"), b + 1)
                link(nc.vector.tensor_scalar(hm[rows, :], bank[b][rows, :], last[rows, 0:1], None, ALU.add))
            dve.wait_ge(sem("decay"), 1)
            nc.vector.tensor_copy(wk[:, 9, 0:1], hm[:, 0:1]).then_inc(sem("h_ready"), 1)

            def mix_norm(n):
                dve.wait_ge(sem("mix_rstd"), n + 1)
                nc.vector.tensor_tensor(wk[:, 7, :], bank[0][:, :], wk[:, 9, :], ALU.mult).then_inc(sem("mix_norm"), 1)

            for l in range(DEPTH):
                mix_norm(2 * l)
                dve.wait_ge(sem("mix_silu"), l + 1)
                link(nc.vector.tensor_tensor(wk[:, 3, :], wk[:, 2, :], ct[:, l, :], ALU.mult))
                decay = pw[:, 3, l:l + 1].to_broadcast([P, S])
                link(nc.vector.tensor_tensor_scan(wk[:, 5, :], decay, wk[:, 3, :], pw[:, 6, l:l + 1], ALU.mult, ALU.add))
                dve.wait_ge(sem("sin_mod"), l + 1)
                nc.vector.tensor_tensor_scan(wk[:, 6, :], decay, wk[:, 4, :], pw[:, 8, l:l + 1], ALU.mult, ALU.add).then_inc(sem("sin_scan"), 1)
                link(nc.vector.tensor_tensor(wk[:, 7, :], wk[:, 5, :], ct[:, l, :], ALU.mult))
                dve.wait_ge(sem("sin_demod"), l + 1)
                link(nc.vector.tensor_tensor(wk[:, 7, :], wk[:, 7, :], wk[:, 8, :], ALU.add))
                nc.vector.scalar_tensor_tensor(out=hm[:, :], in0=wk[:, 7, :], scalar=chan[:, 6, l:l + 1], in1=hm[:, :],
                                               op0=ALU.mult, op1=ALU.add).then_inc(sem("h_ready"), 1)
                dve.wait_ge(sem("h_ready"), 2 * l + 2)
                mix_norm(2 * l + 1)
                dve.wait_ge(sem("mix_norm"), 2 * l + 2)
                nc.vector.tensor_scalar(wk[:, 8, :], wk[:, 7, :], chan[:, 7, l:l + 1], chan[:, 8, l:l + 1],
                                        ALU.mult, ALU.add).then_inc(sem("mix_affine"), 1)
                dve.wait_ge(sem("mix_down"), l + 1)
                nc.vector.scalar_tensor_tensor(out=hm[:, :], in0=bank[6][:, :], scalar=chan[:, 9, l:l + 1], in1=hm[:, :],
                                               op0=ALU.add, op1=ALU.add).then_inc(sem("h_ready"), 1)
                dve.wait_ge(sem("h_ready"), 2 * l + 3)
            mix_norm(2 * DEPTH)
            dve.wait_ge(sem("mix_norm"), 2 * DEPTH + 1)
            nc.vector.tensor_scalar(wk[:, 8, :], wk[:, 7, :], last[:, 1:2], last[:, 2:3], ALU.mult, ALU.add).then_inc(sem("mix_affine"), 1)

            def mixer_y(t):
                dve.wait_ge(sem("mix_out"), t + 1)
                nc.vector.tensor_tensor(y[:, t, :], bank[2 + t % 2][:, :], bout[:, :], ALU.add).then_inc(sem("y_ready2"), 1)

            norm_out(2, mixer_y)
            ffn(3)

        @block.tensor
        def _(pe):
            def xt_tile(s, t):
                if 0 <= t < NT:
                    pe.wait_ge(sem(f"xn{s}"), t + 1)
                    if t >= 2:
                        pe.wait_ge(sem(f"xt_ready{s}"), t - 1)
                    for k in range(KD):
                        ins = nc.tensor.transpose(bank[6 + t % 2][:, k * P:(k + 1) * P], xn[:, t % 2, k * P:(k + 1) * P], ident[:, :])
                    ins.then_inc(sem(f"xt_psum{s}"), 1)

            def split_product(dst, lhs, rhs, ks, start=True, stop=True):
                todo = [(k, i, j) for k in ks for i, j in COMBOS]
                for n, (k, i, j) in enumerate(todo):
                    ins = nc.tensor.matmul(dst, lhs(i, k), rhs(j, k), start=start and n == 0, stop=stop and n == len(todo) - 1)
                return ins

            pe.wait_ge(sem("consts_in"), 7 * 16)
            for t in range(NT):
                xt_tile(0, t)
            pe.wait_ge(sem("xt_ready0"), NT)
            W = (w_hi, w_lo)
            for t in range(NT):
                for j in range(3):
                    u = 3 * t + j
                    if t == 0:
                        pe.wait_ge(sem("w_split"), j + 1)
                    if t >= 2:
                        pe.wait_ge(sem("v_ready" if j == 2 else "rotated"), t - 1 if j == 2 else 2 * (t - 2) + j + 1)
                    split_product(bank[u % 6][:, :], lambda i, k: XT[i][:, k, t * P:(t + 1) * P],
                                  lambda i, k: W[i][:, j, k, :], range(KD)).then_inc(sem("proj"), 1)

            pe.wait_ge(sem("qk_ready"), 2 * NT)
            pe.wait_ge(sem("v_ready"), NT)

            pe.wait_ge(sem("spread_ready"), 1)
            pe.wait_ge(sem("v_ones"), 1)
            pe.wait_ge(sem("ident_r"), 1)

            def ring_free(e):
                n = RINGED.index(e)
                if n >= 3:
                    before = RINGED[n - 3]
                    for reader in {ONE: ("row_max",), TWO: ("exp",), TURN: ("block_split",), FLIP: ("o_ready",),
                                   SPREAD: ("k_stack", "q_stack")}[before[0]]:
                        pe.wait_ge(sem(reader), nth[before] + 1)

            def masked(dst, lhs, rhs, diagonal, mask, unit):
                for h in range(2):
                    rows = slice(64 * h, 64 * h + 64)
                    nc.tensor.matmul(dst[:, h, :], lhs[rows, :], rhs[rows, :], start=True, stop=False)
                for h in range(2):
                    ins = nc.tensor.matmul(dst[:, h, diagonal:diagonal + P], mask, unit, start=False, stop=True)
                return ins

            for e in PERIODS:
                what, g, i = e
                if what == TURN:
                    b, c = divmod(g, KD)
                    ring_free(e)
                    for j in range(2):
                        for t in range(TB):
                            ins = nc.tensor.transpose(pair_of_banks(e)[:, j, t * P:(t + 1) * P], qk[:, j, TB * b + t, c * P:(c + 1) * P],
                                                      ident[:, :])
                    ins.then_inc(sem("block_psum"), 1)
                elif what == SPREAD:
                    ring_free(e)
                    pe.wait_ge(sem("block_split"), g // 4 + 1)
                    for j in range(2):
                        for part in range(2):
                            ins = nc.tensor.matmul(pair_of_banks(e)[:, j, :], spread[:, 2 * j + part, g % 4, :],
                                                   W[part][:, 1 + g // 4 % 2, j, :], start=(part == 0), stop=(part == 1))
                    ins.then_inc(sem("stack_psum"), 1)
                elif what == ONE:
                    ring_free(e)
                    if i == 3:
                        pe.wait_ge(sem("q_stack"), g + 1)
                        pe.wait_ge(sem("k_stack"), g + 1)
                    n = (i + 1) * P
                    masked(pair_of_banks(e)[:, :, 0:n], q_stack(g)[:, i * P:n], k_stack(g)[:, 0:n], i * P,
                           ident16[:, :], causal16[:, :]).then_inc(sem("scores"), 1)
                elif what == FLIP:
                    ring_free(e)
                    pe.wait_ge(sem("heads_t"), g + 1)
                    for t in range(TB):
                        ins = nc.tensor.transpose(pair_of_banks(e)[:, 0, t * P:(t + 1) * P], heads_t[:, g % 2, t * P:(t + 1) * P], ident[:, :])
                    ins.then_inc(sem("flipped"), 1)
                elif what == PLACE:
                    pe.wait_ge(sem("max_row"), g + 1)
                    if g:
                        pe.wait_ge(sem("q_less_max"), g)
                    for t in range(TB):
                        ins = nc.tensor.matmul(bank[6][:, t * P:(t + 1) * P], max_row[:, t, :], ident_r[:, :], start=True, stop=True)
                    ins.then_inc(sem("placed"), 1)
                elif what == TWO:
                    ring_free(e)
                    if i == 0:
                        pe.wait_ge(sem("q_less_max"), g + 1)
                    masked(pair_of_banks(e)[:, :, 0:(TB - i) * P], k_stack(g)[:, i * P:(i + 1) * P], q_less_max(g)[:, i * P:S], 0,
                           causal16[:, :], ident16[:, :]).then_inc(sem("scores_t"), 1)
                else:
                    b, p = PAIRS[g]
                    pe.wait_ge(sem("exp"), TB * g + i + 1)
                    if i == 0 and g % 2 == 0 and g:
                        pe.wait_ge(sem("heads_t"), g // 2)
                    for h in range(2):
                        row, col = 32 * (g % 2 * 2 + h), (2 * p + h) * (HD + 1)
                        ins = nc.tensor.matmul(bank[7][row:row + 32, i * P:S], v[:, TB * b + i, col:col + 32],
                                               probs[:, (TB * g + i) % 3, h, 0:(TB - i) * P], start=(i == 0), stop=(i == TB - 1))
                    ins.then_inc(sem("pv"), 1)
            pe.wait_ge(sem("o_ready"), NPR // 2)
            for t in range(NT + XT_LAG + 1):
                if t < NT:
                    if t >= 2:
                        pe.wait_ge(sem("o_split"), t - 1)
                    for k in range(KD):
                        ins = nc.tensor.transpose(bank[4 + t % 2][:, k * P:(k + 1) * P], y[:, t, k * P:(k + 1) * P], ident[:, :])
                    ins.then_inc(sem("o_psum"), 1)
                if 1 <= t <= NT:
                    c = t - 1
                    pe.wait_ge(sem("o_split"), c + 1)
                    if c >= 2:
                        pe.wait_ge(sem("y_ready0"), c - 1)
                    split_product(bank[c % 2][:, :], lambda i, k: (o_hi, o_lo)[i][:, c % 2, k, :],
                                  lambda i, k: W[i][:, 0, k, :], range(KD)).then_inc(sem("wo_done"), 1)
                xt_tile(1, t - 1 - XT_LAG)

            def ffn(s):
                def prep(m):
                    h0, n = HT[m]
                    for c in range(3):
                        q = 3 * m + c
                        if q >= 2:
                            pe.wait_ge(sem(f"wfull{s}"), q - 1)
                        elif q == 0:
                            pe.wait_ge(sem(f"side_in{s}"), 96 if s == 1 else 144)
                            pe.wait_ge(sem(f"xt_ready{s}"), NT)
                        dst = bank[6 + q % 2]
                        if c < 2:
                            for k in range(KD):
                                if s == 1:
                                    lhs, rhs = lora_b[32 * c:32 * c + RANK, k * P:(k + 1) * P], lora_a[32 * c:32 * c + RANK, h0:h0 + n]
                                else:
                                    lhs, rhs = s4sel[32 * c:32 * c + 8, k, :], s4[32 * c:32 * c + 8, h0:h0 + n]
                                ins = nc.tensor.matmul(dst[:, k * P:k * P + n], lhs, rhs, start=True, stop=True)
                        elif s == 1:
                            ins = nc.tensor.matmul(dst[0:n, :], lora_a[64:64 + RANK, h0:h0 + n], lora_b[64:64 + RANK, :], start=True, stop=True)
                        else:
                            for e in range(2):
                                if e:
                                    ins.then_inc(sem("scales_even"), 1)
                                    pe.wait_ge(sem("scales_even"), m + 1)
                                ins = nc.tensor.matmul(dst[0:n, e * 256:e * 256 + 256], s4dsel[64 * e:64 * e + 43, h0:h0 + n], s4d[64 * e:64 * e + 43, :], start=True, stop=True)
                        ins.then_inc(sem(f"prep{s}"), 1)

                def gate_up(m):
                    n = hid(m)
                    for hf_ in range(2):
                        u = 2 * m + hf_
                        pe.wait_ge(sem(f"wlo{s}"), 3 * m + 2)
                        if u >= 2:
                            pe.wait_ge(sem(f"h_full{s}"), u - 1)
                        for g in range(2):
                            ins = split_product(bank[2 * (u % 2) + g][0:n, :],
                                                lambda i, k: (wgu_hi, wgu_lo)[i][:, 2 * (m % 2) + g, k, 0:n],
                                                lambda i, k: XT[i][:, k, hf_ * 512:hf_ * 512 + 512], range(KD))
                        ins.then_inc(sem(f"gu{s}"), 1)

                def down(gq):
                    m0, m1 = GROUPS[gq]
                    pe.wait_ge(sem(f"h_lo{s}"), 2 * m1)
                    pe.wait_ge(sem(f"wlo{s}"), 3 * m1)
                    for t in range(NT):
                        if t >= 2:
                            pe.wait_ge(sem(f"y_ready{s}" if gq else f"y_part{s}"), t - 1)
                        elif gq:
                            pe.wait_ge(sem(f"y_part{s}"), NT)
                        todo = [(m, i, j) for m in range(m0, m1) for i, j in COMBOS]
                        for c, (m, i, j) in enumerate(todo):
                            n = hid(m)
                            ins = nc.tensor.matmul(bank[4 + t % 2][:, :], (h_hi, h_lo)[i][0:n, m % RING, t * P:(t + 1) * P],
                                                   (wd_hi, wd_lo)[j][0:n, m % RING, :], start=(c == 0), stop=(c == len(todo) - 1))
                        ins.then_inc(sem(f"down{s}"), 1)
                        if gq and s < 3:
                            xt_tile(s + 1, t - XT_LAG)

                prep(0)
                for m in range(len(HT)):
                    if m + 1 < len(HT):
                        prep(m + 1)
                    gate_up(m)
                    if m == GROUPS[0][1]:
                        down(0)
                down(1)

            ffn(1)
            for t in range(NT - XT_LAG, NT):
                xt_tile(2, t)
            pe.wait_ge(sem("xt_ready2"), NT)
            pe.wait_ge(sem("win_split"), 1)
            for b in range(B):
                split_product(bank[b][:, :], lambda i, k: (win_hi, win_lo)[i][:, k, :],
                              lambda i, k: XT[i][:, k, b * S:(b + 1) * S], range(KD)).then_inc(sem("mix_in"), 1)

            def mix_norm(n):
                pe.wait_ge(sem("h_ready"), n + 1)
                nc.tensor.matmul(bank[0][:, :], cmat[:, :], hm[:, :], start=True, stop=True).then_inc(sem("centred"), 1)
                pe.wait_ge(sem("mix_sq"), n + 1)
                nc.tensor.matmul(bank[1][:, :], bmat[:, :], wk[:, 0, :], start=True, stop=True).then_inc(sem("mix_var"), 1)

            for l in range(DEPTH):
                mix_norm(2 * l)
                mix_norm(2 * l + 1)
                pe.wait_ge(sem("mix_affine"), l + 1)
                for f in range(2):
                    for b in range(B):
                        rows = slice(C * b, C * b + C)
                        nc.tensor.matmul(bank[2 + 2 * f + b][:, :], w1t[rows, l, f * P:(f + 1) * P], wk[rows, 8, :],
                                         start=True, stop=True).then_inc(sem("mix_up"), 1)
                pe.wait_ge(sem("mix_act"), 4 * l + 4)
                for b in range(B):
                    for f in range(2):
                        ins = nc.tensor.matmul(bank[6][C * b:C * b + C, :], w2t[:, l, f, :], g1[:, 2 * f + b, :],
                                               start=(f == 0), stop=(f == 1))
                ins.then_inc(sem("mix_down"), 1)
            mix_norm(2 * DEPTH)
            pe.wait_ge(sem("mix_affine"), DEPTH + 1)
            for t in range(NT + XT_LAG):
                if t < NT:
                    rows = slice(C * (t // TB), C * (t // TB) + C)
                    if t >= 2:
                        pe.wait_ge(sem("y_ready2"), t - 1)
                    nc.tensor.matmul(bank[2 + t % 2][:, :], wk[rows, 8, (t % TB) * P:(t % TB + 1) * P], wout[rows, :],
                                     start=True, stop=True).then_inc(sem("mix_out"), 1)
                xt_tile(3, t - XT_LAG)
            ffn(3)


def kernel(**inputs):
    import numpy as np
    import concourse.bacc as bacc
    from concourse import mybir as _mybir
    from concourse.bass_utils import run_bass_kernel_spmd as _run
    import ml_dtypes

    A = {k: np.asarray(w) for k, w in inputs.items()}
    f32 = np.float32
    arr = {}
    arr["x"] = A["L0_attn_x"].reshape(N, D)
    for n in ("wq", "wk", "wv", "wo"):
        arr[n] = A["L0_attn_" + n]
    arr["ident"] = np.eye(P, dtype=f32)
    arr["ident16"] = np.eye(P).astype(ml_dtypes.bfloat16)
    arr["causal16"] = np.where(np.arange(P)[None, :] > np.arange(P)[:, None], -1e30, 0.0).astype(ml_dtypes.bfloat16)
    arr["neghalf"] = np.full((P, 4), -0.5, f32)
    inv = 1.0 / 10000.0 ** (np.arange(0, HD, 2)[:HD // 2].astype(f32) / HD)
    ang = np.outer(np.arange(S), inv).astype(f32)
    cos, sin = np.cos(ang), np.sin(ang)
    c2 = np.stack([cos, cos], -1).reshape(TB, P, HD).transpose(1, 0, 2)
    s2 = np.stack([-sin, sin], -1).reshape(TB, P, HD).transpose(1, 0, 2)
    scale = 1.0 / np.sqrt(f32(HD))
    arr["rope_c"] = np.stack([c2 * scale, c2], 1).astype(f32)
    arr["rope_s"] = np.stack([s2 * scale, s2], 1).astype(f32)
    row = np.arange(P)
    copy = row % 64 // HD
    spread = np.zeros((P, 2, 2, 4, P), f32)
    for j, low in enumerate((copy == 2, copy == 1)):
        for pair in range(4):
            for r in row[copy < 3]:
                spread[2 * HD * pair + HD * (r // 64) + r % HD, j, int(low[r]), pair, r] = 1.0
    arr["k_one"] = np.isin(row % 64, (3 * HD, 3 * HD + 1)).astype(f32)[:, None]
    arr["spread"] = spread.reshape(P, 4, D)
    arr["gu_t"] = np.stack([A["L0_ffn_gate_w"].T, A["L0_ffn_up_w"].T])
    arr["down_t"] = A["L0_ffn_down_w"].T
    for n in ("gate", "up"):
        arr[n + "_a"] = A[f"L0_ffn_{n}_a"]
        arr[n + "_bt"] = A[f"L0_ffn_{n}_b"].T
    arr["down_a"] = A["L0_ffn_down_a"]
    arr["down_bt"] = A["L0_ffn_down_b"].T
    def byte_of(w, rows, cols):
        return np.concatenate([w, w], axis=1).reshape(rows, cols).T
    arr["w13"] = np.stack([byte_of(A["L1_ffn_w1"], F, D), byte_of(A["L1_ffn_w3"], F, D)])
    arr["w2"] = byte_of(A["L1_ffn_w2"], D, F)
    arr["s13"] = np.stack([A["L1_ffn_s1"].reshape(F, 8).T, A["L1_ffn_s3"].reshape(F, 8).T])
    arr["s2"] = A["L1_ffn_s2"].reshape(D // 2, 43).T
    sel = np.zeros((8, KD, P), f32)
    for k in range(KD):
        for p in range(P):
            sel[2 * k + p // GROUP4, k, p] = 1.0
    arr["s4sel"] = sel
    dsel = np.zeros((2, 43, F), f32)
    for e in range(2):
        dsel[e, (F * e + np.arange(F)) // GROUP4, np.arange(F)] = 1.0
    arr["s4dsel"] = dsel
    sh = np.zeros((P, 5, 2), np.int32)
    for e in range(5):
        low = ((F * e + np.arange(P)) % P if e < 4 else np.arange(P)) >= GROUP4
        sh[:, e, 0] = np.where(low, 28, 0)
        sh[:, e, 1] = np.where(low, 28, 4)
    arr["shifts"] = sh
    arr["win_t"] = np.concatenate([A["L1_attn_Win"], A["L1_attn_Win"]], 0).T.reshape(KD, P, P).transpose(1, 0, 2)
    w1 = A["L1_attn_W1"].transpose(2, 0, 1)
    arr["w1_t"] = np.concatenate([w1, w1], 0)
    arr["w2_t"] = A["L1_attn_W2"].transpose(0, 2, 1).reshape(DEPTH, 2, P, C).transpose(2, 0, 1, 3)
    arr["wout_t"] = np.concatenate([A["L1_attn_Wout"].T] * 2, 0)
    block64 = np.kron(np.eye(2), np.full((C, C), 1.0 / C))
    arr["bmat"] = block64.astype(f32)
    arr["cmat"] = (np.eye(P) - block64).astype(f32)
    names = ("ln1_w", "ln1_b", "phz_re", "phz_im", "lc_re", "lc_im", "sc_lin", "ln2_w", "ln2_b", "b2")
    ch = np.stack([A["L1_attn_" + n].T for n in names], 1)
    arr["chan"] = np.concatenate([ch, ch], 0)
    arr["b1"] = A["L1_attn_b1"].reshape(DEPTH, 2, P).transpose(2, 0, 1)
    la = np.stack([A["L1_attn_bin"], A["L1_attn_lnl_w"], A["L1_attn_lnl_b"]], 1)
    arr["last"] = np.concatenate([la, la], 0)
    arr["bout"] = A["L1_attn_bout"]

    nc = bacc.Bacc("TRN2", target_bir_lowering=False, num_devices=1)
    arrays, aps = {}, {}
    for name, w in arr.items():
        w = np.ascontiguousarray(w)
        arrays["in_" + name] = w
        aps[name] = nc.dram_tensor("in_" + name, w.shape, _mybir.dt.from_np(w.dtype), kind="ExternalInput").ap()
    out = nc.dram_tensor("out", (N, D), F32, kind="ExternalOutput").ap()
    sandwich(nc, aps, out)
    r = _run(nc, [arrays], core_ids=[0])
    return r.results[0]["out"].reshape(B, S, D)
```

```python
from contextlib import ExitStack

import concourse.bass as bass
from concourse import mybir

F32 = mybir.dt.float32
F32R = mybir.dt.float32r
BF16 = mybir.dt.bfloat16
I32 = mybir.dt.int32
ALU = mybir.AluOpType
ACT = mybir.ActivationFunctionType
AX_X = mybir.AxisListType.X

P = 128
B, S, D = 2, 512, 512
N = B * S
NT = N // P
TB = S // P
KD = D // P
H, HD = 32, 16
NPAIR = H // 2
F = 1376
HT = [(k * P, min(P, F - k * P)) for k in range((F + P - 1) // P)]
GROUPS = [(0, 6), (6, 11)]
RING = 7
RANK = 16
GROUP4 = 64
C = 64
DEPTH, DFF = 4, 256
EPS = 1e-5
HALF = S // 2
TURN_LOW, TURN_HIGH = 32, 16


def sandwich(nc, a, out):
    es = ExitStack()
    sems = {}

    def sem(name):
        if name not in sems:
            sems[name] = es.enter_context(nc.semaphore(name))
        return sems[name]

    def sb(ctx, name, shape, dt=F32):
        return ctx.enter_context(nc.sbuf_tensor(name, shape, dt))

    with es:
        psum = es.enter_context(nc.psum_tensor("psum", [P, 8, 512], F32))
        bank = [psum[:, i, :] for i in range(8)]
        PAIRS = [(b, p) for b in range(B) for p in range(NPAIR)]
        x = sb(es, "x", [P, NT, D])
        xt_hi = sb(es, "xt_hi", [P, KD, N], F32R)
        xt_lo = sb(es, "xt_lo", [P, KD, N], F32R)
        y = sb(es, "y", [P, NT, D])
        ident = sb(es, "ident", [P, P])
        ident16 = sb(es, "ident16", [P, P], BF16)
        causal16 = sb(es, "causal16", [P, P], BF16)
        neghalf = sb(es, "neghalf", [P, 4])
        bnst = sb(es, "bnst", [P, 6])
        mv = sb(es, "mv", [P, 8, NT, 2])
        ve = sb(es, "ve", [P, 8, NT])
        rstd = sb(es, "rstd", [P, 8, NT])
        xn = sb(es, "xn", [P, 2, D])
        shifts = sb(es, "shifts", [P, 5, 2], I32)
        low_rows = sb(es, "low_rows", [P, 3])
        at = ExitStack()
        with at:
            qk = sb(at, "qk", [P, 2, NT, D])
            v = sb(at, "v", [P, NT, H * (HD + 1) + 32 - (HD + 1)])
            w_hi = sb(at, "w_hi", [P, 3, KD, D], F32R)
            w_lo = sb(at, "w_lo", [P, 3, KD, D], F32R)
            rope_c = sb(at, "rope_c", [P, 2, TB, HD])
            rope_s = sb(at, "rope_s", [P, 2, TB, HD])
            negmax = sb(at, "negmax", [P, len(PAIRS), TB, 2])
            einv = sb(at, "einv", [P, len(PAIRS) // 2, TB, 4])
            k_one = sb(at, "k_one", [P, 1])
            with ExitStack() as sub:
                w_raw = sb(sub, "w_raw", [P, KD, D])
                rot_c = sb(sub, "rot_c", [P, 2, D])
                rot_s = sb(sub, "rot_s", [P, 2, D])
            with ExitStack() as sub:
                spread = sb(sub, "spread", [P, 4, 4, P], F32R)
                probs = sb(sub, "probs", [P, 3, 2, S])
                heads_t = sb(sub, "heads_t", [P, 2, S])
                max_row = sb(sub, "max_row", [P, TB, P], F32R)
                ident_r = sb(sub, "ident_r", [P, P], F32R)
                o_hi = sb(sub, "o_hi", [P, 2, KD, P], F32R)
                o_lo = sb(sub, "o_lo", [P, 2, KD, P], F32R)
        with ExitStack() as sub:
            sb(sub, "beside_hi", [P, NT * 2 * D + NT * (H * (HD + 1) + 32 - (HD + 1)) + KD * D])
            lora = sb(sub, "lora", [P, 2 * KD * D])
            sb(sub, "beside_lo", [P, KD * D])
            lora_hi = sb(sub, "lora_hi", [P, 2 * KD * D], F32R)
            LORA = [(rows, slice(c * (F + D), (c + 1) * (F + D))) for c, rows in enumerate((112, 48))]
        ph = ExitStack()
        with ph:
            chan = sb(ph, "chan", [P, 10, DEPTH])
            pw = sb(ph, "pw", [P, 8, DEPTH])
            low_turn = sb(ph, "low_turn", [P, 2, DEPTH, TURN_LOW])
            high_turn = sb(ph, "high_turn", [P, 2, DEPTH, TURN_HIGH + 1])
            turn_tmp = sb(ph, "turn_tmp", [P, 2, DEPTH, TURN_LOW // 2])
            ff = ExitStack()
            with ff:
                side_gu = sb(ff, "side_gu", [112, F + D], F32R)
                side_d = sb(ff, "side_d", [107, F + D], F32R)
                wgu_raw = sb(ff, "wgu_raw", [P, 4, KD, P])
                wd_raw = sb(ff, "wd_raw", [P, 2, D])
                wgu_hi = sb(ff, "wgu_hi", [P, 4, KD, P], F32R)
                wgu_lo = sb(ff, "wgu_lo", [P, 4, KD, P], F32R)
                with ExitStack() as rest:
                    wd_hi = sb(rest, "wd_hi", [P, RING, D], F32R)
                    wd_lo = sb(rest, "wd_lo", [P, RING, D], F32R)
                    h_hi = sb(rest, "h_hi", [P, RING, N], F32R)
                    h_lo = sb(rest, "h_lo", [P, RING, N], F32R)
                    sg = sb(rest, "sg", [P, 2, D])
                    hf = sb(rest, "hf", [P, 2, D])
                mx = ExitStack()
                with mx:
                    win_raw = sb(mx, "win_raw", [P, KD, P])
                    win_hi = sb(mx, "win_hi", [P, KD, P], F32R)
                    win_lo = sb(mx, "win_lo", [P, KD, P], F32R)
                    w1t = sb(mx, "w1t", [P, DEPTH, DFF])
                    w2t = sb(mx, "w2t", [P, DEPTH, 2, C])
                    wout = sb(mx, "wout", [P, D])
                    bout = sb(mx, "bout", [P, D])
                    cmat = sb(mx, "cmat", [P, P])
                    bmat = sb(mx, "bmat", [P, P])
                    b1 = sb(mx, "b1", [P, DEPTH, 2])
                    last = sb(mx, "last", [P, 3])
                    turns = sb(mx, "turns", [P, DEPTH, 2, S])
                    hm = sb(mx, "hm", [P, S])
                    squares, centred, normed, active, cos_in, sin_in, cos_out, sin_out, demod, sin_demod, affine = (
                        sb(mx, name, [P, 2, HALF]) for name in ("squares", "centred", "normed", "active", "cos_in", "sin_in", "cos_out",
                                                               "sin_out", "demod", "sin_demod", "affine"))
                    var_eps = sb(mx, "var_eps", [P, 2, 4])
                    inv_dev = sb(mx, "inv_dev", [P, 2, 4])
                    inv_dev_c = sb(mx, "inv_dev_c", [P, 2, 2, P])
                    turn_a = sb(mx, "turn_a", [P, 2, HALF])
                    g1 = sb(mx, "g1", [P, 2, 2, B, HALF])
                    scale_gu = sb(mx, "scale_gu", [48, F + D])
                    scale_d = sb(mx, "scale_d", [107, F + D // 2])
                    scale_hi = sb(mx, "scale_hi", [48, F], F32R)
        block = es.enter_context(nc.Block())

        ONE, TWO, TURN, FLIP, SPREAD, PV, PLACE = range(7)
        NPR = len(PAIRS)
        PERIODS = []
        for g in range(-3, NPR + 1):
            todo = [(ONE, g + 1, 3), (TWO, g, 0), (PV, g - 1, 2), (ONE, g + 1, 2), (PV, g - 1, 3), (TWO, g, 1), (ONE, g + 1, 1), (PV, g, 0),
                    (TWO, g, 2), (ONE, g + 1, 0), (PV, g, 1), (FLIP, g // 2 - 1, 0), (TURN, (g + 3) // 4, 0),
                    (SPREAD, g + 2, 0), (TWO, g, 3), (PLACE, g + 1, 0)]
            PERIODS += [(what, p, i) for what, p, i in todo
                        if ((g + 3) % 4 == 0 and g + 3 < NPR if what == TURN else
                            g % 2 == 0 and g >= 2 if what == FLIP else 0 <= p < NPR)]
        RINGED = [e for e in PERIODS if e[0] in (ONE, TWO, TURN, FLIP, SPREAD)]
        nth = {}
        for what in (ONE, TWO, TURN, FLIP, SPREAD):
            for n, e in enumerate([e for e in RINGED if e[0] == what]):
                nth[e] = n
        ring = {e: n % 3 for n, e in enumerate(RINGED)}

        def pair_of_banks(e):
            return psum[:, 2 * ring[e]:2 * ring[e] + 2, :]

        COMBOS = ((0, 0), (0, 1), (1, 0))
        ROPE_LAG = 3
        RAW = [w_raw[:, :, :], y[:, 0:KD, :], y[:, KD:2 * KD, :]]
        EARLY = (NT + 2, NT + 3)
        XT_LAG = 4
        XT = (xt_hi, xt_lo)

        def k_stack(g):
            return w_hi[:, 1 + g % 3 // 2, 2 + g % 3 % 2, :]

        def q_stack(g):
            return (w_hi, w_lo)[g % 2][:, 2, 3, :]

        def q_less_max(g):
            return w_lo[:, 1, 2 + g % 2, :]

        def turn(l):
            return turns[:, l, :, :]

        def turn_half(l, c):
            return turns[:, l, :, c * HALF:(c + 1) * HALF]

        CENTRE, VAR, SPREAD_DEV, SILU, MOD, SCAN, DEMOD, AFFINE, UP, DOWN, TABLE, SIDE = range(12)
        stages = [(n, c) for l in range(DEPTH) for n in (2 * l, 2 * l + 1) for c in range(2)] + [(2 * DEPTH, 0), (2 * DEPTH, 1)]

        def steps_of(n, c):
            first = [(CENTRE, n, c, 0), (VAR, n, c, 0), (SPREAD_DEV, n, c, 0)]
            if n == 2 * DEPTH:
                return first + [(AFFINE, n, c, 0)]
            if n % 2 == 0:
                return first + [(SILU, n, c, 0), (MOD, n, c, 0), (SCAN, n, c, 0), (DEMOD, n, c, 0)]
            return first + [(AFFINE, n, c, 0), (UP, n, c, 0), (UP, n, c, 1), (DOWN, n, c, 0)]

        MIXER = steps_of(*stages[0])
        for i in range(1, len(stages) - 1, 2):
            one, two = steps_of(*stages[i]), steps_of(*stages[i + 1])
            for k in range(max(len(one), len(two))):
                MIXER += one[k:k + 1] + two[k:k + 1]
                if k == 4:
                    n, c = stages[i + 1]
                    l = (n + 1) // 2
                    if l < DEPTH:
                        MIXER.append((TABLE, l, 0, 0) if n % 2 else (TABLE, l, 1, 0))
            if i // 2 < 4:
                MIXER.append((SIDE, i // 2, 0, 0))
        MIXER += steps_of(*stages[-1])
        done_at = {}
        for e in MIXER:
            done_at[e] = sum(f[0] == e[0] for f in MIXER[:MIXER.index(e) + 1])
        h_at = {(-1, 0): 1, (-1, 1): 1}
        for e in MIXER:
            if e[0] in (DEMOD, DOWN):
                h_at[e[1], e[2]] = len(h_at)

        PREPS, done = [], 3
        for u in range(2 * len(HT)):
            upto = min(done + 2, 3 * (u // 2 + 3), 3 * len(HT))
            PREPS.append(range(done, upto))
            done = upto

        def hid(m):
            return HT[m][1]

        @block.sync
        def _(sp):
            for t in range(NT):
                sp.dma_start(x[:, t, :], a["x"][t * P:(t + 1) * P, :]).then_inc(sem(f"x_in{t}"), 16)
                if t == 0:
                    sp.dma_start(ident[:, :], a["ident"]).then_inc(sem("ident_in"), 16)
                elif t in (1, 3, 4):
                    j = (1, 3, 4).index(t)
                    sp.dma_start(RAW[j], a[("wq", "wk", "wv")[j]].rearrange("(k p) n -> p k n", p=P)).then_inc(sem(f"w_in{j}"), 16)
            for dst, name in ((rope_c[:, :, :, :], "rope_c"), (rope_s[:, :, :, :], "rope_s"), (ident16[:, :], "ident16"),
                              (causal16[:, :], "causal16"), (k_one[:, :], "k_one"), (shifts[:, :, :], "shifts"), (low_rows[:, :], "low_rows")):
                sp.dma_start(dst, a[name]).then_inc(sem("consts_in"), 16)
            sp.wait_ge(sem("w_split"), 2)
            sp.dma_start(RAW[1], a["spread"]).then_inc(sem("spread_in"), 16)
            sp.wait_ge(sem("w_split"), 3)
            sp.dma_start(RAW[2], a["wo"].rearrange("(k p) n -> p k n", p=P)).then_inc(sem("wo_in"), 16)

            def ffn_loads(s):
                if s == 1:
                    for (rows, cols), name in zip(LORA, ("side_gu1", "side_d1")):
                        sp.dma_start(lora[0:rows, cols], a[name]).then_inc(sem("side_in1"), 16)
                    wgu, wd, raw_gu, raw_d = a["gu_t"], a["down_t"], wgu_raw[:, :, :, :], wd_raw[:, :, :]
                else:
                    sp.dma_start(scale_gu[:, :], a["side_gu3"]).then_inc(sem("side_in3"), 16)
                    sp.dma_start(scale_d[:, :], a["side_d3"]).then_inc(sem("side_in3"), 16)
                    wgu, wd = a["w13"], a["w2"]
                    raw_gu, raw_d = wgu_raw[:, :, :, :].bitcast(I32), wd_raw[:, :, :].bitcast(I32)
                for m, (h0, n) in enumerate(HT):
                    if m >= 2:
                        sp.wait_ge(sem(f"wlo{s}"), 3 * (m - 1))
                    for g in range(2):
                        sp.dma_start(raw_gu[:, 2 * (m % 2) + g, :, 0:n],
                                     wgu[g].rearrange("(k p) h -> p k h", p=P)[:, :, h0:h0 + n]).then_inc(sem(f"wraw{s}_{m % 2}"), 16)
                    sp.dma_start(raw_d[0:n, m % 2, :], wd[h0:h0 + n, :]).then_inc(sem(f"wraw{s}_{m % 2}"), 16)
                    if s == 1 and m == 1:
                        sp.dma_start(chan[:, :, :], a["chan"]).then_inc(sem("chan_in"), 16)

            sp.wait_ge(sem("o_ready"), NPR // 2)
            ffn_loads(1)
            sp.wait_ge(sem("y_ready1"), NT)
            for dst, name in ((win_raw[:, :, :], "win_t"), (w1t[:, :, :], "w1_t"), (w2t[:, :, :, :], "w2_t"), (wout[:, :], "wout_t"),
                              (cmat[:, :], "cmat"), (bmat[:, :], "bmat"), (b1[:, :, :], "b1"),
                              (last[:, :], "last")):
                sp.dma_start(dst, a[name]).then_inc(sem("mixer_in"), 16)
            sp.dma_start(bout[:, :], a["bout"].partition_broadcast(P)).then_inc(sem("mixer_in"), 16)
            ffn_loads(3)
            for t in range(NT):
                sp.wait_ge(sem("x_sum3"), t + 1)
                sp.dma_start(out[t * P:(t + 1) * P, :], x[:, t, :]).then_inc(sem("stored"), 16)
            sp.wait_ge(sem("stored"), 16 * NT)

        @block.gpsimd
        def _(pool):
            pool_steps = [0]

            def link(ins):
                pool_steps[0] += 1
                ins.then_inc(sem("pool_step"), 1)
                pool.wait_ge(sem("pool_step"), pool_steps[0])

            def inv_std(n, t, stats, done):
                pool.wait_ge(sem(stats), t + 1)
                link(nc.gpsimd.tensor_scalar(ve[:, n, t:t + 1], mv[:, n, t, 1:2], EPS, None, ALU.add))
                nc.gpsimd.tensor_tensor(rstd[:, n, t:t + 1], ve[:, n, t:t + 1], neghalf[:, 0:1], ALU.pow).then_inc(sem(done), 1)

            def gu_low(s, m, g):
                r, n = 2 * (m % 2) + g, hid(m)
                pool.wait_ge(sem(f"whi{s}"), 3 * m + g + 1)
                if m >= 2:
                    pool.wait_ge(sem(f"gu{s}"), 2 * (m - 1))
                nc.gpsimd.tensor_tensor(wgu_lo[:, r, :, 0:n], wgu_raw[:, r, :, 0:n],
                                        wgu_hi[:, r, :, 0:n].bitcast(F32), ALU.subtract).then_inc(sem(f"wlo{s}"), 1)

            def norm_out(s):
                for t in range(NT + 2):
                    if t < NT:
                        inv_std(2 * s + 1, t, f"y_stats{s}", f"y_rstd{s}")
                    if 1 <= t <= NT:
                        u = t - 1
                        pool.wait_ge(sem(f"y_norm{s}"), u + 1)
                        nc.gpsimd.tensor_tensor(x[:, u, :], x[:, u, :], y[:, u, :], ALU.add).then_inc(sem(f"x_sum{s}"), 1)
                    if t >= 2 and s < 3:
                        inv_std(2 * s + 2, t - 2, f"x_stats{s + 1}", f"x_rstd{s + 1}")
                    if s in (0, 2) and t == NT - 2:
                        for g in range(2):
                            gu_low(s + 1, 0, g)

            nc.gpsimd.memset(neghalf[:, :], -0.5).then_inc(sem("neghalf_set"), 1)
            nc.gpsimd.memset(v[:, :, :], 1.0).then_inc(sem("v_ones"), 1)
            pool.wait_ge(sem("neghalf_set"), 1)
            for t in range(NT + ROPE_LAG):
                if t < NT:
                    inv_std(0, t, "x_stats0", "x_rstd0")
                if t >= ROPE_LAG:
                    for j in range(2):
                        pool.wait_ge(sem("rotated"), 2 * (t - ROPE_LAG) + j + 1)
                        nc.gpsimd.tensor_tensor(qk[:, j, t - ROPE_LAG, :], rot_c[:, j, :], rot_s[:, j, :], ALU.add).then_inc(sem("qk_ready"), 1)
            pool.wait_ge(sem("wo_in"), 16)
            pool.wait_ge(sem("proj"), 3 * NT)
            nc.gpsimd.tensor_copy(w_hi[:, 0, :, :], RAW[2]).then_inc(sem("wo_hi"), 1)
            pool.wait_ge(sem("wo_hi"), 1)
            nc.gpsimd.tensor_tensor(w_lo[:, 0, :, :], RAW[2], w_hi[:, 0, :, :].bitcast(F32), ALU.subtract).then_inc(sem("wo_split"), 1)
            for e in PERIODS:
                if e[0] == TWO:
                    pool.wait_ge(sem("exp"), nth[e] + 1)
                    diagonal = probs[:, nth[e] % 3, :, 0:P]
                    nc.gpsimd.affine_select(out=diagonal, in_=diagonal, pattern=[[0, 2], [1, P]], compare_op=ALU.is_ge, fill=0.0, base=0,
                                            channel_multiplier=-1).then_inc(sem("probs"), 1)

            norm_out(0)

            def ffn(s):
                def wd_low(m):
                    n = hid(m)
                    pool.wait_ge(sem(f"whi{s}"), 3 * m + 3)
                    if m >= RING:
                        pool.wait_ge(sem(f"down{s}"), NT)
                    nc.gpsimd.tensor_tensor(wd_lo[0:n, m % RING, :], wd_raw[0:n, m % 2, :],
                                            wd_hi[0:n, m % RING, :].bitcast(F32), ALU.subtract).then_inc(sem(f"wlo{s}"), 1)

                def h_low(u):
                    m, n, cols = u // 2, hid(u // 2), slice(u % 2 * 512, u % 2 * 512 + 512)
                    pool.wait_ge(sem(f"h_hi{s}"), u + 1)
                    if m >= RING:
                        pool.wait_ge(sem(f"down{s}"), NT)
                    nc.gpsimd.tensor_tensor(h_lo[0:n, m % RING, cols], hf[0:n, u % 2, :], h_hi[0:n, m % RING, cols].bitcast(F32),
                                            ALU.subtract).then_inc(sem(f"h_lo{s}"), 1)

                wd_low(0)
                for m in range(len(HT)):
                    if m < 2:
                        h_low(2 * m)
                    if m + 1 < len(HT):
                        for g in range(2):
                            gu_low(s, m + 1, g)
                    if m >= 2:
                        h_low(2 * m)
                    h_low(2 * m + 1)
                    if s == 1 and m == 3:
                        pool.wait_ge(sem("p_sq"), 1)
                        nc.gpsimd.tensor_tensor(pw[:, 1, :], pw[:, 0, :], neghalf[:, 0:4], ALU.pow).then_inc(sem("p_inv"), 1)
                    if m + 1 < len(HT):
                        wd_low(m + 1)

            ffn(1)
            norm_out(1)
            for e in MIXER:
                what, n, c, f = e
                if what == VAR:
                    pool.wait_ge(sem("mix_var_eps"), done_at[e])
                    nc.gpsimd.tensor_tensor(inv_dev[:, c, :], var_eps[:, c, :], neghalf[:, 0:4], ALU.pow).then_inc(sem("mix_inv_dev"), 1)
                elif what == MOD:
                    pool.wait_ge(sem("mix_silu"), done_at[e])
                    nc.gpsimd.tensor_tensor(sin_in[:, c, :], active[:, c, :], turn_half(n // 2, c)[:, 1, :], ALU.mult).then_inc(sem("sin_mod"), 1)
                elif what == DEMOD:
                    pool.wait_ge(sem("sin_scan"), done_at[e])
                    nc.gpsimd.tensor_tensor(sin_demod[:, c, :], sin_out[:, c, :], turn_half(n // 2, c)[:, 1, :], ALU.mult).then_inc(sem("sin_demod"), 1)
            norm_out(2)
            ffn(3)
            norm_out(3)

        @block.scalar
        def _(act):
            def xt_tile(s, t):
                if 0 <= t < NT:
                    act.wait_ge(sem(f"xt_psum{s}"), t + 1)
                    nc.scalar.activation(xt_hi[:, :, t * P:(t + 1) * P], bank[6 + t % 2][:, :].rearrange("p (k n) -> p k n", k=KD),
                                         ACT.Copy).then_inc(sem(f"xt_hi{s}"), 1)

            for t in range(NT + 2):
                if t < NT:
                    xt_tile(0, t)
                if t < 3:
                    act.wait_ge(sem(f"w_in{t}"), 16)
                    nc.scalar.activation(w_hi[:, t, :, :], RAW[t], ACT.Copy).then_inc(sem("w_split_hi"), 1)
                if t >= 2:
                    u = t - 2
                    if u == 0:
                        act.wait_ge(sem("v_ones"), 1)
                    act.wait_ge(sem("proj"), 3 * u + 3)
                    nc.scalar.activation(v[:, u, 0:H * (HD + 1)].rearrange("p (h d) -> p h d", h=H)[:, :, 0:HD],
                                         bank[(3 * u + 2) % 6][:, :].rearrange("p (h d) -> p h d", h=H), ACT.Copy).then_inc(sem("v_ready"), 1)
                if t == NT // 2:
                    act.wait_ge(sem("spread_in"), 16)
                    nc.scalar.activation(spread[:, :, :, :], RAW[1].rearrange("p a (b c) -> p a b c", b=4), ACT.Copy).then_inc(sem("spread_ready"), 1)
            act.wait_ge(sem("qk_ready"), 2 * NT)

            nc.scalar.activation(ident_r[:, :], ident[:, :], ACT.Copy).then_inc(sem("ident_r"), 1)

            for e in PERIODS:
                what, g, i = e
                if what == TURN:
                    act.wait_ge(sem("block_psum"), g + 1)
                    nc.scalar.activation(w_hi[:, 1 + g % 2, 0:2, :], pair_of_banks(e), ACT.Copy).then_inc(sem("block_hi"), 1)
                elif what == TWO:
                    act.wait_ge(sem("scores_t"), nth[e] + 1)
                    if nth[e] >= 3:
                        act.wait_ge(sem("pv"), nth[e] - 2)
                    nc.scalar.activation(probs[:, nth[e] % 3, :, 0:(TB - i) * P], pair_of_banks(e)[:, :, 0:(TB - i) * P],
                                         ACT.Exp).then_inc(sem("exp"), 1)
                elif what == PV and i == TB - 1 and g % 2:
                    act.wait_ge(sem("pv"), TB * (g + 1))
                    if g >= 4:
                        act.wait_ge(sem("flipped"), g // 2 - 1)
                    nc.scalar.activation(heads_t[:, g // 2 % 2, :], bank[7][:, :], ACT.Copy).then_inc(sem("heads_t"), 1)
                elif what == SPREAD:
                    act.wait_ge(sem("stack_psum"), g + 1)
                    nc.scalar.activation(k_stack(g), pair_of_banks(e)[:, 1, :], ACT.Identity, bias=k_one[:, 0:1]).then_inc(sem("k_stack"), 1)
            def w_high(s, m):
                n = hid(m)
                for g in range(2):
                    r = 2 * (m % 2) + g
                    act.wait_ge(sem(f"wfull{s}"), 3 * m + g + 1)
                    if m >= 2:
                        act.wait_ge(sem(f"gu{s}"), 2 * (m - 1))
                    nc.scalar.activation(wgu_hi[:, r, :, 0:n], wgu_raw[:, r, :, 0:n], ACT.Copy).then_inc(sem(f"whi{s}"), 1)

            for t in range(NT + XT_LAG + 1):
                if t in (1, 2):
                    rows, cols = LORA[t - 1]
                    act.wait_ge(sem("side_in1"), 32)
                    nc.scalar.activation(lora_hi[0:rows, cols], lora[0:rows, cols], ACT.Copy).then_inc(sem("side_hi1"), 1)
                elif t == 6:
                    w_high(1, 0)
                if t < NT:
                    act.wait_ge(sem("o_psum"), t + 1)
                    if t >= 2:
                        act.wait_ge(sem("wo_done"), t - 1)
                    nc.scalar.activation(o_hi[:, t % 2, :, :], bank[4 + t % 2][:, :].rearrange("p (k n) -> p k n", k=KD),
                                         ACT.Copy).then_inc(sem("o_hi"), 1)
                if 1 <= t <= NT:
                    act.wait_ge(sem("wo_done"), t)
                    nc.scalar.activation(y[:, t - 1, :], bank[(t - 1) % 2][:, :], ACT.Copy).then_inc(sem("y_ready0"), 1)
                xt_tile(1, t - 1 - XT_LAG)

            def ffn(s):
                def wd_high(m):
                    n = hid(m)
                    act.wait_ge(sem(f"wfull{s}"), 3 * m + 3)
                    if m >= RING:
                        act.wait_ge(sem(f"down{s}"), NT)
                    nc.scalar.activation(wd_hi[0:n, m % RING, :], wd_raw[0:n, m % 2, :], ACT.Copy).then_inc(sem(f"whi{s}"), 1)

                def hidden(u):
                    m, n, cols = u // 2, hid(u // 2), slice(u % 2 * 512, u % 2 * 512 + 512)
                    act.wait_ge(sem(f"gu{s}"), u + 1)
                    if u >= 2:
                        act.wait_ge(sem(f"h_full{s}"), u - 1)
                    nc.scalar.activation(sg[0:n, u % 2, :], bank[2 * (u % 2)][0:n, :], ACT.Silu).then_inc(sem(f"silu{s}"), 1)
                    act.wait_ge(sem(f"h_full{s}"), u + 1)
                    if m >= RING:
                        act.wait_ge(sem(f"down{s}"), NT)
                    nc.scalar.activation(h_hi[0:n, m % RING, cols], hf[0:n, u % 2, :], ACT.Copy).then_inc(sem(f"h_hi{s}"), 1)

                def partial():
                    for t in range(NT):
                        act.wait_ge(sem(f"down{s}"), t + 1)
                        nc.scalar.activation(y[:, t, :], bank[4 + t % 2][:, :], ACT.Copy).then_inc(sem(f"y_part{s}"), 1)

                wd_high(0)
                for m in range(len(HT)):
                    if m < 2:
                        hidden(2 * m)
                    if m + 1 < len(HT):
                        w_high(s, m + 1)
                    if m >= 2:
                        hidden(2 * m)
                    hidden(2 * m + 1)
                    if m == GROUPS[0][1]:
                        partial()
                    if m + 1 < len(HT):
                        wd_high(m + 1)

            ffn(1)
            for t in range(NT):
                xt_tile(2, t)
            act.wait_ge(sem("mixer_in"), 144)
            nc.scalar.activation(win_hi[:, :, :], win_raw[:, :, :], ACT.Copy).then_inc(sem("win_hi"), 1)
            act.wait_ge(sem("p_abs"), 1)
            nc.scalar.activation(pw[:, 3, :], pw[:, 2, :], ACT.Tanh).then_inc(sem("decay"), 1)
            for e in MIXER:
                what, n, c, f = e
                if what == CENTRE:
                    act.wait_ge(sem("mix_centre"), done_at[e])
                    nc.scalar.activation(squares[:, c, :], bank[c][:, 0:HALF], ACT.Square).then_inc(sem("mix_squares"), 1)
                    nc.scalar.activation(centred[:, c, :], bank[c][:, 0:HALF], ACT.Copy).then_inc(sem("mix_centred"), 1)
                elif what == VAR:
                    act.wait_ge(sem("mix_inv_dev"), done_at[e])
                    nc.scalar.activation(inv_dev_c[:, c, :, :].rearrange("p i (b d) -> p (i b) d", b=B),
                                         inv_dev[:, c, :].unsqueeze(2).to_broadcast([P, 4, C]), ACT.Copy).then_inc(sem("mix_repeated"), 1)
                elif what == SILU:
                    act.wait_ge(sem("mix_norm"), done_at[SPREAD_DEV, n, c, 0])
                    nc.scalar.activation(active[:, c, :], normed[:, c, :], ACT.Silu, bias=chan[:, 1, n // 2:n // 2 + 1],
                                         scale=chan[:, 0, n // 2:n // 2 + 1]).then_inc(sem("mix_silu"), 1)
                elif what == UP:
                    act.wait_ge(sem("mix_up"), done_at[e])
                    nc.scalar.activation(g1[:, c, f, :, :], psum[:, 4 + 2 * f:6 + 2 * f, 0:HALF], ACT.Silu,
                                         bias=b1[:, n // 2, f:f + 1]).then_inc(sem("mix_act"), 1)
                elif what == SIDE and n < 3:
                    dst, raw = ((scale_hi[:, :], scale_gu[:, 0:F]), (side_gu[0:48, F:F + D], scale_gu[:, F:F + D]),
                                (side_d[:, 0:F + D // 2], scale_d[:, :]))[n]
                    act.wait_ge(sem("side_in3"), 32)
                    nc.scalar.activation(dst, raw, ACT.Copy).then_inc(sem("side_hi3"), 1)
            for t in range(NT):
                xt_tile(3, t)
                if t == 1:
                    w_high(3, 0)
            ffn(3)

        @block.vector
        def _(dve):
            dve_steps = [0]

            def link(ins):
                dve_steps[0] += 1
                ins.then_inc(sem("dve_step"), 1)
                dve.wait_ge(sem("dve_step"), dve_steps[0])

            def stats(n, t, src, done):
                link(nc.vector.bn_stats(bnst[:, :], src))
                nc.vector.bn_aggr(mv[:, n, t, :], bnst[:, :]).then_inc(sem(done), 1)
                dve.wait_ge(sem(done), t + 1)

            def norm_x(s, t):
                dve.wait_ge(sem(f"x_rstd{s}"), t + 1)
                if t >= 2:
                    dve.wait_ge(sem(f"xt_psum{s}"), t - 1)
                nc.vector.tensor_scalar(xn[:, t % 2, :], x[:, t, :], mv[:, 2 * s, t, 0:1], rstd[:, 2 * s, t:t + 1],
                                        ALU.subtract, ALU.mult).then_inc(sem(f"xn{s}"), 1)

            def low_xt(s, t):
                dve.wait_ge(sem(f"xt_hi{s}"), t + 1)
                nc.vector.tensor_tensor(xt_lo[:, :, t * P:(t + 1) * P], bank[6 + t % 2][:, :].rearrange("p (k n) -> p k n", k=KD),
                                        xt_hi[:, :, t * P:(t + 1) * P].bitcast(F32), ALU.subtract).then_inc(sem(f"xt_ready{s}"), 1)

            def full(s, m, c):
                n, q = hid(m), 3 * m + c
                dve.wait_ge(sem(f"wraw{s}_{m % 2}"), 48 * (m // 2 + 1))
                if c < 2:
                    r = 2 * (m % 2) + c
                    w, ps = wgu_raw[:, r, :, 0:n], bank[6 + q % 2][:, :].rearrange("p (k n) -> p k n", k=KD)[:, :, 0:n]
                else:
                    w, ps = wd_raw[0:n, m % 2, :], bank[6 + q % 2][0:n, :]
                if s == 1:
                    dve.wait_ge(sem(f"prep{s}"), q + 1)
                    nc.vector.tensor_tensor(w, w, ps, ALU.add).then_inc(sem(f"wfull{s}"), 1)
                    return
                wi = w.bitcast(I32)
                if c < 2:
                    link(nc.vector.tensor_scalar(wi, wi, shifts[:, 4, 0:1], shifts[:, 4, 1:2],
                                                 ALU.logical_shift_left, ALU.arith_shift_right))
                else:
                    for e in range(4):
                        part = wi.rearrange("p (d e) -> p d e", e=4)[:, :, e]
                        ins = nc.vector.tensor_scalar(part, part, shifts[0:n, e, 0:1], shifts[0:n, e, 1:2],
                                                      ALU.logical_shift_left, ALU.arith_shift_right)
                    link(ins)
                dve.wait_ge(sem(f"prep{s}"), q + 1)
                if c < 2:
                    nc.vector.tensor_tensor(w, wi, ps, ALU.mult).then_inc(sem(f"wfull{s}"), 1)
                else:
                    nc.vector.tensor_tensor(w.rearrange("p (e two) -> p two e", two=2), wi.rearrange("p (e two) -> p two e", two=2),
                                            ps.rearrange("p (two e) -> p two e", two=2), ALU.mult).then_inc(sem(f"wfull{s}"), 1)

            def norm_out(s, make_y=None):
                for t in range(NT + XT_LAG):
                    if s == 0 and t in (2, 3):
                        n, cols = LORA[t - 2]
                        raw, hi, dst = lora[0:n, cols], lora_hi[0:n, cols], (side_gu, side_d)[t - 2]
                        dve.wait_ge(sem("side_hi1"), t - 1)
                        for c, cols in enumerate((slice(0, F), slice(F, F + D))):
                            nc.vector.scalar_tensor_tensor(out=dst[0:n, cols], in0=hi[:, cols].bitcast(F32), scalar=low_rows[0:n, c:c + 1],
                                                           in1=raw[:, cols], op0=ALU.mult, op1=ALU.add).then_inc(sem("side_ready1"), 1)
                    if s in (0, 2) and t == XT_LAG:
                        for c in range(2):
                            full(s + 1, 0, c)
                    if s == 0:
                        for u in (0, 1) if t == 0 else (t + 1,) if t + 1 < NT else ():
                            turned_low(u)
                    if t < NT:
                        if make_y:
                            make_y(t)
                        dve.wait_ge(sem(f"y_ready{s}"), t + 1)
                        stats(2 * s + 1, t, y[:, t, :], f"y_stats{s}")
                    if 1 <= t <= NT:
                        dve.wait_ge(sem(f"y_rstd{s}"), t)
                        nc.vector.tensor_scalar(y[:, t - 1, :], y[:, t - 1, :], mv[:, 2 * s + 1, t - 1, 0:1],
                                                rstd[:, 2 * s + 1, t - 1:t], ALU.subtract, ALU.mult).then_inc(sem(f"y_norm{s}"), 1)
                    if s < 3:
                        if 2 <= t <= NT + 1:
                            dve.wait_ge(sem(f"x_sum{s}"), t - 1)
                            stats(2 * s + 2, t - 2, x[:, t - 2, :], f"x_stats{s + 1}")
                        if 3 <= t <= NT + 2:
                            norm_x(s + 1, t - 3)
                        if t >= 4:
                            low_xt(s + 1, t - 4)

            def rope(t):
                for j in range(2):
                    u = 2 * t + j
                    dve.wait_ge(sem("proj"), 3 * t + j + 1)
                    if t:
                        dve.wait_ge(sem("qk_ready"), u - 1)
                    src = bank[(3 * t + j) % 6][:, :].rearrange("p (h d) -> p h d", h=H)
                    cs = rope_c[:, j, t % TB, :].unsqueeze(1).to_broadcast([P, H, HD])
                    nc.vector.tensor_tensor(rot_c[:, j, :].rearrange("p (h d) -> p h d", h=H), src, cs, ALU.mult)
                    src = bank[(3 * t + j) % 6][:, :].rearrange("p (h f two) -> p h f two", h=H, two=2)
                    dst = rot_s[:, j, :].rearrange("p (h f two) -> p h f two", h=H, two=2)
                    ss = rope_s[:, j, t % TB, :].rearrange("p (f two) -> p f two", two=2)
                    for e in range(2):
                        ins = nc.vector.tensor_tensor(dst[:, :, :, e], src[:, :, :, 1 - e],
                                                      ss[:, :, e].unsqueeze(1).to_broadcast([P, H, HD // 2]), ALU.mult)
                    ins.then_inc(sem("rotated"), 1)

            for t in range(NT + ROPE_LAG):
                if t < NT:
                    dve.wait_ge(sem(f"x_in{t}"), 16)
                    stats(0, t, x[:, t, :], "x_stats0")
                if 1 <= t <= NT:
                    norm_x(0, t - 1)
                if 2 <= t <= NT + 1:
                    low_xt(0, t - 2)
                if 2 <= t <= 4:
                    dve.wait_ge(sem("w_split_hi"), t - 1)
                    nc.vector.tensor_tensor(w_lo[:, t - 2, :, :], RAW[t - 2], w_hi[:, t - 2, :, :].bitcast(F32), ALU.subtract).then_inc(sem("w_split"), 1)
                if t >= ROPE_LAG:
                    if t == ROPE_LAG:
                        dve.wait_ge(sem("consts_in"), 7 * 16)
                    rope(t - ROPE_LAG)

            dve.wait_ge(sem("qk_ready"), 2 * NT)
            link(nc.vector.memset(max_row[:, :, :].bitcast(F32), 0.0))

            for e in PERIODS:
                what, g, i = e
                if what == TURN:
                    dve.wait_ge(sem("block_hi"), g + 1)
                    nc.vector.tensor_tensor(w_lo[:, 1 + g % 2, 0:2, :], pair_of_banks(e), w_hi[:, 1 + g % 2, 0:2, :].bitcast(F32),
                                            ALU.subtract).then_inc(sem("block_split"), 1)
                elif what == ONE:
                    dve.wait_ge(sem("scores"), nth[e] + 1)
                    nc.vector.tensor_reduce(negmax[:, g, i, :], pair_of_banks(e)[:, :, 0:(i + 1) * P], AX_X, ALU.max,
                                            negate=True).then_inc(sem("row_max"), 1)
                    if i == 0:
                        dve.wait_ge(sem("row_max"), TB * (g + 1))
                        rows = max_row[:, :, :].rearrange("p i (h r) -> p i h r", h=2)
                        link(nc.vector.tensor_copy(rows[:, :, :, 3 * HD], negmax[:, g, :, :]))
                        nc.vector.tensor_tensor(rows[:, :, :, 3 * HD + 1], negmax[:, g, :, :], rows[:, :, :, 3 * HD].bitcast(F32),
                                                ALU.subtract).then_inc(sem("max_row"), 1)
                elif what == FLIP:
                    b, n = divmod(g, NPAIR // 2)
                    dve.wait_ge(sem("flipped"), g + 1)
                    if b:
                        dve.wait_ge(sem("wo_split"), 1)
                    src = pair_of_banks(e)[:, 0, :].rearrange("p (i h r) -> p i h r", i=TB, h=4)
                    link(nc.vector.reciprocal(einv[:, g, :, :], src[:, :, :, HD]))
                    nc.vector.tensor_tensor(y[:, TB * b:TB * b + TB, 4 * HD * n:4 * HD * (n + 1)].rearrange("p i (h d) -> p i h d", h=4),
                                            src[:, :, :, 0:HD], einv[:, g, :, :].unsqueeze(3).to_broadcast([P, TB, 4, HD]),
                                            ALU.mult).then_inc(sem("o_ready"), 1)
                elif what == SPREAD:
                    dve.wait_ge(sem("stack_psum"), g + 1)
                    nc.vector.tensor_copy(q_stack(g), pair_of_banks(e)[:, 0, :]).then_inc(sem("q_stack"), 1)
                elif what == PLACE:
                    dve.wait_ge(sem("placed"), g + 1)
                    nc.vector.tensor_tensor(q_less_max(g), bank[6][:, :], q_stack(g).bitcast(F32), ALU.add).then_inc(sem("q_less_max"), 1)

            def turned_low(t):
                dve.wait_ge(sem("o_hi"), t + 1)
                nc.vector.tensor_tensor(o_lo[:, t % 2, :, :], bank[4 + t % 2][:, :].rearrange("p (k n) -> p k n", k=KD),
                                        o_hi[:, t % 2, :, :].bitcast(F32), ALU.subtract).then_inc(sem("o_split"), 1)

            norm_out(0)

            PR, PI, LR, LI = 2, 3, 4, 5

            def complex_mul(dst, ac, as_, bc, bs, t1, t2):
                nc.vector.tensor_tensor(t1, ac, bc, ALU.mult)
                link(nc.vector.tensor_tensor(t2, as_, bs, ALU.mult))
                link(nc.vector.tensor_tensor(dst[0], t1, t2, ALU.subtract))
                nc.vector.tensor_tensor(t1, ac, bs, ALU.mult)
                link(nc.vector.tensor_tensor(t2, as_, bc, ALU.mult))
                link(nc.vector.tensor_tensor(dst[1], t1, t2, ALU.add))

            def phasor_square():
                dve.wait_ge(sem("chan_in"), 16)
                nc.vector.tensor_tensor(pw[:, 4, :], chan[:, PR, :], chan[:, PR, :], ALU.mult)
                link(nc.vector.tensor_tensor(pw[:, 5, :], chan[:, PI, :], chan[:, PI, :], ALU.mult))
                link(nc.vector.tensor_tensor(pw[:, 5, :], pw[:, 4, :], pw[:, 5, :], ALU.add))
                link(nc.vector.tensor_scalar(pw[:, 7, :], pw[:, 5, :], 0.0, None, ALU.is_equal))
                nc.vector.tensor_tensor(pw[:, 0, :], pw[:, 5, :], pw[:, 7, :], ALU.add).then_inc(sem("p_sq"), 1)

            def double(table, n):
                last_c, last_s = (table[:, c, :, n - 1:n].to_broadcast([P, DEPTH, n]) for c in range(2))
                complex_mul([table[:, c, :, n:2 * n] for c in range(2)], table[:, 0, :, 0:n], table[:, 1, :, 0:n], last_c, last_s,
                            turn_tmp[:, 0, :, 0:n], turn_tmp[:, 1, :, 0:n])

            def low_powers():
                dve.wait_ge(sem("p_inv"), 1)
                nc.vector.tensor_tensor(pw[:, 2, :], pw[:, 5, :], pw[:, 1, :], ALU.mult).then_inc(sem("p_abs"), 1)
                nc.vector.tensor_tensor(low_turn[:, 1, :, 0], chan[:, PI, :], pw[:, 1, :], ALU.mult)
                link(nc.vector.tensor_tensor(low_turn[:, 0, :, 0], chan[:, PR, :], pw[:, 1, :], ALU.mult))
                link(nc.vector.tensor_tensor(low_turn[:, 0, :, 0], low_turn[:, 0, :, 0], pw[:, 7, :], ALU.add))
                n = 1
                while n < TURN_LOW:
                    double(low_turn, n)
                    n *= 2

            def high_powers():
                nc.vector.memset(high_turn[:, 0, :, 0:1], 1.0)
                nc.vector.memset(high_turn[:, 1, :, 0:1], 0.0)
                link(nc.vector.tensor_copy(high_turn[:, :, :, 1], low_turn[:, :, :, TURN_LOW - 1]))
                n = 1
                while n < TURN_HIGH:
                    double(high_turn[:, :, :, 1:TURN_HIGH + 1], n)
                    n *= 2

            def full_turn(l, c, t1, t2):
                grid = [P, TURN_HIGH // 2, TURN_LOW]

                def square(ap):
                    return ap.rearrange("p (i j) -> p i j", j=TURN_LOW)

                low = [low_turn[:, k, l, :].unsqueeze(1).to_broadcast(grid) for k in range(2)]
                high = [high_turn[:, k, l, TURN_HIGH // 2 * c:TURN_HIGH // 2 * (c + 1)].unsqueeze(2).to_broadcast(grid) for k in range(2)]
                complex_mul([square(turn_half(l, c)[:, k, :]) for k in range(2)], low[0], low[1], high[0], high[1], square(t1), square(t2))

            def ffn(s):
                full(s, 0, 2)
                for u in range(2 * len(HT)):
                    n = hid(u // 2)
                    dve.wait_ge(sem(f"silu{s}"), u + 1)
                    if u >= 2:
                        dve.wait_ge(sem(f"h_lo{s}"), u - 1)
                    nc.vector.tensor_tensor(hf[0:n, u % 2, :], sg[0:n, u % 2, :], bank[2 * (u % 2) + 1][0:n, :],
                                            ALU.mult).then_inc(sem(f"h_full{s}"), 1)
                    for q in PREPS[u]:
                        full(s, q // 3, q % 3)
                    if s == 1:
                        if u == 7:
                            phasor_square()
                        elif u == 9:
                            low_powers()
                        elif u == 11:
                            high_powers()

                def make_y(t):
                    dve.wait_ge(sem(f"down{s}"), NT + t + 1)
                    dve.wait_ge(sem(f"y_part{s}"), t + 1)
                    nc.vector.tensor_tensor(y[:, t, :], y[:, t, :], bank[4 + t % 2][:, :], ALU.add).then_inc(sem(f"y_ready{s}"), 1)

                norm_out(s, make_y)

            ffn(1)

            dve.wait_ge(sem("mixer_in"), 144)
            dve.wait_ge(sem("win_hi"), 1)
            nc.vector.tensor_tensor(win_lo[:, :, :], win_raw[:, :, :], win_hi[:, :, :].bitcast(F32), ALU.subtract).then_inc(sem("win_split"), 1)
            link(nc.vector.tensor_scalar(pw[:, 6, :], chan[:, LI, :], -1.0, None, ALU.mult))
            for c in range(2):
                full_turn(0, c, turn_a[:, 0, :], turn_a[:, 1, :])
            for b in range(B):
                rows = slice(C * b, C * b + C)
                dve.wait_ge(sem("mix_in"), b + 1)
                link(nc.vector.tensor_scalar(hm[rows, :], bank[b][rows, :], last[rows, 0:1], None, ALU.add))
            dve.wait_ge(sem("decay"), 1)
            nc.vector.tensor_copy(turn_a[:, 0, 0:1], hm[:, 0:1]).then_inc(sem("h_ready"), 1)

            for e in MIXER:
                what, n, c, f = e
                l, cols = n // 2, slice(c * HALF, (c + 1) * HALF)
                decay = pw[:, 3, l % DEPTH:l % DEPTH + 1].to_broadcast([P, HALF])
                if what == VAR:
                    dve.wait_ge(sem("mix_var"), done_at[e])
                    nc.vector.tensor_scalar(var_eps[:, c, :], bank[2 + c][:, HALF:HALF + 4], EPS, None, ALU.add).then_inc(sem("mix_var_eps"), 1)
                elif what == SPREAD_DEV:
                    dve.wait_ge(sem("mix_spread"), done_at[e])
                    nc.vector.tensor_tensor(normed[:, c, :], bank[2 + c][:, 0:HALF], centred[:, c, :], ALU.mult).then_inc(sem("mix_norm"), 1)
                elif what == AFFINE:
                    w, bias = (last[:, 1:2], last[:, 2:3]) if n == 2 * DEPTH else (chan[:, 7, l:l + 1], chan[:, 8, l:l + 1])
                    dve.wait_ge(sem("mix_norm"), done_at[SPREAD_DEV, n, c, 0])
                    nc.vector.tensor_scalar(affine[:, c, :], normed[:, c, :], w, bias, ALU.mult, ALU.add).then_inc(sem("mix_affine"), 1)
                elif what == MOD:
                    dve.wait_ge(sem("mix_silu"), done_at[e])
                    link(nc.vector.tensor_tensor(cos_in[:, c, :], active[:, c, :], turn_half(l, c)[:, 0, :], ALU.mult))
                elif what == SCAN:
                    start = (cos_out[:, 0, HALF - 1:HALF], sin_out[:, 0, HALF - 1:HALF]) if c else (chan[:, LR, l:l + 1], pw[:, 6, l:l + 1])
                    link(nc.vector.tensor_tensor_scan(cos_out[:, c, :], decay, cos_in[:, c, :], start[0], ALU.mult, ALU.add))
                    dve.wait_ge(sem("sin_mod"), done_at[e])
                    nc.vector.tensor_tensor_scan(sin_out[:, c, :], decay, sin_in[:, c, :], start[1], ALU.mult, ALU.add).then_inc(sem("sin_scan"), 1)
                    link(nc.vector.tensor_tensor(demod[:, c, :], cos_out[:, c, :], turn_half(l, c)[:, 0, :], ALU.mult))
                elif what == DEMOD:
                    dve.wait_ge(sem("sin_demod"), done_at[e])
                    link(nc.vector.tensor_tensor(demod[:, c, :], demod[:, c, :], sin_demod[:, c, :], ALU.add))
                    nc.vector.scalar_tensor_tensor(out=hm[:, cols], in0=demod[:, c, :], scalar=chan[:, 6, l:l + 1], in1=hm[:, cols],
                                                   op0=ALU.mult, op1=ALU.add).then_inc(sem("h_ready"), 1)
                elif what == DOWN:
                    dve.wait_ge(sem("mix_down"), done_at[e])
                    nc.vector.scalar_tensor_tensor(out=hm[:, cols], in0=bank[c][:, HALF:S], scalar=chan[:, 9, l:l + 1], in1=hm[:, cols],
                                                   op0=ALU.add, op1=ALU.add).then_inc(sem("h_ready"), 1)
                elif what == TABLE:
                    full_turn(n, c, turn_a[:, 0, :], turn_a[:, 1, :])
                elif what == SIDE and n == 3:
                    dve.wait_ge(sem("side_hi3"), 3)
                    nc.vector.scalar_tensor_tensor(out=side_gu[0:48, 0:F], in0=scale_hi[:, :].bitcast(F32), scalar=low_rows[0:48, 2:3],
                                                   in1=scale_gu[:, 0:F], op0=ALU.mult, op1=ALU.add).then_inc(sem("side_ready3"), 1)
                    nc.vector.tensor_tensor(side_d[:, F + D // 2:F + D], scale_d[:, F:F + D // 2], side_d[:, F:F + D // 2].bitcast(F32),
                                            ALU.subtract).then_inc(sem("side_ready3"), 1)

            def mixer_y(t):
                dve.wait_ge(sem("mix_out"), t + 1)
                nc.vector.tensor_tensor(y[:, t, :], bank[2 + t % 2][:, :], bout[:, :], ALU.add).then_inc(sem("y_ready2"), 1)

            norm_out(2, mixer_y)
            ffn(3)

        @block.tensor
        def _(pe):
            def xt_tile(s, t):
                if 0 <= t < NT:
                    pe.wait_ge(sem(f"xn{s}"), t + 1)
                    if t >= 2:
                        pe.wait_ge(sem(f"xt_ready{s}"), t - 1)
                    elif s in (1, 3):
                        pe.wait_ge(sem(f"wfull{s}"), t + 1)
                    for k in range(KD):
                        ins = nc.tensor.transpose(bank[6 + t % 2][:, k * P:(k + 1) * P], xn[:, t % 2, k * P:(k + 1) * P], ident[:, :])
                    ins.then_inc(sem(f"xt_psum{s}"), 1)

            def split_product(dst, lhs, rhs, ks, start=True, stop=True):
                todo = [(k, i, j) for k in ks for i, j in COMBOS]
                for n, (k, i, j) in enumerate(todo):
                    ins = nc.tensor.matmul(dst, lhs(i, k), rhs(j, k), start=start and n == 0, stop=stop and n == len(todo) - 1)
                return ins

            pe.wait_ge(sem("ident_in"), 16)
            W = (w_hi, w_lo)
            for t in range(NT + 2):
                if t < NT:
                    xt_tile(0, t)
                if t >= 2:
                    u = t - 2
                    pe.wait_ge(sem("xt_ready0"), u + 1)
                    for j in range(3):
                        if u == 0:
                            pe.wait_ge(sem("w_split"), j + 1)
                        if u >= 2:
                            pe.wait_ge(sem("v_ready" if j == 2 else "rotated"), u - 1 if j == 2 else 2 * (u - 2) + j + 1)
                        split_product(bank[(3 * u + j) % 6][:, :], lambda i, k: XT[i][:, k, u * P:(u + 1) * P],
                                      lambda i, k: W[i][:, j, k, :], range(KD)).then_inc(sem("proj"), 1)

            pe.wait_ge(sem("consts_in"), 7 * 16)
            pe.wait_ge(sem("qk_ready"), 2 * NT)
            pe.wait_ge(sem("v_ready"), NT)

            pe.wait_ge(sem("spread_ready"), 1)
            pe.wait_ge(sem("v_ones"), 1)
            pe.wait_ge(sem("ident_r"), 1)

            def ring_free(e):
                n = RINGED.index(e)
                if n >= 3:
                    before = RINGED[n - 3]
                    for reader in {ONE: ("row_max",), TWO: ("exp",), TURN: ("block_split",), FLIP: ("o_ready",),
                                   SPREAD: ("k_stack", "q_stack")}[before[0]]:
                        pe.wait_ge(sem(reader), nth[before] + 1)

            def masked(dst, lhs, rhs, diagonal, mask, unit):
                for h in range(2):
                    rows = slice(64 * h, 64 * h + 64)
                    nc.tensor.matmul(dst[:, h, :], lhs[rows, :], rhs[rows, :], start=True, stop=False)
                for h in range(2):
                    ins = nc.tensor.matmul(dst[:, h, diagonal:diagonal + P], mask, unit, start=False, stop=True)
                return ins

            for e in PERIODS:
                what, g, i = e
                if what == TURN:
                    b, c = divmod(g, KD)
                    ring_free(e)
                    for j in range(2):
                        for t in range(TB):
                            ins = nc.tensor.transpose(pair_of_banks(e)[:, j, t * P:(t + 1) * P], qk[:, j, TB * b + t, c * P:(c + 1) * P],
                                                      ident[:, :])
                    ins.then_inc(sem("block_psum"), 1)
                elif what == SPREAD:
                    ring_free(e)
                    pe.wait_ge(sem("block_split"), g // 4 + 1)
                    for j in range(2):
                        for part in range(2):
                            ins = nc.tensor.matmul(pair_of_banks(e)[:, j, :], spread[:, 2 * j + part, g % 4, :],
                                                   W[part][:, 1 + g // 4 % 2, j, :], start=(part == 0), stop=(part == 1))
                    ins.then_inc(sem("stack_psum"), 1)
                elif what == ONE:
                    ring_free(e)
                    if i == 3:
                        pe.wait_ge(sem("q_stack"), g + 1)
                        pe.wait_ge(sem("k_stack"), g + 1)
                    n = (i + 1) * P
                    masked(pair_of_banks(e)[:, :, 0:n], q_stack(g)[:, i * P:n], k_stack(g)[:, 0:n], i * P,
                           ident16[:, :], causal16[:, :]).then_inc(sem("scores"), 1)
                elif what == FLIP:
                    ring_free(e)
                    pe.wait_ge(sem("heads_t"), g + 1)
                    for t in range(TB):
                        ins = nc.tensor.transpose(pair_of_banks(e)[:, 0, t * P:(t + 1) * P], heads_t[:, g % 2, t * P:(t + 1) * P], ident[:, :])
                    ins.then_inc(sem("flipped"), 1)
                elif what == PLACE:
                    pe.wait_ge(sem("max_row"), g + 1)
                    if g:
                        pe.wait_ge(sem("q_less_max"), g)
                    for t in range(TB):
                        ins = nc.tensor.matmul(bank[6][:, t * P:(t + 1) * P], max_row[:, t, :], ident_r[:, :], start=True, stop=True)
                    ins.then_inc(sem("placed"), 1)
                elif what == TWO:
                    ring_free(e)
                    if i == 0:
                        pe.wait_ge(sem("q_less_max"), g + 1)
                    for h in range(2):
                        rows = slice(64 * h, 64 * h + 64)
                        ins = nc.tensor.matmul(pair_of_banks(e)[:, h, 0:(TB - i) * P], k_stack(g)[rows, i * P:(i + 1) * P],
                                               q_less_max(g)[rows, i * P:S], start=True, stop=True)
                    ins.then_inc(sem("scores_t"), 1)
                else:
                    b, p = PAIRS[g]
                    pe.wait_ge(sem("probs"), TB * g + i + 1)
                    if i == 0 and g % 2 == 0 and g:
                        pe.wait_ge(sem("heads_t"), g // 2)
                    for h in range(2):
                        row, col = 32 * (g % 2 * 2 + h), (2 * p + h) * (HD + 1)
                        ins = nc.tensor.matmul(bank[7][row:row + 32, i * P:S], v[:, TB * b + i, col:col + 32],
                                               probs[:, (TB * g + i) % 3, h, 0:(TB - i) * P], start=(i == 0), stop=(i == TB - 1))
                    ins.then_inc(sem("pv"), 1)
            pe.wait_ge(sem("o_ready"), NPR // 2)
            pe.wait_ge(sem("wo_split"), 1)
            def prep(s, q):
                m, c = divmod(q, 3)
                h0, n = HT[m]
                height, up_row = (3 * RANK, 64) if s == 1 else (16, 32)
                if q == 0:
                    pe.wait_ge(sem(f"side_ready{s}"), 4 if s == 1 else 2)
                elif q == 2:
                    pe.wait_ge(sem(f"xt_ready{s}"), NT)
                if q >= 2:
                    pe.wait_ge(sem(f"wfull{s}"), q - 1)
                dst = bank[6 + q % 2]
                if c < 2:
                    rows = slice(up_row * c, up_row * c + height)
                    for k in range(KD):
                        ins = nc.tensor.matmul(dst[:, k * P:k * P + n], side_gu[rows, F + k * P:F + k * P + P], side_gu[rows, h0:h0 + n],
                                               start=True, stop=True)
                elif s == 1:
                    ins = nc.tensor.matmul(dst[0:n, :], side_d[0:height, h0:h0 + n], side_d[0:height, F:F + D], start=True, stop=True)
                else:
                    for e in range(2):
                        if e:
                            ins.then_inc(sem("scales_even"), 1)
                            pe.wait_ge(sem("scales_even"), m + 1)
                        rows = slice(64 * e, 64 * e + 43)
                        for part in range(2):
                            cols = slice(F + D // 2 * part, F + D // 2 * (part + 1))
                            ins = nc.tensor.matmul(dst[0:n, e * 256:e * 256 + 256], side_d[rows, h0:h0 + n], side_d[rows, cols],
                                                   start=(part == 0), stop=(part == 1))
                ins.then_inc(sem(f"prep{s}"), 1)

            def gate_up(s, u, g):
                m, n = u // 2, hid(u // 2)
                if g == 0:
                    if u < 2:
                        pe.wait_ge(sem(f"xt_ready{s}"), NT // 2 * (u + 1))
                    pe.wait_ge(sem(f"wlo{s}"), 3 * m + 2)
                    if u >= 2:
                        pe.wait_ge(sem(f"h_full{s}"), u - 1)
                ins = split_product(bank[2 * (u % 2) + g][0:n, :], lambda i, k: (wgu_hi, wgu_lo)[i][:, 2 * (m % 2) + g, k, 0:n],
                                    lambda i, k: XT[i][:, k, u % 2 * 512:u % 2 * 512 + 512], range(KD))
                if g:
                    ins.then_inc(sem(f"gu{s}"), 1)

            for t in range(NT + XT_LAG + 1):
                if t < NT:
                    if t >= 2:
                        pe.wait_ge(sem("o_split"), t - 1)
                    for k in range(KD):
                        ins = nc.tensor.transpose(bank[4 + t % 2][:, k * P:(k + 1) * P], y[:, t, k * P:(k + 1) * P], ident[:, :])
                    ins.then_inc(sem("o_psum"), 1)
                if 1 <= t <= NT:
                    c = t - 1
                    pe.wait_ge(sem("o_split"), c + 1)
                    if c >= 2:
                        pe.wait_ge(sem("y_ready0"), c - 1)
                    split_product(bank[c % 2][:, :], lambda i, k: (o_hi, o_lo)[i][:, c % 2, k, :],
                                  lambda i, k: W[i][:, 0, k, :], range(KD)).then_inc(sem("wo_done"), 1)
                if t == XT_LAG:
                    for q in range(2):
                        prep(1, q)
                xt_tile(1, t - 1 - XT_LAG)
                if t in EARLY:
                    pe.wait_ge(sem("y_ready0"), NT)
                    gate_up(1, 0, EARLY.index(t))

            def ffn(s):
                def down(gq):
                    m0, m1 = GROUPS[gq]
                    for t in range(NT):
                        if t >= 2:
                            pe.wait_ge(sem(f"y_ready{s}" if gq else f"y_part{s}"), t - 1)
                        elif gq:
                            pe.wait_ge(sem(f"y_part{s}"), NT)
                        todo = [(m, i, j) for m in range(m0, m1) for i, j in COMBOS]
                        for c, (m, i, j) in enumerate(todo):
                            n = hid(m)
                            if t == 0 and (i, j) == COMBOS[0]:
                                pe.wait_ge(sem(f"h_lo{s}"), 2 * m + 2)
                                pe.wait_ge(sem(f"wlo{s}"), 3 * m + 3)
                            ins = nc.tensor.matmul(bank[4 + t % 2][:, :], (h_hi, h_lo)[i][0:n, m % RING, t * P:(t + 1) * P],
                                                   (wd_hi, wd_lo)[j][0:n, m % RING, :], start=(c == 0), stop=(c == len(todo) - 1))
                        ins.then_inc(sem(f"down{s}"), 1)
                        if gq and s < 3:
                            xt_tile(s + 1, t - XT_LAG)

                prep(s, 2)
                for u in range(2 * len(HT)):
                    if u:
                        for g in range(2):
                            gate_up(s, u, g)
                    for q in PREPS[u]:
                        prep(s, q)
                    if u == 2 * GROUPS[0][1] + 1:
                        down(0)
                down(1)

            ffn(1)
            for t in range(NT - XT_LAG, NT):
                xt_tile(2, t)
            pe.wait_ge(sem("xt_ready2"), NT)
            pe.wait_ge(sem("win_split"), 1)
            for b in range(B):
                split_product(bank[b][:, :], lambda i, k: (win_hi, win_lo)[i][:, k, :],
                              lambda i, k: XT[i][:, k, b * S:(b + 1) * S], range(KD)).then_inc(sem("mix_in"), 1)

            for e in MIXER:
                what, n, c, f = e
                l, cols = n // 2, slice(c * HALF, (c + 1) * HALF)
                if what == CENTRE:
                    pe.wait_ge(sem("h_ready"), h_at[n - 1, c])
                    nc.tensor.matmul(bank[c][:, 0:HALF], cmat[:, :], hm[:, cols], start=True, stop=True).then_inc(sem("mix_centre"), 1)
                elif what == VAR:
                    pe.wait_ge(sem("mix_squares"), done_at[CENTRE, n, c, 0])
                    for i in range(2):
                        ins = nc.tensor.matmul(bank[2 + c][:, HALF + 2 * i:HALF + 2 * i + 2], squares[:, c, i * P:(i + 1) * P], bmat[:, 0:P:C],
                                               start=True, stop=True)
                    ins.then_inc(sem("mix_var"), 1)
                elif what == SPREAD_DEV:
                    pe.wait_ge(sem("mix_repeated"), done_at[VAR, n, c, 0])
                    for i in range(2):
                        ins = nc.tensor.matmul(bank[2 + c][:, i * P:(i + 1) * P], inv_dev_c[:, c, i, :], ident[:, :], start=True, stop=True)
                    ins.then_inc(sem("mix_spread"), 1)
                elif what == UP:
                    pe.wait_ge(sem("mix_affine"), done_at[AFFINE, n, c, 0])
                    if done_at[e] > 2:
                        pe.wait_ge(sem("mix_act"), done_at[e] - 2)
                    for b in range(B):
                        rows = slice(C * b, C * b + C)
                        ins = nc.tensor.matmul(bank[4 + 2 * f + b][:, 0:HALF], w1t[rows, l, f * P:(f + 1) * P], affine[rows, c, :],
                                               start=True, stop=True)
                    ins.then_inc(sem("mix_up"), 1)
                elif what == DOWN:
                    pe.wait_ge(sem("mix_act"), done_at[UP, n, c, 1])
                    for f in range(2):
                        for b in range(B):
                            ins = nc.tensor.matmul(bank[c][C * b:C * b + C, HALF:S], w2t[:, l, f, :], g1[:, c, f, b, :],
                                                   start=(f == 0), stop=(f == 1))
                    ins.then_inc(sem("mix_down"), 1)
            pe.wait_ge(sem("mix_affine"), 2 * DEPTH + 2)
            for t in range(NT + XT_LAG):
                if t < NT:
                    rows = slice(C * (t // TB), C * (t // TB) + C)
                    if t >= 2:
                        pe.wait_ge(sem("y_ready2"), t - 1)
                    nc.tensor.matmul(bank[2 + t % 2][:, :], affine[rows, t % TB // 2, t % 2 * P:(t % 2 + 1) * P], wout[rows, :],
                                     start=True, stop=True).then_inc(sem("mix_out"), 1)
                if t == XT_LAG - 1:
                    for q in range(2):
                        prep(3, q)
                xt_tile(3, t - XT_LAG)
                if t + 1 in EARLY:
                    gate_up(3, 0, EARLY.index(t + 1))
            ffn(3)


def kernel(**inputs):
    import numpy as np
    import concourse.bacc as bacc
    from concourse import mybir as _mybir
    from concourse.bass_utils import run_bass_kernel_spmd as _run
    import ml_dtypes

    A = {k: np.asarray(w) for k, w in inputs.items()}
    f32 = np.float32
    arr = {}
    arr["x"] = A["L0_attn_x"].reshape(N, D)
    for n in ("wq", "wk", "wv", "wo"):
        arr[n] = A["L0_attn_" + n]
    arr["ident"] = np.eye(P, dtype=f32)
    arr["ident16"] = np.eye(P).astype(ml_dtypes.bfloat16)
    arr["causal16"] = np.where(np.arange(P)[None, :] > np.arange(P)[:, None], -1e30, 0.0).astype(ml_dtypes.bfloat16)
    inv = 1.0 / 10000.0 ** (np.arange(0, HD, 2)[:HD // 2].astype(f32) / HD)
    ang = np.outer(np.arange(S), inv).astype(f32)
    cos, sin = np.cos(ang), np.sin(ang)
    c2 = np.stack([cos, cos], -1).reshape(TB, P, HD).transpose(1, 0, 2)
    s2 = np.stack([-sin, sin], -1).reshape(TB, P, HD).transpose(1, 0, 2)
    scale = 1.0 / np.sqrt(f32(HD))
    arr["rope_c"] = np.stack([c2 * scale, c2], 1).astype(f32)
    arr["rope_s"] = np.stack([s2 * scale, s2], 1).astype(f32)
    row = np.arange(P)
    copy = row % 64 // HD
    spread = np.zeros((P, 2, 2, 4, P), f32)
    for j, low in enumerate((copy == 2, copy == 1)):
        for pair in range(4):
            for r in row[copy < 3]:
                spread[2 * HD * pair + HD * (r // 64) + r % HD, j, int(low[r]), pair, r] = 1.0
    arr["k_one"] = np.isin(row % 64, (3 * HD, 3 * HD + 1)).astype(f32)[:, None]
    arr["spread"] = spread.reshape(P, 4, D)
    arr["gu_t"] = np.stack([A["L0_ffn_gate_w"].T, A["L0_ffn_up_w"].T])
    arr["down_t"] = A["L0_ffn_down_w"].T
    def factors(name):
        return np.tile(np.concatenate([A[f"L0_ffn_{name}_b"].T, A[f"L0_ffn_{name}_a"]], 1), (3, 1))
    arr["side_gu1"] = np.concatenate([factors("gate"), np.zeros((64 - 3 * RANK, F + D), f32), factors("up")], 0)
    arr["side_d1"] = np.tile(np.concatenate([A["L0_ffn_down_a"], A["L0_ffn_down_b"].T], 1), (3, 1))
    low = np.zeros((P, 3), f32)
    low[:, 0] = -1.0 * (row % 64 // RANK == 2)
    low[:, 1] = -1.0 * (row % 64 // RANK == 1)
    low[:, 2] = -1.0 * (row % 32 // 8 == 1)
    arr["low_rows"] = low
    def byte_of(w, rows, cols):
        return np.concatenate([w, w], axis=1).reshape(rows, cols).T
    arr["w13"] = np.stack([byte_of(A["L1_ffn_w1"], F, D), byte_of(A["L1_ffn_w3"], F, D)])
    arr["w2"] = byte_of(A["L1_ffn_w2"], D, F)
    sel = np.zeros((8, KD, P), f32)
    for k in range(KD):
        for p in range(P):
            sel[2 * k + p // GROUP4, k, p] = 1.0
    side = np.zeros((48, F + D), f32)
    for c, n in enumerate(("s1", "s3")):
        for part in range(2):
            rows = slice(32 * c + 8 * part, 32 * c + 8 * part + 8)
            side[rows, :F] = A["L1_ffn_" + n].reshape(F, 8).T
            side[rows, F:] = sel.reshape(8, D)
    arr["side_gu3"] = side
    side = np.zeros((107, F + D // 2), f32)
    for e in range(2):
        side[64 * e + (F * e + np.arange(F)) // GROUP4, np.arange(F)] = 1.0
        side[64 * e:64 * e + 43, F:] = A["L1_ffn_s2"].reshape(D // 2, 43).T
    arr["side_d3"] = side
    sh = np.zeros((P, 5, 2), np.int32)
    for e in range(5):
        low = ((F * e + np.arange(P)) % P if e < 4 else np.arange(P)) >= GROUP4
        sh[:, e, 0] = np.where(low, 28, 0)
        sh[:, e, 1] = np.where(low, 28, 4)
    arr["shifts"] = sh
    arr["win_t"] = np.concatenate([A["L1_attn_Win"], A["L1_attn_Win"]], 0).T.reshape(KD, P, P).transpose(1, 0, 2)
    w1 = A["L1_attn_W1"].transpose(2, 0, 1)
    arr["w1_t"] = np.concatenate([w1, w1], 0)
    arr["w2_t"] = A["L1_attn_W2"].transpose(0, 2, 1).reshape(DEPTH, 2, P, C).transpose(2, 0, 1, 3)
    arr["wout_t"] = np.concatenate([A["L1_attn_Wout"].T] * 2, 0)
    block64 = np.kron(np.eye(2), np.full((C, C), 1.0 / C))
    arr["bmat"] = block64.astype(f32)
    arr["cmat"] = (np.eye(P) - block64).astype(f32)
    names = ("ln1_w", "ln1_b", "phz_re", "phz_im", "lc_re", "lc_im", "sc_lin", "ln2_w", "ln2_b", "b2")
    ch = np.stack([A["L1_attn_" + n].T for n in names], 1)
    arr["chan"] = np.concatenate([ch, ch], 0)
    arr["b1"] = A["L1_attn_b1"].reshape(DEPTH, 2, P).transpose(2, 0, 1)
    la = np.stack([A["L1_attn_bin"], A["L1_attn_lnl_w"], A["L1_attn_lnl_b"]], 1)
    arr["last"] = np.concatenate([la, la], 0)
    arr["bout"] = A["L1_attn_bout"]

    nc = bacc.Bacc("TRN2", target_bir_lowering=False, num_devices=1)
    arrays, aps = {}, {}
    for name, w in arr.items():
        w = np.ascontiguousarray(w)
        arrays["in_" + name] = w
        aps[name] = nc.dram_tensor("in_" + name, w.shape, _mybir.dt.from_np(w.dtype), kind="ExternalInput").ap()
    out = nc.dram_tensor("out", (N, D), F32, kind="ExternalOutput").ap()
    sandwich(nc, aps, out)
    r = _run(nc, [arrays], core_ids=[0])
    return r.results[0]["out"].reshape(B, S, D)
```
